# Optimizing a Trainium2 kernel written in Bass

```python
import numpy as np
import jax
import jax.numpy as jnp

def _softmax(x, axis=-1):
    return jax.nn.softmax(x, axis=axis)

def _gelu(x):
    return jax.nn.gelu(x, approximate=True)

def _silu(x):
    return jax.nn.silu(x)

def _sigmoid(x):
    return jax.nn.sigmoid(x)

def _layernorm(x, axis=-1, eps=1e-05):
    m = jnp.mean(x, axis=axis, keepdims=True)
    v = jnp.var(x, axis=axis, keepdims=True)
    return (x - m) / jnp.sqrt(v + eps)

def _scatter_add(tgt, idx, src, axis=0):
    return tgt.at[idx].add(src)

def _segment_sum(src, seg, n):
    return jax.ops.segment_sum(src, seg, n)
kernel_name = 'mk_flamingo_gated_d2_seqx_r4_84d505'

def setup_inputs(seed: int=0):
    np.random.seed(seed)
    _w = jnp.asarray

    def _rec_inputs():
        import jax
        import jax.numpy as jnp
        _rk = jax.random.key(seed)
        x = -0.000125 + 0.9999 * jax.random.normal(jax.random.fold_in(_rk, 1), (2, 512, 1024), jnp.float32)
        _lenS = 512 - jax.random.randint(jax.random.fold_in(_rk, 7), (2,), 0, max(1, 512 // 4) + 1, jnp.int32)
        _lenS2 = 1024 - jax.random.randint(jax.random.fold_in(_rk, 8), (2,), 0, max(1, 1024 // 4) + 1, jnp.int32)
        _ctx_4096P = jax.random.normal(jax.random.fold_in(_rk, 11), (2, 16, 1024), jnp.float32)
        _ctx_4096c = jax.random.dirichlet(jax.random.fold_in(_rk, 511), 0.3 * jnp.ones((16,), jnp.float32), (2, 1024))
        _ctx_4096t = jnp.einsum('bsk,bkd->bsd', _ctx_4096c, _ctx_4096P)
        _ctx_4096t = _ctx_4096t * jax.lax.rsqrt(jnp.mean(jnp.square(_ctx_4096t)) + 1e-12) * 0.953939
        ctx_4096 = -5.72187e-05 + 0.999849 * (_ctx_4096t + 0.3 * jax.random.normal(jax.random.fold_in(_rk, 611), (2, 1024, 1024), jnp.float32))
        _g = jax.random.normal(jax.random.fold_in(_rk, 9001), (2, 2), jnp.float32)
        _g = jnp.sign(_g) * jnp.maximum(jnp.abs(_g), 1.0) + (_g == 0) * 1.0
        g_xattn = _g[0]
        g_ffn = _g[1]
        return (x, ctx_4096, g_xattn, g_ffn)
    x, ctx_4096, g_xattn, g_ffn = _rec_inputs()

    def _L0_xattn_setup():
        import jax, jax.numpy as jnp
        import numpy as np
        QMIN = 0.0
        QMAX = 255.0

        def fake_quant(x, scale, zp):
            s = scale.reshape(())
            z = zp.reshape(())
            q = jnp.clip(jnp.round(x / s + z), QMIN, QMAX)
            return (q - z) * s
        key = jax.random.key(seed)
        k1, k2 = jax.random.split(key)
        B, M, K, N = (4, 512, 1024, 1024)
        x1 = jax.random.normal(k1, (B, M, K), dtype=jnp.float32)
        x2 = jax.random.normal(k2, (B, K, N), dtype=jnp.float32)
        x1_scale = jnp.full((1,), 8.0 / 255.0, dtype=jnp.float32)
        x1_zp = jnp.full((1,), 128.0, dtype=jnp.float32)
        x2_scale = jnp.full((1,), 8.0 / 255.0, dtype=jnp.float32)
        x2_zp = jnp.full((1,), 128.0, dtype=jnp.float32)
        return {'x1': x1, 'x2': x2, 'x1_scale': x1_scale, 'x1_zp': x1_zp, 'x2_scale': x2_scale, 'x2_zp': x2_zp}
    _L0_xattn_all = _L0_xattn_setup()
    _L0_xattn_in = {k: v for k, v in _L0_xattn_all.items() if k in ('x1_scale', 'x1_zp', 'x2_scale', 'x2_zp')}
    del _L0_xattn_all

    def _L0_ffn_setup():
        import math
        import jax, jax.numpy as jnp
        import numpy as np
        SCALING = 16.0 / 32.0

        def real_fourier_orthogonal_multiply(c):
            n = c.shape[-1]
            sqrt_n = math.sqrt(n)
            pair_scale = math.sqrt(n / 2.0)
            max_f = (n - 1) // 2
            work = c.astype(jnp.float32)
            dc = (work[..., 0] * sqrt_n)[..., None].astype(jnp.complex64)
            cos = work[..., 1:1 + 2 * max_f:2] * pair_scale
            sin = work[..., 2:2 + 2 * max_f:2] * pair_scale
            mid = (cos - 1j * sin).astype(jnp.complex64)
            parts = [dc, mid]
            if n % 2 == 0:
                parts.append((work[..., -1] * sqrt_n)[..., None].astype(jnp.complex64))
            spectrum = jnp.concatenate(parts, axis=-1)
            return jnp.fft.irfft(spectrum, n=n, axis=-1).astype(c.dtype)
        key = jax.random.key(seed)
        ks = jax.random.split(key, 9)
        B, S, D_in, D_out, R0, R1, E = (4, 512, 1024, 1024, 32, 8, 3)
        x = jax.random.normal(ks[0], (B, S, D_in), dtype=jnp.float32)
        W_base = jax.random.normal(ks[1], (D_out, D_in), dtype=jnp.float32) * 0.02
        b_base = jax.random.normal(ks[2], (D_out,), dtype=jnp.float32) * 0.02
        enc0 = jax.random.normal(ks[3], (R0, D_in), dtype=jnp.float32) * 0.02
        enc1 = jax.random.normal(ks[4], (R1, D_in), dtype=jnp.float32) * 0.02
        coefs0 = jax.random.normal(ks[5], (E, D_out, R0), dtype=jnp.float32) * 0.02
        coefs1 = jax.random.normal(ks[6], (E, D_out, R1), dtype=jnp.float32) * 0.02
        mask0 = jax.random.randint(ks[7], (E, D_out, R0), 0, 2).astype(bool)
        mask1 = jax.random.randint(ks[8], (E, D_out, R1), 0, 2).astype(bool)
        return dict(x=x, W_base=W_base, b_base=b_base, enc0=enc0, enc1=enc1, coefs0=coefs0, coefs1=coefs1, mask0=mask0, mask1=mask1)
    _L0_ffn_all = _L0_ffn_setup()
    _L0_ffn_in = {k: v for k, v in _L0_ffn_all.items() if k in ('W_base', 'b_base', 'enc0', 'enc1', 'coefs0', 'coefs1', 'mask0', 'mask1')}
    del _L0_ffn_all

    def _L1_xattn_setup():
        import jax, jax.numpy as jnp
        import numpy as np
        B, Q, D = (8, 64, 1024)
        CTX = 1024
        H, KV, HD = (16, 4, 96)
        G = H // KV
        key = jax.random.key(seed)
        ks = jax.random.split(key, 6)
        s = 0.02
        return {'latents': jax.random.normal(ks[0], (B, Q, D), jnp.float32), 'context': jax.random.normal(ks[1], (B, CTX, D), jnp.float32), 'Wq': jax.random.normal(ks[2], (H * HD, D), jnp.float32) * s, 'Wk': jax.random.normal(ks[3], (KV * HD, D), jnp.float32) * s, 'Wv': jax.random.normal(ks[4], (KV * HD, D), jnp.float32) * s, 'Wo': jax.random.normal(ks[5], (D, H * HD), jnp.float32) * s}
    _L1_xattn_all = _L1_xattn_setup()
    _L1_xattn_in = {k: v for k, v in _L1_xattn_all.items() if k in ('Wq', 'Wk', 'Wv', 'Wo')}
    del _L1_xattn_all

    def _L1_ffn_setup():
        import jax, jax.numpy as jnp
        import numpy as np
        K_TOP = 8
        key = jax.random.key(seed)
        k1, k2, k3 = jax.random.split(key, 3)
        B, S, H, E = (4, 1024, 1024, 64)
        hidden_states = jax.random.normal(k1, (B, S, H), dtype=jnp.float32)
        router_weight = jax.random.normal(k2, (E, H), dtype=jnp.float32)
        router_bias = jnp.zeros((E,), dtype=jnp.float32)
        expert_bias = jax.random.normal(k3, (E, H), dtype=jnp.float32) * 0.1
        return {'hidden_states': hidden_states, 'router_weight': router_weight, 'router_bias': router_bias, 'expert_bias': expert_bias}
    _L1_ffn_all = _L1_ffn_setup()
    _L1_ffn_in = {k: v for k, v in _L1_ffn_all.items() if k in ('router_weight', 'router_bias', 'expert_bias')}
    del _L1_ffn_all
    return {'x': x, 'ctx_4096': ctx_4096, 'g_xattn': g_xattn, 'g_ffn': g_ffn, 'L0_xattn_x1_scale': _L0_xattn_in['x1_scale'], 'L0_xattn_x1_zp': _L0_xattn_in['x1_zp'], 'L0_xattn_x2_scale': _L0_xattn_in['x2_scale'], 'L0_xattn_x2_zp': _L0_xattn_in['x2_zp'], 'L0_ffn_W_base': _L0_ffn_in['W_base'], 'L0_ffn_b_base': _L0_ffn_in['b_base'], 'L0_ffn_enc0': _L0_ffn_in['enc0'], 'L0_ffn_enc1': _L0_ffn_in['enc1'], 'L0_ffn_coefs0': _L0_ffn_in['coefs0'], 'L0_ffn_coefs1': _L0_ffn_in['coefs1'], 'L0_ffn_mask0': _L0_ffn_in['mask0'], 'L0_ffn_mask1': _L0_ffn_in['mask1'], 'L1_xattn_Wq': _L1_xattn_in['Wq'], 'L1_xattn_Wk': _L1_xattn_in['Wk'], 'L1_xattn_Wv': _L1_xattn_in['Wv'], 'L1_xattn_Wo': _L1_xattn_in['Wo'], 'L1_ffn_router_weight': _L1_ffn_in['router_weight'], 'L1_ffn_router_bias': _L1_ffn_in['router_bias'], 'L1_ffn_expert_bias': _L1_ffn_in['expert_bias']}

def reference(x, ctx_4096, g_xattn, g_ffn, L0_xattn_x1_scale, L0_xattn_x1_zp, L0_xattn_x2_scale, L0_xattn_x2_zp, L0_ffn_W_base, L0_ffn_b_base, L0_ffn_enc0, L0_ffn_enc1, L0_ffn_coefs0, L0_ffn_coefs1, L0_ffn_mask0, L0_ffn_mask1, L1_xattn_Wq, L1_xattn_Wk, L1_xattn_Wv, L1_xattn_Wo, L1_ffn_router_weight, L1_ffn_router_bias, L1_ffn_expert_bias):
    import jax
    import jax.numpy as jnp

    def _L0_xattn_ref(x1, x2, x1_scale, x1_zp, x2_scale, x2_zp):
        import jax, jax.numpy as jnp
        import numpy as np
        QMIN = 0.0
        QMAX = 255.0

        def fake_quant(x, scale, zp):
            s = scale.reshape(())
            z = zp.reshape(())
            q = jnp.clip(jnp.round(x / s + z), QMIN, QMAX)
            return (q - z) * s
        q1 = fake_quant(x1, x1_scale, x1_zp)
        q2 = fake_quant(x2, x2_scale, x2_zp)
        return jnp.matmul(q1, q2)

    def _L0_ffn_ref(x, W_base, b_base, enc0, enc1, coefs0, coefs1, mask0, mask1):
        import math
        import jax, jax.numpy as jnp
        import numpy as np
        SCALING = 16.0 / 32.0

        def real_fourier_orthogonal_multiply(c):
            n = c.shape[-1]
            sqrt_n = math.sqrt(n)
            pair_scale = math.sqrt(n / 2.0)
            max_f = (n - 1) // 2
            work = c.astype(jnp.float32)
            dc = (work[..., 0] * sqrt_n)[..., None].astype(jnp.complex64)
            cos = work[..., 1:1 + 2 * max_f:2] * pair_scale
            sin = work[..., 2:2 + 2 * max_f:2] * pair_scale
            mid = (cos - 1j * sin).astype(jnp.complex64)
            parts = [dc, mid]
            if n % 2 == 0:
                parts.append((work[..., -1] * sqrt_n)[..., None].astype(jnp.complex64))
            spectrum = jnp.concatenate(parts, axis=-1)
            return jnp.fft.irfft(spectrum, n=n, axis=-1).astype(c.dtype)
        base = jnp.einsum('bsd,od->bso', x, W_base) + b_base
        e0 = jnp.einsum('bsd,rd->bsr', x, enc0)
        e1 = jnp.einsum('bsd,rd->bsr', x, enc1)
        w0 = coefs0 * mask0.astype(coefs0.dtype)
        w1 = coefs1 * mask1.astype(coefs1.dtype)
        decoded = jnp.einsum('bsr,eor->ebso', e0, w0) + jnp.einsum('bsr,eor->ebso', e1, w1)
        transformed = real_fourier_orthogonal_multiply(decoded)
        update = transformed.sum(axis=0)
        return base + update * SCALING

    def _L1_xattn_ref(latents, context, Wq, Wk, Wv, Wo):
        import jax, jax.numpy as jnp
        import numpy as np
        B, Q, D = (8, 64, 1024)
        CTX = 1024
        H, KV, HD = (16, 4, 96)
        G = H // KV
        b, q_len, _ = latents.shape
        hidden = jnp.concatenate([context, latents], axis=1)
        s_len = hidden.shape[1]
        q = (latents @ Wq.T).reshape(b, q_len, H, HD)
        k = (hidden @ Wk.T).reshape(b, s_len, KV, HD)
        v = (hidden @ Wv.T).reshape(b, s_len, KV, HD)
        q = q.transpose(0, 2, 1, 3).reshape(b, KV, G, q_len, HD)
        k = k.transpose(0, 2, 1, 3)
        v = v.transpose(0, 2, 1, 3)
        scale = 1.0 / jnp.sqrt(jnp.asarray(HD, q.dtype))
        scores = jnp.einsum('bkgqd,bksd->bkgqs', q, k) * scale
        attn = jax.nn.softmax(scores.astype(jnp.float32), axis=-1).astype(q.dtype)
        out = jnp.einsum('bkgqs,bksd->bkgqd', attn, v)
        out = out.reshape(b, H, q_len, HD).transpose(0, 2, 1, 3).reshape(b, q_len, H * HD)
        return out @ Wo.T

    def _L1_ffn_ref(hidden_states, router_weight, router_bias, expert_bias):
        import jax, jax.numpy as jnp
        import numpy as np
        K_TOP = 8
        B, S, H = hidden_states.shape
        E = router_weight.shape[0]
        T = B * S
        flat = hidden_states.reshape(T, H)
        logits = jnp.einsum('th,eh->te', flat, router_weight) + router_bias
        scores = jax.nn.softmax(logits, axis=-1)
        topk_w, topk_idx = jax.lax.top_k(scores, K_TOP)
        w_sum = topk_w.sum(axis=-1, keepdims=True)
        w_dense = jnp.zeros((T, E), dtype=scores.dtype).at[jnp.arange(T)[:, None], topk_idx].add(topk_w)
        bias_mix = jnp.einsum('te,eh->th', w_dense, expert_bias)
        out = flat * w_sum + bias_mix
        return out.reshape(B, S, H)
    x = x + jnp.tanh(g_xattn[0]) * _L0_xattn_ref(_layernorm(x, axis=-1), ctx_4096, L0_xattn_x1_scale, L0_xattn_x1_zp, L0_xattn_x2_scale, L0_xattn_x2_zp)
    x = x + jnp.tanh(g_ffn[0]) * _L0_ffn_ref(_layernorm(x, axis=-1), L0_ffn_W_base, L0_ffn_b_base, L0_ffn_enc0, L0_ffn_enc1, L0_ffn_coefs0, L0_ffn_coefs1, L0_ffn_mask0, L0_ffn_mask1)
    x = x + jnp.tanh(g_xattn[1]) * _L1_xattn_ref(_layernorm(x, axis=-1), ctx_4096, L1_xattn_Wq, L1_xattn_Wk, L1_xattn_Wv, L1_xattn_Wo)
    x = x + jnp.tanh(g_ffn[1]) * _L1_ffn_ref(_layernorm(x, axis=-1), L1_ffn_router_weight, L1_ffn_router_bias, L1_ffn_expert_bias)
    return x

_drawn_inputs = setup_inputs


def setup_inputs(seed=0):
    import zlib

    import numpy as np

    out = dict(_drawn_inputs(seed))
    spreads = {'g_ffn': (-1.0, 0.6), 'L1_ffn_router_bias': (0.0, 0.8)}
    factors = {'L0_ffn_b_base': 8.0,
     'L0_ffn_enc0': 8.0,
     'L0_ffn_enc1': 8.0,
     'L0_ffn_coefs0': 8.0,
     'L0_ffn_coefs1': 8.0,
     'L1_xattn_Wq': 8.0,
     'L1_xattn_Wk': 8.0,
     'L1_xattn_Wv': 7.404,
     'L1_xattn_Wo': 7.137,
     'L1_ffn_router_weight': 8.0,
     'L1_ffn_expert_bias': 8.0}
    for name, (base, spread) in spreads.items():
        noise = np.random.default_rng([zlib.crc32(name.encode()), seed]).standard_normal(out[name].shape)
        drawn = base * np.exp(spread * noise) if base else spread * noise
        out[name] = jnp.asarray(drawn.astype(out[name].dtype))
    for name, factor in factors.items():
        out[name] = (out[name] * factor).astype(out[name].dtype)
    return out
```

```python
from contextlib import ExitStack

import concourse.bass as bass
from concourse import mybir
from concourse.alu_op_type import AluOpType as ALU

ACT = mybir.ActivationFunctionType
F32 = mybir.dt.float32
F16 = mybir.dt.float16
U8 = mybir.dt.uint8
I32 = mybir.dt.int32
AX = mybir.AxisListType.X

P = 128
D = 1024
NC = D // P
B, QL, CTX = 2, 512, 1024
NT = B * QL // P
TPB = QL // P
SL = CTX + QL
NS = SL // P
KV, G, HD = 4, 4, 96
KVD = KV * HD
QG = G * HD
NJ = QG // P
VW = 2 * HD + 1
E, R = 3, 40
NE, TOP = 64, 8
EPS = 1e-5
MAGIC = 1.5 * 2.0 ** 23
MID = 128.0
QMAX = 255.0
WS = 64.0
SCALE = 1.0 / float(HD) ** 0.5
RING = 4
LAG = 3
NPF, NPB = 4, 6
HSLAB = 2 * NC * P
HI, LO = 0, 1


def flamingo(nc, x_d, ctx_d, ctx_t_d, par_d, ident_d, wk_d, wv_d, wq_d, wo_d, wb_d, bb_d, ft_d,
             coef_d, mask_d, enc_d, rw_d, rb_d, eb_d, out_d):
    with ExitStack() as ctx:
        def sb(name, shape, dt):
            return ctx.enter_context(nc.sbuf_tensor(name, shape, dt))

        def sem(name):
            return ctx.enter_context(nc.semaphore(name))

        x_res = sb("x_res", [P, NT * D], F32)
        ln_t = sb("ln_t", [P, NT * HSLAB], F16)
        stage = sb("stage", [P, RING, D], F32)
        region_w = sb("region_w", [P, 4 * NC * KVD], F16)
        region_o = sb("region_o", [P, 6176], F16)
        region_c = sb("region_c", [P, 16384], F16)
        region_q = sb("region_q", [P, 16384], F16)
        region_y = sb("region_y", [P, 2 * D], F32)
        region_s = sb("region_s", [P, 2 * D], F16)
        region_b = sb("region_b", [P, 2 * D], F32)

        def view(region, start, n, dt=F16):
            per = 2 if (dt == F32 and region.dtype == F16) else 1
            v = region[:, start:start + n * per]
            return v.bitcast(F32) if per == 2 else v

        wk = view(region_w, 0, 2 * NC * KVD).rearrange("p (h c n) -> p h c n", h=2, c=NC)
        wv = view(region_w, 2 * NC * KVD, 2 * NC * KVD).rearrange("p (h c n) -> p h c n", h=2, c=NC)
        wq = wk
        wo = view(region_w, 2 * NC * KVD, 2 * NJ * D).rearrange("p (h j n) -> p h j n", h=2, j=NJ)
        k_out = view(region_o, 0, NJ * 2 * QL).rearrange("p (j h s) -> p j h s", j=NJ, h=2)
        v_out = view(region_o, NJ * 2 * QL, KV * 4 * VW).rearrange("p (k t w) -> p k t w", k=KV, t=4)
        enc_f = view(region_o, 0, D, F32)
        enc = view(region_o, 2 * D, 2 * D).rearrange("p (h d) -> p h d", h=2)
        u_t = view(region_o, 4 * D, 2 * D).rearrange("p (h o) -> p h o", h=2)
        ctx_t = view(region_c, 0, 16384).rearrange("p (b c h s) -> p b c h s", b=2, c=NC, h=2)
        w_eff = view(region_c, 0, 16384).rearrange("p (h c n) -> p h c n", h=2, c=NC)
        q_head = view(region_c, 0, 8192).rearrange("p (b g h s) -> p b g h s", b=2, g=G, h=2)
        p_hi = view(region_c, 8192, NPB * QL).rearrange("p (r q) -> p r q", r=NPB)
        p_lo = view(region_c, 8192 + NPB * QL, NPB * QL).rearrange("p (r q) -> p r q", r=NPB)
        neg_max = view(region_c, 8192 + 2 * NPB * QL, 2 * TPB * 98).rearrange("p (b t n) -> p b t n", b=2, t=TPB)
        q2 = region_q[:, :]
        k_head = view(region_q, 0, 4 * SL).rearrange("p (b h s) -> p b h s", b=2, h=2)
        v_head = view(region_q, 4 * SL, 2 * NS * VW).rearrange("p (b s w) -> p b s w", b=2, s=NS)
        q_blk = view(region_q, 10776, NJ * 2 * QL).rearrange("p (j h s) -> p j h s", j=NJ, h=2)
        o_sum = view(region_q, 13848, TPB * HD, F32).rearrange("p (t d) -> p t d", t=TPB)
        o_raw = view(region_q, 14616, TPB * VW, F32).rearrange("p (t w) -> p t w", t=TPB)
        o_tok = view(region_o, 0, 2 * TPB * QG, F32).rearrange("p (b t n) -> p b t n", b=2, t=TPB)
        y_buf = region_y[:, :].rearrange("p (b d) -> p b d", b=2)
        p_f32 = region_y[:, :].rearrange("p (r q) -> p r q", r=NPF)
        q1_buf = region_s[:, :].rearrange("p (b d) -> p b d", b=2)
        bc_buf = region_b[:, :].rearrange("p (b d) -> p b d", b=2)
        coef = bc_buf[:, 0, 0:NC * R * E].rearrange("p (n e) -> p n e", e=E)
        mask_words = bc_buf[:, 1, 0:NC * R * E // 4].bitcast(I32)
        mask = bc_buf[:, 1, 0:NC * R * E // 4].bitcast(U8).rearrange("p (n e) -> p n e", e=E)
        y3_buf = region_b[:, 0:D]
        bias_rows = region_b[:, D:2 * D]
        o_t = region_b[:, 0:NJ * QL].bitcast(F16).rearrange("p (j h s) -> p j h s", j=NJ, h=2)

        rw = region_s[:, 0:NC * 2 * NE].rearrange("p (c n) -> p c n", c=NC)
        eb_hi = region_s[:, D:2 * D]
        eb_lo = region_b[0:NE, 3 * D // 2:2 * D].bitcast(F16)

        ident = sb("ident", [P, P], F32)
        ident_h = sb("ident_h", [P, P], F16)
        ones_h = sb("ones_h", [P, P], F16)
        par = sb("par", [P, 8], F32)
        tg = sb("tg", [P, 4], F32)
        sc = sb("sc", [P, 16], F32)
        w_sum = sb("w_sum", [P, NC, R], F32)
        bn = sb("bn", [P, 2, 6], F32)
        mv = sb("mv", [P, 2], F32)
        var_c = sb("var_c", [P, 4 * NT], F32)
        nmean = sb("nmean", [P, 4 * NT], F32)
        rstd = sb("rstd", [P, 4 * NT], F32)
        nmr = sb("nmr", [P, 4 * NT], F32)
        mhalf = sb("mhalf", [P, 1], F32)
        row_q = sb("row_q", [P, NT], F32)
        beta = sb("beta", [P, NT], F32)
        pre_max = sb("pre_max", [P, 2, TPB, SL // 512], F32)
        row_max = sb("row_max", [P, TPB], F32)
        den_inv = sb("den_inv", [P, TPB], F32)
        rb = sb("rb", [P, NE], F32)
        logit = sb("logit", [P, 2, NE], F32)
        prob = sb("prob", [P, 2, NE], F32)
        rest = sb("rest", [P, NE], F32)
        top8 = sb("top8", [P, TOP], F32)
        nmx = sb("nmx", [P, 2], F32)
        esum = sb("esum", [P, 2], F32)
        einv = sb("einv", [P, 1], F32)
        wsum8 = sb("wsum8", [P, 1], F32)
        ascale = sb("ascale", [P, 2], F32)
        w_tok = sb("w_tok", [P, 2 * NE], F16)
        w_exp = sb("w_exp", [P, P], F16)
        ps = ctx.enter_context(nc.psum_tensor("ps", [P, 8, 512], F32))

        S1, Z1, S2, Z2 = 4, 5, 6, 7
        RS1, RS2, ALPHA, CC, CR, CK, TGW, D1, D2, TMP = range(10)

        k_dram = nc.dram_tensor("k_scratch", (B, 2, KVD, SL), F16).ap()
        v_dram = nc.dram_tensor("v_scratch", (B, KV, P, NS, VW), F16).ap()

        par_ld, x_ld, id_ld, small_ld, enc_ld, bb_ld, rb_ld = (
            sem(n) for n in ("par_ld", "x_ld", "id_ld", "small_ld", "enc_ld", "bb_ld", "rb_ld"))
        ld = [sem(f"ld{s}") for s in range(RING)]
        const_ok, tanh_ok, scal_step, scal_ok = (sem(n) for n in ("const_ok", "tanh_ok", "scal_step", "scal_ok"))
        wsum_step, wsum_ok = sem("wsum_step"), sem("wsum_ok")
        w_hi, w_split = sem("w_hi"), sem("w_split")
        c_hi, c_split = sem("c_hi"), sem("c_split")
        n_aff, n_clip, n_done = sem("n_aff"), sem("n_clip"), sem("n_done")
        k_ready, k_hi_ok, k_lo_ok = sem("k_ready"), sem("k_hi_ok"), sem("k_lo_ok")
        v_ready, v_hi_ok, v_lo_ok = sem("v_ready"), sem("v_hi_ok"), sem("v_lo_ok")
        kv_stored = sem("kv_stored")
        bn_step, bn_go, ln_var, ln_pow, ln_ok = sem("bn_step"), sem("bn_go"), sem("ln_var"), sem("ln_pow"), sem("ln_ok")
        y1_ok, t1_ok, q1_clip, q1_ok, rowq_ok, beta_ok = (
            sem(n) for n in ("y1_ok", "t1_ok", "q1_clip", "q1_ok", "rowq_ok", "beta_ok"))
        xb_ok, xc_ok = sem("xb_ok"), sem("xc_ok")
        tq_ready, tq_ok, cs_ready, cs_ok = (sem(n) for n in ("tq_ready", "tq_ok", "cs_ready", "cs_ok"))
        f_used, u_hi, u_lo, enc_hi, enc_ok = (sem(n) for n in ("f_used", "u_hi", "u_lo", "enc_hi", "enc_ok"))
        dl_ready, we_sum, we_hi, we_ok = (sem(n) for n in ("dl_ready", "we_sum", "we_hi", "we_ok"))
        bias_ok, xbias_ok = sem("bias_ok"), sem("xbias_ok")
        xa_ready, xa_ok = sem("xa_ready"), sem("xa_ok")
        y2_ok, y3_ok = sem("y2_ok"), sem("y3_ok")
        tl_ready, tl_hi, tl_lo = sem("tl_ready"), sem("tl_hi"), sem("tl_lo")
        ff_ready, ff_ok = sem("ff_ready"), sem("ff_ok")
        k_ld = [sem(f"k_ld{b}") for b in range(B)]
        v_ld = [sem(f"v_ld{b}") for b in range(B)]
        q_ld = [sem(f"q_ld{b}") for b in range(B)]
        sp_ready, sp_hi, sp_free = sem("sp_ready"), sem("sp_hi"), sem("sp_free")
        pre_ready, pre_ok, max_step, nm_ok = sem("pre_ready"), sem("pre_ok"), sem("max_step"), sem("nm_ok")
        row_ready, row_ok = sem("row_ready"), sem("row_ok")
        sc_ready, exp_ok, plo_ok, pv_ok = (sem(n) for n in ("sc_ready", "exp_ok", "plo_ok", "pv_ok"))
        oraw_ok, osum_ok, o_ok = sem("oraw_ok"), sem("osum_ok"), sem("o_ok")
        y4_ok, t4_ready, t4_hi, t4_lo = (sem(n) for n in ("y4_ok", "t4_ready", "t4_hi", "t4_lo"))
        lg_ready, lg_step, lg_ok, ex_ok = (sem(n) for n in ("lg_ready", "lg_step", "lg_ok", "ex_ok"))
        top_step, top_go, wt_ok, wx_ready, wx_ok, ya_ok, xy_ok, mix_ready, fin_ok = (
            sem(n) for n in ("top_step", "top_go", "wt_ok", "wx_ready", "wx_ok", "ya_ok", "xy_ok", "mix_ready", "fin_ok"))
        out_st = sem("out_st")

        def cols(t, start, n):
            return t[:, bass.ds(start, n)]

        def x_tile(i, start=0, n=D):
            return cols(x_res, i * D + start, n)

        def slab(i, h):
            return cols(ln_t, i * HSLAB + h * NC * P, NC * P)

        def batch_slabs(b):
            return cols(ln_t, b * TPB * HSLAB, TPB * HSLAB).rearrange(
                "p (t h c k) -> p t h c k", t=TPB, h=2, c=NC)

        def bank(i, n=512, m=P):
            return ps[0:m, i, 0:n]

        def wide(i, dt=F32):
            if dt == F16:
                return ps[:, i, :].bitcast(F16)
            return ps[:, i:i + 2, :].rearrange("p b n -> p (b n)")

        def split_passes(a, b):
            return ((a(HI), b(HI)), (a(HI), b(LO)), (a(LO), b(HI)))

        CY_B, CY_F, CY_WB, CY_WQ0, CY_E, CY_G = 2, 10, 12, 14, 15, 16
        W_WQ0, W_E, W_G = 2 * RING, 3 * RING, 4 * RING
        EB_CUTS = (0, 384, 704, D)
        LG_STEPS, TOP_STEPS = 3, 6
        LN1, LN2, LN3, LN4 = 0, NT, 2 * NT, 3 * NT

        SLOTS = B * G
        PRE_AT = (2, 1, 1, 2, 1, 1, 2, 1, 1, 0, 0, 0)
        N_PRE = TPB * (SL // 512)
        MAX_STEP, ROW_STEP = 9, 10
        SP_ITER = 2 * NJ + 2 * (NJ + 8)
        SP0 = NJ
        SPQ1, SPT0, SPO0, SPQ0 = 0, NJ, 2 * NJ, 2 * NJ + 8
        Q1_TAKE = {(0, 8): 0, (1, 4): 1, (2, 0): 2}
        T0_STEPS = {7: 0, 8: 1, 9: 2}
        WO_STEPS = {5: {1: 0, 5: 1, 9: 2}, 6: {1: 3, 5: 4, 9: 5}, 7: {1: 6, 5: 7}}
        WO_SPLIT, WQ_SPLIT = 2, 5
        SPLIT_STEPS = {1: 0, 4: 1, 7: 2, 10: 3}

        def spare(k):
            return 6 + (SP0 + k) % 2

        def pre_bank(v, k):
            return 2 + (v + k) % 2

        block = ctx.enter_context(nc.Block())

        @block.sync
        def _(sp):
            def ring(s, dst, src, used=None, count=0):
                if used is not None:
                    sp.wait_ge(used, count)
                sp.dma_start(dst, src).then_inc(ld[s], 16)

            def pair(s, n):
                return stage[:, s, 0:2 * n].rearrange("p (c n) -> p c n", c=2)

            def load_ctx_t(t, used, count):
                b, half = t // 2, t % 2
                src = ctx_t_d[b].rearrange("(c p) s -> p c s", p=P)
                for s in range(RING):
                    ring(s, pair(s, QL), src[:, 2 * s:2 * s + 2, half * QL:(half + 1) * QL], used, count + s)

            def load_ctx(b):
                for n in range(NC):
                    used, count = (c_split, RING * (2 * b + 1) + n + 1) if n < RING else (n_done, NC * b + n - RING + 1)
                    ring(n % RING, stage[:, n % RING, :], ctx_d[b, n * P:(n + 1) * P, :], used, count)

            def load_x(b):
                for k in range(TPB):
                    i = TPB * b + k
                    sp.dma_start(x_tile(i), x_d[i * P:(i + 1) * P, :]).then_inc(x_ld, 16)

            def store_kv(t, b, s0):
                sp.wait_ge(k_lo_ok, NJ * (t + 1))
                for h in (HI, LO):
                    dst = k_dram[b, h].rearrange("(j p) s -> p j s", p=P)[:, :, s0:s0 + QL]
                    sp.dma_start(dst, k_out[:, :, h, :]).then_inc(kv_stored, 16)
                sp.wait_ge(v_lo_ok, 4 * (t + 1))
                dst = v_dram[b].rearrange("k p s w -> p k s w")[:, :, s0 // P:s0 // P + 4, :]
                sp.dma_start(dst, v_out[:, :, :, :]).then_inc(kv_stored, 16)

            sp.dma_start(par[:, :], par_d).then_inc(par_ld, 16)
            for s in range(RING):
                ring(s, pair(s, KVD), wk_d[:, 2 * s:2 * s + 2, :])
            for s in range(RING):
                ring(s, pair(s, KVD), wv_d[:, 2 * s:2 * s + 2, :], w_split, s + 1)
            load_ctx_t(0, w_split, RING + 1)
            sp.dma_start(ident[:, :], ident_d).then_inc(id_ld, 16)
            load_x(0)
            load_ctx_t(1, c_split, 1)
            sp.dma_start(coef, coef_d).then_inc(small_ld, 16)
            sp.dma_start(mask_words, mask_d).then_inc(small_ld, 16)
            sp.dma_start(rb[:, :], rb_d).then_inc(rb_ld, 16)
            load_ctx(0)
            store_kv(0, 0, 0)
            sp.wait_ge(x_ld, 16 * TPB)
            load_x(1)
            load_ctx_t(2, n_done, RING + 1)
            store_kv(1, 0, QL)
            load_ctx_t(3, c_split, 2 * RING + 1)
            load_ctx(1)
            store_kv(2, 1, 0)
            for n in range(NC):
                if n == RING:
                    store_kv(3, 1, QL)
                    sp.wait_ge(kv_stored, 4 * 48)
                    sp.dma_start(enc_f[0:R, :], enc_d).then_inc(enc_ld, 16)
                used, count = (n_done, NC + RING + n + 1) if n < RING else (f_used, n - RING + 1)
                ring(n % RING, stage[:, n % RING, :], ft_d[:, n, :], used, count)
            for n in range(NC):
                used, count = (f_used, RING + n + 1) if n < RING else (we_ok, n - RING + 1)
                ring(n % RING, stage[:, n % RING, :], wb_d[n * P:(n + 1) * P, :], used, count)
            sp.wait_ge(xc_ok, NT)
            sp.dma_start(bias_rows, bb_d).then_inc(bb_ld, 16)

            def load_wq(g, used, count):
                for s in range(RING):
                    ring(s, pair(s, QG), wq_d[bass.ds(g * P, P), 2 * s:2 * s + 2, :], used, count + s)

            def load_wo(g, used, count):
                for s in range(RING):
                    dst = stage[:, s, 0:NJ * 256].rearrange("p (j n) -> p j n", j=NJ)
                    ring(s, dst, wo_d[bass.ds(g * P, P), :, s * 256:(s + 1) * 256], used, count + s)

            def load_kv(g, b):
                src = k_dram[b, :, bass.ds(g * HD, HD), :].rearrange("h d s -> d h s")
                sp.dma_start(k_head[0:HD, b, :, :], src).then_inc(k_ld[b], 16)
                src = v_dram[b, bass.ds(g, 1), :, :, :].rearrange("k p s w -> (k p) (s w)")
                sp.dma_start(v_head[:, b, :, :].rearrange("p s w -> p (s w)"), src).then_inc(v_ld[b], 16)

            def load_q(first, b):
                for j in range(NJ):
                    sp.wait_ge(sp_free, first + j + 1)
                    row = j * P
                    while row < (j + 1) * P:
                        h, d = row // HD, row % HD
                        n = min(HD - d, (j + 1) * P - row)
                        sp.dma_start(q_head[d:d + n, b, h, :, :], q_blk[row - j * P:row - j * P + n, j, :, :]
                                     ).then_inc(q_ld[b], 16)
                        row += n

            load_wq(0, we_ok, RING + 1)
            for b in range(B):
                store_kv(4 + b, b, CTX)
            ring(0, stage[:, 0, 0:NC * NE], rw_d, w_split, W_WQ0 + 1)
            for s in range(1, RING):
                c0, c1 = EB_CUTS[s - 1:s + 1]
                ring(s, stage[:, s, 0:c1 - c0], eb_d[:, c0:c1], w_split, W_WQ0 + s + 1)
            sp.wait_ge(kv_stored, 6 * 48)
            sp.wait_ge(xa_ok, 2 * NT)
            load_kv(0, 0)
            load_q(0, 0)

            def iteration(g, last):
                sp.wait_ge(pv_ok, NPB + SLOTS * NS * g)
                load_kv(g, 1)
                load_wo(g, w_split, W_G + 2 * RING * g - RING + 1)
                load_q(SP0 + SP_ITER * g + SPQ1, 1)
                if not last:
                    load_wq(g + 1, w_split, W_G + 2 * RING * g + 1)
                    sp.wait_ge(pv_ok, NPB + SLOTS * NS * g + G * NS)
                    load_kv(g + 1, 0)
                    load_q(SP0 + SP_ITER * g + SPQ0, 0)

            with sp.Fori(0, KV - 1) as g:
                iteration(g, False)
            iteration(KV - 1, True)

            with sp.Fori(0, NT) as i:
                sp.wait_ge(fin_ok, 2 * i + 2)
                sp.dma_start(out_d[bass.ds(i * P, P), :], x_tile(i)).then_inc(out_st, 16)
            sp.wait_ge(out_st, 16 * NT)

        @block.tensor
        def _(pe):
            def passes(out, pairs, first, last):
                for n, (a, b) in enumerate(pairs):
                    ins = nc.tensor.matmul(out, a, b, start=first and n == 0, stop=last and n == len(pairs) - 1)
                return ins

            def by_tile(out):
                return out.rearrange("p (t k) -> p t k", t=TPB)

            def project_kv(t, chunk_wait, x_of, tile_of, shape=lambda out: out):
                pe.wait_ge(k_lo_ok, NJ * t)
                for c in range(NC):
                    chunk_wait(c)
                    for j in range(NJ):
                        ins = passes(shape(bank(j)), split_passes(lambda h: wk[:, h, c, j * P:(j + 1) * P],
                                                                  lambda h: x_of(c, h)), c == 0, c == NC - 1)
                        if c == NC - 1:
                            ins.then_inc(k_ready, 1)
                for tt in range(TPB):
                    pe.wait_ge(v_lo_ok, 4 * t + max(0, tt - 1))
                    for c in range(NC):
                        ins = passes(bank(3 + tt % 2, KVD), split_passes(lambda h: tile_of(tt, c, h),
                                                                         lambda h: wv[:, h, c, :]), c == 0, c == NC - 1)
                    ins.then_inc(v_ready, 1)

            def transpose_q1(i, k):
                pe.wait_ge(q1_ok, i + 1)
                for c in range(NC):
                    ins = nc.tensor.transpose(wide((5, 0)[k % 2], F16)[:, c * P:(c + 1) * P],
                                              q1_buf[:, k % 2, c * P:(c + 1) * P], ident_h[:, :])
                ins.then_inc(tq_ready, 1)

            pe.sem_inc(pv_ok, NPB)
            pe.wait_ge(const_ok, 2)
            pe.wait_ge(w_split, 2 * RING)
            with pe.Fori(0, B) as b:
                for half in range(2):
                    t = 2 * b + half

                    def chunk(c):
                        if c == 0:
                            pe.wait_ge(tq_ok, TPB * b + 2 * half)
                        if c % 2 == 0:
                            pe.wait_ge(c_split, RING * t + c // 2 + 1)

                    project_kv(t, chunk, lambda c, h: ctx_t[:, half, c, h, :],
                               lambda tt, c, h: ctx_t[:, half, c, h, tt * P:(tt + 1) * P])
                    for k in (2 * half, 2 * half + 1):
                        if k % 2 == 1:
                            pe.wait_ge(k_lo_ok, NJ * (t + 1))
                        pe.wait_ge(tq_ok, TPB * b + 2 * half)
                        transpose_q1(TPB * b + k, k)
                pe.wait_ge(n_done, NC * (b + 1))
                pe.wait_ge(cs_ok, 2 * b)
                for half in range(2):
                    for c in range(NC):
                        ins = nc.tensor.matmul(bank(6 + half), ones_h[:, :],
                                               cols(q2, b * NC * D + c * D + half * 512, 512),
                                               start=c == 0, stop=c == NC - 1)
                    ins.then_inc(cs_ready, 1)

            pe.wait_ge(wsum_ok, 1)
            pe.wait_ge(k_lo_ok, 4 * NJ)
            for c in range(NC):
                pe.wait_ge(ld[c % RING], 16 * (CY_F + c // RING + 1))
                for half in range(2):
                    ins = nc.tensor.matmul(bank(1 + half, 512, R), w_sum[:, c, :],
                                           stage[:, c % RING, half * 512:(half + 1) * 512],
                                           start=c == 0, stop=c == NC - 1)
                ins.then_inc(f_used, 1)
            pe.wait_ge(enc_ok, 1)
            pe.wait_ge(u_lo, 2)
            pe.wait_ge(cs_ok, 2 * B)
            pe.wait_ge(v_lo_ok, 4 * 4)
            pe.wait_ge(tq_ok, NT)
            for c in range(NC):
                if c >= 2:
                    pe.wait_ge(we_sum, 2 * (c - 1))
                for half in range(2):
                    ins = passes(bank((4, 6)[c % 2] + half),
                                 split_passes(lambda h: enc[0:R, h, c * P:(c + 1) * P],
                                              lambda h: u_t[0:R, h, half * 512:(half + 1) * 512]), True, True)
                    ins.then_inc(dl_ready, 1)

            with pe.Fori(0, B) as b:
                for k in range(TPB):
                    i = TPB * b + k
                    pe.wait_ge(xa_ok, 2 * (TPB * b + max(0, k - 1)))
                    for half in range(2):
                        for c in range(NC):
                            ins = nc.tensor.matmul(bank(2 * (k % 2) + half), cols(ln_t, i * HSLAB + c * P, P),
                                                   cols(q2, b * NC * D + c * D + half * 512, 512),
                                                   start=c == 0, stop=c == NC - 1)
                        ins.then_inc(xa_ready, 1)

            def transpose_y(src, n):
                pe.wait_ge(tl_lo, n)
                for c in range(NC):
                    ins = nc.tensor.transpose(wide(6)[:, c * P:(c + 1) * P], src[:, c * P:(c + 1) * P], ident[:, :])
                ins.then_inc(tl_ready, 1)

            def ffn_half(i, half):
                if half or not isinstance(i, int) or i > 0:
                    pe.wait_ge(ff_ok, 2 * i + half - 1)
                for c in range(NC):
                    ins = passes(bank(4 + half),
                                 split_passes(lambda h: cols(ln_t, i * HSLAB + (h * NC + c) * P, P),
                                              lambda h: w_eff[:, h, c, half * 512:(half + 1) * 512]),
                                 c == 0, c == NC - 1)
                ins.then_inc(ff_ready, 1)

            pe.wait_ge(we_sum, 2 * NC)
            pe.wait_ge(y2_ok, 1)
            transpose_y(y_buf[:, 0, :], 0)
            pe.wait_ge(y2_ok, 2)
            transpose_y(y_buf[:, 1, :], 1)
            pe.wait_ge(we_ok, NC)
            for half in range(2):
                ffn_half(0, half)
            pe.wait_ge(y2_ok, 3)
            transpose_y(y_buf[:, 0, :], 2)
            for half in range(2):
                ffn_half(1, half)

            def ffn_step(i, buf):
                if buf is not None:
                    pe.wait_ge(y2_ok, i + 2)
                    transpose_y(y_buf[:, buf, :], 2 * i - 1)
                ffn_half(i, 0)
                pe.wait_ge(y3_ok, i - 1)
                transpose_y(y3_buf, 2 * i if buf is not None else 2 * i - 1)
                ffn_half(i, 1)

            with pe.Fori(0, 2) as r:
                for k in range(2):
                    ffn_step(2 * r + 2 + k, (k + 1) % 2)
            ffn_step(6, 1)
            ffn_step(7, None)

            with pe.Fori(0, B) as b:
                pe.wait_ge(y3_ok, 7 + b)
                transpose_y(y3_buf, 14 + b)
                pe.wait_ge(tl_lo, 14 + 2 * b)
                pe.wait_ge(ff_ok, 2 * NT)
                src = batch_slabs(b)
                project_kv(4 + b, lambda c: None, lambda c, h: src[:, :, h, c, :],
                           lambda tt, c, h: cols(ln_t, (TPB * b + tt) * HSLAB + (h * NC + c) * P, P), by_tile)

            def q_parts(g, b, k0):
                src = ln_t[:, b * TPB * HSLAB:(b + 1) * TPB * HSLAB].rearrange(
                    "p (t h c k) -> p t h c k", t=TPB, h=2, c=NC)
                for j in range(NJ):
                    for c in range(NC):
                        for n, (hw, hx) in enumerate(((HI, HI), (HI, LO), (LO, HI))):
                            yield j, c, n, wq[:, hw, c, j * P:(j + 1) * P], src[:, :, hx, c, :]

            def q_product(base, k0, part):
                j, c, n, a, x = part
                if c == 0 and n == 0:
                    pe.wait_ge(sp_free, base + k0 + j - 1)
                ins = nc.tensor.matmul(by_tile(bank(spare(k0 + j))), a, x,
                                       start=c == 0 and n == 0, stop=c == NC - 1 and n == 2)
                if c == NC - 1 and n == 2:
                    ins.then_inc(sp_ready, 1)

            def o_transposes(base, k, b, j):
                pe.wait_ge(sp_free, base + k - 1)
                for qt in range(TPB):
                    ins = nc.tensor.transpose(bank(spare(k))[:, qt * P:(qt + 1) * P],
                                              o_tok[:, b, qt, j * P:(j + 1) * P], ident[:, :])
                ins.then_inc(sp_ready, 1)

            def out_product(base, k, w):
                if w == 0:
                    pe.wait_ge(sp_free, base + k)
                else:
                    pe.wait_ge(sp_free, base + k - 1)
                qt, half = w // 2, w % 2
                for j in range(NJ):
                    ins = passes(bank(spare(k)), split_passes(lambda h: o_t[:, j, h, qt * P:(qt + 1) * P],
                                                              lambda h: wo[:, h, j, half * 512:(half + 1) * 512]),
                                 j == 0, j == NJ - 1)
                ins.then_inc(sp_ready, 1)

            def pre_product(v, s, b, h, k):
                if k == 0:
                    pe.wait_ge(pre_ok, N_PRE * v)
                elif k == 1:
                    pe.wait_ge(row_ok, v)
                else:
                    pe.wait_ge(pre_ok, N_PRE * v + k - 1)
                qt, sb_ = k // 3, k % 3
                nc.tensor.matmul(bank(pre_bank(s, k)), q_head[0:HD, b, h, HI, qt * P:(qt + 1) * P],
                                 k_head[0:HD, b, HI, sb_ * 512:(sb_ + 1) * 512], start=True, stop=True
                                 ).then_inc(pre_ready, 1)

            def row_transpose(v, s):
                pe.wait_ge(nm_ok, v + 1)
                for qt in range(TPB):
                    ins = nc.tensor.matmul(bank(pre_bank(s, N_PRE), 512, HD + 1)[:, qt * P:(qt + 1) * P],
                                           neg_max[:, s % 2, qt, 0:HD + 1], ident_h[:, :], start=True, stop=True)
                ins.then_inc(row_ready, 1)

            def score_block(u, n, b, h, i):
                if i == 0:
                    pe.wait_ge(row_ok, u + 1)
                pe.wait_ge(exp_ok, n + 1)
                ks = slice(i * P, (i + 1) * P)
                out = bank(i % 2)
                nc.tensor.matmul(out, k_head[0:HD + 1, b, HI, ks], q_head[0:HD + 1, b, h, HI, :], start=True, stop=False)
                nc.tensor.matmul(out, k_head[0:HD, b, HI, ks], q_head[0:HD, b, h, LO, :], start=False, stop=False)
                nc.tensor.matmul(out, k_head[0:HD, b, LO, ks], q_head[0:HD, b, h, HI, :], start=False, stop=True
                                 ).then_inc(sc_ready, 1)

            def pv_block(g, u, n, b, i):
                if i == 0:
                    pe.wait_ge(oraw_ok, u)
                    pe.wait_ge(v_ld[b], 16 * (g + 1))
                pe.wait_ge(plo_ok, NPF + n + 1)
                for qt in range(TPB):
                    tok = slice(qt * P, (qt + 1) * P)
                    out = bank(4 + qt // 2)[:, (qt % 2) * VW:(qt % 2 + 1) * VW]
                    nc.tensor.matmul(out, p_hi[:, i % NPB, tok], v_head[:, b, i, :],
                                     start=i == 0 and qt % 2 == 0, stop=False, skip_group_check=True)
                    ins = nc.tensor.matmul(out[:, 0:HD + 1], p_lo[:, i % NPB, tok], v_head[:, b, i, 0:HD + 1],
                                           start=False, stop=i == NS - 1, skip_group_check=True)
                ins.then_inc(pv_ok, 1)

            pe.wait_ge(w_split, W_WQ0 + RING)
            pe.wait_ge(tl_lo, 2 * NT)
            pe.wait_ge(k_lo_ok, 6 * NJ)
            pe.wait_ge(v_lo_ok, 6 * 4)
            for part in q_parts(0, 0, 0):
                j, c, n, a, x = part
                if j == 2 and c == 0 and n == 0:
                    pe.wait_ge(sp_free, 1)
                ins = nc.tensor.matmul(by_tile(bank(6 + j % 2)), a, x, start=c == 0 and n == 0, stop=c == NC - 1 and n == 2)
                if c == NC - 1 and n == 2:
                    ins.then_inc(sp_ready, 1)
            pe.wait_ge(k_ld[0], 16)
            pe.wait_ge(q_ld[0], 16 * 6)
            for k in range(N_PRE):
                pre_product(0, 0, 0, 0, k)
            row_transpose(0, 0)

            def iteration(g, last):
                base = SP0 + SP_ITER * g
                u0, n0 = SLOTS * g, SLOTS * NS * g
                queries = list(q_parts(g, 1, SPQ1))
                for s in range(SLOTS):
                    b, h = s // G, s % G
                    nb, nh = (s + 1) // G, (s + 1) % G
                    k = 0
                    if s == G - 1:
                        pe.wait_ge(k_ld[1], 16 * (g + 1))
                        pe.wait_ge(q_ld[1], 16 * 6 * (g + 1))
                    if s == 5:
                        pe.wait_ge(w_split, W_G + 2 * RING * g + RING)
                    for i in range(NS):
                        score_block(u0 + s, n0 + NS * s + i, b, h, i)
                        if s < SLOTS - 1:
                            for _ in range(PRE_AT[i]):
                                pre_product(u0 + s + 1, s + 1, nb, nh, k)
                                k += 1
                            if i == ROW_STEP:
                                row_transpose(u0 + s + 1, s + 1)
                        if i >= LAG:
                            pv_block(g, u0 + s, n0 + NS * s + i - LAG, b, i - LAG)
                        elif s > 0:
                            pv_block(g, u0 + s - 1, n0 + NS * s + i - LAG, (s - 1) // G, NS + i - LAG)
                        for _ in range(3):
                            if s < 2:
                                q_product(base, SPQ1, queries.pop(0))
                        if s == G and i in T0_STEPS:
                            if T0_STEPS[i] == 0:
                                pe.wait_ge(o_ok, u0 + G)
                            o_transposes(base, SPT0 + T0_STEPS[i], 0, T0_STEPS[i])
                        if s in WO_STEPS and i in WO_STEPS[s]:
                            out_product(base, SPO0 + WO_STEPS[s][i], WO_STEPS[s][i])
                for i in range(NS - LAG, NS):
                    pv_block(g, u0 + SLOTS - 1, n0 + NS * (SLOTS - 1) + i, 1, i)
                k = SPQ0
                if not last:
                    pe.wait_ge(w_split, W_G + 2 * RING * (g + 1))
                    for part in q_parts(g, 0, k):
                        q_product(base, k, part)
                    k += NJ
                pe.wait_ge(o_ok, u0 + SLOTS)
                for j in range(NJ):
                    o_transposes(base, k, 1, j)
                    k += 1
                m = 0
                for w in range(8):
                    out_product(base, k, w)
                    k += 1
                    if not last and 2 <= w <= 5:
                        if m == 0:
                            pe.wait_ge(k_ld[0], 16 * (g + 2))
                            pe.wait_ge(q_ld[0], 16 * 6 * (g + 2))
                        for _ in range(3):
                            pre_product(u0 + SLOTS, 0, 0, 0, m)
                            m += 1
                    if not last and w == 6:
                        row_transpose(u0 + SLOTS, 0)

            with pe.Fori(0, KV - 1) as g:
                iteration(g, False)
            iteration(KV - 1, True)

            sp_end = SP0 + SP_ITER * KV - NJ
            pe.wait_ge(sp_free, sp_end)
            def expert_transposes(i, k):
                pe.wait_ge(y4_ok, i + 1)
                if not isinstance(i, int) or i > 1:
                    pe.wait_ge(t4_lo, i - 1)
                for c in range(NC):
                    ins = nc.tensor.transpose(wide(2 * k)[:, c * P:(c + 1) * P],
                                              y_buf[:, k, c * P:(c + 1) * P], ident[:, :])
                ins.then_inc(t4_ready, 1)

            def router(i):
                pe.wait_ge(t4_lo, i + 1)
                if not isinstance(i, int) or i > 0:
                    pe.wait_ge(lg_step, LG_STEPS * i - 1)
                for c in range(NC):
                    nc.tensor.matmul(bank(4, 2 * NE), cols(ln_t, i * HSLAB + c * P, P), rw[:, c, :],
                                     start=c == 0, stop=False, skip_group_check=True)
                    ins = nc.tensor.matmul(bank(4, NE), cols(ln_t, i * HSLAB + (NC + c) * P, P), rw[:, c, 0:NE],
                                           start=False, stop=c == NC - 1, skip_group_check=True)
                ins.then_inc(lg_ready, 1)

            def expert_step(i, k, ahead):
                if ahead:
                    expert_transposes(i + 1, 1 - k)
                pe.wait_ge(wt_ok, i + 1)
                nc.tensor.transpose(wide(5, F16)[:, 0:P], w_tok[:, :], ident_h[:, :]).then_inc(wx_ready, 1)
                if ahead:
                    router(i + 1)
                pe.wait_ge(wx_ok, i + 1)
                pe.wait_ge(fin_ok, 2 * i)
                for half in range(2):
                    hs = slice(half * 512, (half + 1) * 512)
                    nc.tensor.matmul(bank(6 + half), w_exp[:, :], eb_hi[:, hs], start=True, stop=False)
                    nc.tensor.matmul(bank(6 + half), w_exp[0:NE, :], eb_lo[:, hs], start=False, stop=True
                                     ).then_inc(mix_ready, 1)

            expert_transposes(0, 0)
            router(0)
            with pe.Fori(0, NT // 2 - 1) as r:
                for k in range(2):
                    expert_step(2 * r + k, k, True)
            expert_step(NT - 2, 0, True)
            expert_step(NT - 1, 1, False)

        @block.scalar
        def _(act):
            def copy(out, in_):
                return nc.scalar.activation(out, in_, ACT.Copy)

            def affine(out, in_, scale, bias):
                return nc.scalar.activation(out, in_, ACT.Identity, scale=scale, bias=bias)

            def keys(t):
                act.wait_ge(kv_stored, 48 * t)
                for j in range(NJ):
                    act.wait_ge(k_ready, NJ * t + j + 1)
                    copy(k_out[:, j, HI, :], bank(j)).then_inc(k_hi_ok, 1)

            def values(t, tt):
                act.wait_ge(v_ready, 4 * t + tt + 1)
                copy(v_out[:, :, tt, 0:HD], bank(3 + tt % 2, KVD).rearrange("p (k d) -> p k d", k=KV)
                     ).then_inc(v_hi_ok, 1)

            def normalise(out, i, ln):
                act.wait_ge(ln_ok, ln + i + 1)
                return affine(out, x_tile(i), cols(rstd, ln + i, 1), cols(nmr, ln + i, 1))

            act.sem_inc(exp_ok, 2)
            act.wait_ge(par_ld, 16)
            nc.scalar.activation(tg[:, :], par[:, 0:4], ACT.Tanh).then_inc(tanh_ok, 1)
            for n in range(2 * RING):
                s = n % RING
                act.wait_ge(ld[s], 16 * (n // RING + 1))
                w = (wk, wv)[n // RING]
                copy(w[:, HI, 2 * s:2 * s + 2, :], stage[:, s, 0:2 * KVD].rearrange("p (c n) -> p c n", c=2)
                     ).then_inc(w_hi, 1)
            act.wait_ge(scal_ok, 1)
            act.wait_ge(id_ld, 16)
            copy(ident_h[:, :], ident[:, :]).then_inc(const_ok, 1)

            with act.Fori(0, B) as b:
                for half in range(2):
                    t = 2 * b + half
                    act.wait_ge(v_ready, 2 * TPB * b)
                    for s in range(RING):
                        act.wait_ge(ld[s], 64 * b + 16 * (CY_B + half + 1))
                        copy(ctx_t[:, half, 2 * s:2 * s + 2, HI, :],
                             stage[:, s, :].rearrange("p (c n) -> p c n", c=2)).then_inc(c_hi, 1)

                def scale_ctx(n):
                    s = n % RING
                    act.wait_ge(ld[s], 64 * b + 16 * (CY_B + 2 + n // RING + 1))
                    affine(stage[:, s, :], stage[:, s, :], sc[:, RS2:RS2 + 1], par[:, Z2:Z2 + 1]).then_inc(n_aff, 1)

                def scale_x(k):
                    i = TPB * b + k
                    act.wait_ge(q1_ok, TPB * b + max(0, k - 1))
                    normalise(y_buf[:, k % 2, :], i, LN1).then_inc(y1_ok, 1)
                    act.wait_ge(y1_ok, i + 1)
                    affine(y_buf[:, k % 2, :], y_buf[:, k % 2, :], sc[:, RS1:RS1 + 1], par[:, Z1:Z1 + 1]
                           ).then_inc(t1_ok, 1)

                def add_beta(k):
                    i = TPB * b + k
                    act.wait_ge(beta_ok, i + 1)
                    nc.scalar.activation(x_tile(i), x_tile(i), ACT.Identity, bias=cols(beta, i, 1)).then_inc(xb_ok, 1)

                def take_q1(k):
                    i = TPB * b + k
                    act.wait_ge(tq_ready, i + 1)
                    copy(slab(i, HI), wide((5, 0)[k % 2], F16)).then_inc(tq_ok, 1)

                t = 2 * b
                for n in range(4):
                    scale_ctx(n)
                scale_x(0)
                scale_x(1)
                keys(t)
                values(t, 0)
                scale_ctx(4)
                scale_ctx(5)
                values(t, 1)
                scale_ctx(6)
                scale_ctx(7)
                values(t, 2)
                values(t, 3)
                take_q1(0)
                take_q1(1)
                scale_x(2)
                scale_x(3)
                keys(t + 1)
                for tt in range(4):
                    values(t + 1, tt)
                    add_beta(tt)
                take_q1(2)
                take_q1(3)
                act.wait_ge(wsum_ok, 1)
                for half in range(2):
                    act.wait_ge(cs_ready, 2 * b + half + 1)
                    nc.scalar.activation(cols(region_b, b * D + half * 512, 512), bank(6 + half), ACT.Copy,
                                         scale=sc[:, CC:CC + 1]).then_inc(cs_ok, 1)

            act.wait_ge(enc_ld, 16)
            copy(enc[0:R, HI, :], enc_f[0:R, :]).then_inc(enc_hi, 1)
            act.wait_ge(f_used, NC)
            for half in range(2):
                copy(u_t[0:R, HI, half * 512:(half + 1) * 512], bank(1 + half, 512, R)).then_inc(u_hi, 1)
            for c in range(NC):
                act.wait_ge(we_sum, 2 * (c + 1))
                copy(w_eff[:, HI, c, :], stage[:, c % RING, :]).then_inc(we_hi, 1)
            act.wait_ge(bb_ld, 16)
            nc.scalar.activation(bias_rows, bias_rows, ACT.Copy, scale=tg[:, 2:3]).then_inc(bias_ok, 1)

            def take_high(i, n):
                act.wait_ge(tl_ready, n + 1)
                copy(slab(i, HI), wide(6)).then_inc(tl_hi, 1)

            def norm2(i, buf, before):
                if before is not None:
                    act.wait_ge(tl_ready, before)
                normalise(buf, i, LN2).then_inc(y2_ok, 1)

            def norm3(i, before):
                if before is not None:
                    act.wait_ge(tl_ready, before)
                normalise(y3_buf, i, LN3).then_inc(y3_ok, 1)

            norm2(0, y_buf[:, 0, :], None)
            norm2(1, y_buf[:, 1, :], None)
            take_high(0, 0)
            norm2(2, y_buf[:, 0, :], 1)
            take_high(1, 1)
            norm2(3, y_buf[:, 1, :], 2)
            take_high(2, 2)
            act.wait_ge(xc_ok, NT)

            def ffn_step(i, par):
                if par is not None:
                    take_high(i + 1, 2 * i - 1)
                    if not isinstance(i, int):
                        norm2(i + 2, y_buf[:, 1 - par, :], 2 * i - 1)
                norm3(i - 2, 2 * i - 1)
                take_high(i - 2, 2 * i if par is not None else 2 * i - 1)

            with act.Fori(0, 2) as r:
                for k in range(2):
                    ffn_step(2 * r + 2 + k, (k + 1) % 2)
            ffn_step(6, 1)
            ffn_step(7, None)
            with act.Fori(0, B) as b:
                norm3(6 + b, 14 + b)
                take_high(6 + b, 14 + b)
                keys(4 + b)
                for tt in range(TPB):
                    values(4 + b, tt)

            def wq_hi(cycle, s):
                act.wait_ge(ld[s], 16 * (cycle + 1))
                copy(wq[:, HI, 2 * s:2 * s + 2, :], stage[:, s, 0:2 * QG].rearrange("p (c n) -> p c n", c=2)
                     ).then_inc(w_hi, 1)

            def wo_hi(cycle, s):
                act.wait_ge(ld[s], 16 * (cycle + 1))
                copy(wo[:, HI, :, s * 256:(s + 1) * 256], stage[:, s, 0:NJ * 256].rearrange("p (j n) -> p j n", j=NJ)
                     ).then_inc(w_hi, 1)

            def take_q(first, k, j):
                act.wait_ge(sp_ready, first + 1)
                copy(q_blk[:, j, HI, :], bank(spare(k))).then_inc(sp_hi, 1)

            def take_o(first, k, j):
                act.wait_ge(sp_ready, first + 1)
                copy(o_t[:, j, HI, :], bank(spare(k))).then_inc(sp_hi, 1)

            def take_row(v, s, b, h):
                act.wait_ge(row_ready, v + 1)
                copy(q_head[HD:HD + 1, b, h, HI, :], ps[HD:HD + 1, pre_bank(s, N_PRE), :]).then_inc(row_ok, 1)

            def take_sums(u):
                act.wait_ge(pv_ok, NPB + NS * (u + 1))
                act.wait_ge(o_ok, u)
                for k in range(2):
                    ins = copy(o_raw[:, 2 * k:2 * k + 2, :].rearrange("p t w -> p (t w)"), bank(4 + k, 2 * VW))
                ins.then_inc(oraw_ok, 1)

            act.wait_ge(k_ready, 6 * NJ)
            act.wait_ge(v_ready, 6 * 4)
            for s in range(RING):
                wq_hi(CY_WQ0, s)
            act.wait_ge(ld[0], 16 * (CY_E + 1))
            copy(rw[:, :, 0:NE], stage[:, 0, 0:NC * NE].rearrange("p (c n) -> p c n", c=NC)).then_inc(w_hi, 1)
            for s in range(1, RING):
                c0, c1 = EB_CUTS[s - 1:s + 1]
                act.wait_ge(ld[s], 16 * (CY_E + 1))
                copy(eb_hi[:, c0:c1], stage[:, s, 0:c1 - c0]).then_inc(w_hi, 1)
            for j in range(NJ):
                act.wait_ge(sp_ready, j + 1)
                copy(q_blk[:, j, HI, :], bank(6 + j % 2)).then_inc(sp_hi, 1)
            take_row(0, 0, 0, 0)

            def iteration(g, last):
                base = SP0 + SP_ITER * g
                u0, n0 = SLOTS * g, SLOTS * NS * g
                for s in range(SLOTS):
                    for i in range(NS):
                        n = n0 + NS * s + i
                        act.wait_ge(sc_ready, n + 1)
                        act.wait_ge(plo_ok, n + 1)
                        nc.scalar.activation(p_f32[:, i % NPF, :], bank(i % 2), ACT.Exp, scale=SCALE)
                        act.wait_ge(pv_ok, n + 1)
                        nc.scalar.activation(p_hi[:, i % NPB, :], bank(i % 2), ACT.Exp, scale=SCALE).then_inc(exp_ok, 1)
                        if s > 0 and i == LAG:
                            take_sums(u0 + s - 1)
                        if (s, i) in Q1_TAKE:
                            j = Q1_TAKE[s, i]
                            take_q(base + SPQ1 + j, SPQ1 + j, j)
                        if s == G and i - 1 in T0_STEPS:
                            j = T0_STEPS[i - 1]
                            take_o(base + SPT0 + j, SPT0 + j, j)
                        if s == WO_SPLIT and i in SPLIT_STEPS:
                            wo_hi(CY_G + 2 * g, SPLIT_STEPS[i])
                        if s == WQ_SPLIT and i in SPLIT_STEPS and not last:
                            wq_hi(CY_G + 1 + 2 * g, SPLIT_STEPS[i])
                        if s < SLOTS - 1 and i == ROW_STEP + 1:
                            take_row(u0 + s + 1, s + 1, (s + 1) // G, (s + 1) % G)
                take_sums(u0 + SLOTS - 1)
                k = SPQ0
                if not last:
                    for j in range(NJ):
                        take_q(base + k, k, j)
                        k += 1
                for j in range(NJ):
                    take_o(base + k, k, j)
                    k += 1
                if not last:
                    take_row(u0 + SLOTS, 0, 0, 0)

            with act.Fori(0, KV - 1) as g:
                iteration(g, False)
            iteration(KV - 1, True)

            act.wait_ge(plo_ok, NPF + SLOTS * NS * KV)
            def expert_norm(i, k):
                if not isinstance(i, int) or i > 1:
                    act.wait_ge(xy_ok, i - 1)
                normalise(y_buf[:, k, :], i, LN4).then_inc(y4_ok, 1)

            def expert_high(i, k):
                act.wait_ge(t4_ready, i + 1)
                copy(slab(i, HI), wide(2 * k)).then_inc(t4_hi, 1)

            def expert_step(i, k, ahead):
                if ahead:
                    expert_norm(i + 1, 1 - k)
                act.wait_ge(lg_ok, i + 1)
                nc.scalar.activation(prob[:, k, :], logit[:, k, :], ACT.Exp, bias=nmx[:, k:k + 1],
                                     accum_out=esum[:, k:k + 1]).then_inc(ex_ok, 1)
                if ahead:
                    expert_high(i + 1, 1 - k)
                act.wait_ge(wx_ready, i + 1)
                act.wait_ge(mix_ready, 2 * i)
                copy(w_exp[:, :], wide(5, F16)[:, 0:P]).then_inc(wx_ok, 1)
                nc.scalar.activation(y_buf[:, k, :], y_buf[:, k, :], ACT.Copy, scale=ascale[:, k:k + 1]
                                     ).then_inc(ya_ok, 1)

            expert_norm(0, 0)
            expert_high(0, 0)
            with act.Fori(0, NT // 2 - 1) as r:
                for k in range(2):
                    expert_step(2 * r + k, k, True)
            expert_step(NT - 2, 0, True)
            expert_step(NT - 1, 1, False)

        @block.vector
        def _(dve):
            def minus(out, a, b):
                return nc.vector.tensor_tensor(out, a, b, ALU.subtract)

            def stats(i, ln):
                n = ln + i
                dve.sem_inc(bn_go, 1)
                for half in range(2):
                    ins = nc.vector.bn_stats(bn[:, half, :], x_tile(i, half * 512, 512))
                ins.then_inc(bn_step, 1)
                dve.wait_ge(bn_step, 2 * n + 1)
                dve.sem_inc(bn_go, 1)
                nc.vector.bn_aggr(mv[:, :], bn[:, :, :]).then_inc(bn_step, 1)
                dve.wait_ge(bn_step, 2 * n + 2)
                nc.vector.tensor_scalar(cols(nmean, n, 1), mv[:, 0:1], -1.0, None, ALU.mult)
                nc.vector.tensor_scalar(cols(var_c, n, 1), mv[:, 1:2], EPS, None, ALU.add).then_inc(ln_var, 1)

            def keys(t):
                for j in range(NJ):
                    dve.wait_ge(k_hi_ok, NJ * t + j + 1)
                    minus(k_out[:, j, LO, :], bank(j), k_out[:, j, HI, :]).then_inc(k_lo_ok, 1)

            def values(t, tt):
                dve.wait_ge(v_hi_ok, 4 * t + tt + 1)
                minus(v_out[:, :, tt, HD + 1:VW], bank(3 + tt % 2, KVD).rearrange("p (k d) -> p k d", k=KV),
                      v_out[:, :, tt, 0:HD]).then_inc(v_lo_ok, 1)

            def col(i):
                return sc[:, i:i + 1]

            def scalar(i, out, in_, s1, s2, op0, op1=ALU.bypass):
                nc.vector.tensor_scalar(col(out), in_, s1, s2, op0, op1).then_inc(scal_step, 1)
                dve.wait_ge(scal_step, i + 1)

            nc.vector.memset(v_out[:, :, :, HD:HD + 1], 1.0)
            nc.vector.memset(ones_h[:, :], 1.0).then_inc(const_ok, 1)
            dve.wait_ge(par_ld, 16)
            dve.wait_ge(tanh_ok, 1)
            nc.vector.reciprocal(col(RS1), par[:, S1:S1 + 1])
            nc.vector.reciprocal(col(RS2), par[:, S2:S2 + 1])
            scalar(0, ALPHA, tg[:, 0:1], par[:, S1:S1 + 1], par[:, S2:S2 + 1], ALU.mult, ALU.mult)
            scalar(1, D1, par[:, Z1:Z1 + 1], -1.0, MID, ALU.mult, ALU.add)
            scalar(2, D2, par[:, Z2:Z2 + 1], -1.0, MID, ALU.mult, ALU.add)
            scalar(3, CC, col(D1), col(ALPHA), None, ALU.mult)
            scalar(4, CR, col(D2), col(ALPHA), None, ALU.mult)
            scalar(5, CK, col(CR), col(D1), float(D), ALU.mult, ALU.mult)
            nc.vector.tensor_scalar(col(TGW), tg[:, 2:3], 1.0 / WS, None, ALU.mult).then_inc(scal_ok, 1)
            for n in range(2 * RING):
                s, w = n % RING, (wk, wv)[n // RING]
                dve.wait_ge(w_hi, n + 1)
                minus(w[:, LO, 2 * s:2 * s + 2, :], stage[:, s, 0:2 * KVD].rearrange("p (c n) -> p c n", c=2),
                      w[:, HI, 2 * s:2 * s + 2, :]).then_inc(w_split, 1)
            dve.wait_ge(small_ld, 32)
            nc.vector.tensor_tensor(coef, coef, mask, ALU.mult).then_inc(wsum_step, 1)
            dve.wait_ge(wsum_step, 1)
            nc.vector.reduce_sum(w_sum[:, :, :].rearrange("p c r -> p (c r)"), coef, axis=AX).then_inc(wsum_ok, 1)
            dve.wait_ge(scal_ok, 1)

            with dve.Fori(0, B) as b:
                dve.wait_ge(x_ld, 16 * TPB * (b + 1))
                for k in range(TPB):
                    stats(TPB * b + k, LN1)

                def quant_ctx(n):
                    s = n % RING
                    dve.wait_ge(n_aff, NC * b + n + 1)
                    nc.vector.tensor_scalar(stage[:, s, :], stage[:, s, :], 0.0, QMAX, ALU.max, ALU.min
                                            ).then_inc(n_clip, 1)
                    dve.wait_ge(n_clip, NC * b + n + 1)
                    nc.vector.tensor_scalar(cols(q2, b * NC * D + n * D, D), stage[:, s, :], MAGIC, MAGIC + MID,
                                            ALU.add, ALU.subtract).then_inc(n_done, 1)

                def quant_x(k):
                    i = TPB * b + k
                    y, q = y_buf[:, k % 2, :], q1_buf[:, k % 2, :]
                    dve.wait_ge(t1_ok, i + 1)
                    nc.vector.tensor_scalar(y, y, 0.0, QMAX, ALU.max, ALU.min).then_inc(q1_clip, 1)
                    dve.wait_ge(q1_clip, i + 1)
                    dve.wait_ge(tq_ready, TPB * b + max(0, k - 1))
                    nc.vector.tensor_scalar(q, y, MAGIC, MAGIC + MID, ALU.add, ALU.subtract).then_inc(q1_ok, 1)
                    dve.wait_ge(q1_ok, i + 1)
                    nc.vector.reduce_sum(cols(row_q, i, 1), q, axis=AX).then_inc(rowq_ok, 1)
                    dve.wait_ge(rowq_ok, i + 1)
                    nc.vector.tensor_scalar(cols(beta, i, 1), cols(row_q, i, 1), col(CR), col(CK), ALU.mult, ALU.add
                                            ).then_inc(beta_ok, 1)

                t = 2 * b
                for n in range(4):
                    quant_ctx(n)
                quant_x(0)
                quant_x(1)
                keys(t)
                values(t, 0)
                quant_ctx(4)
                quant_ctx(5)
                values(t, 1)
                quant_ctx(6)
                quant_ctx(7)
                values(t, 2)
                values(t, 3)
                quant_x(2)
                quant_x(3)
                keys(t + 1)
                for tt in range(TPB):
                    values(t + 1, tt)

            dve.wait_ge(enc_hi, 1)
            minus(enc[0:R, LO, :], enc_f[0:R, :], enc[0:R, HI, :]).then_inc(enc_ok, 1)
            for half in range(2):
                hs = slice(half * 512, (half + 1) * 512)
                dve.wait_ge(u_hi, half + 1)
                minus(u_t[0:R, LO, hs], bank(1 + half, 512, R), u_t[0:R, HI, hs]).then_inc(u_lo, 1)
            for c in range(NC):
                s = c % RING
                dve.wait_ge(ld[s], 16 * (CY_WB + c // RING + 1))
                for half in range(2):
                    part = stage[:, s, half * 512:(half + 1) * 512]
                    dve.wait_ge(dl_ready, 2 * c + half + 1)
                    nc.vector.scalar_tensor_tensor(part, part, WS, bank((4, 6)[c % 2] + half), ALU.mult, ALU.add
                                                   ).then_inc(we_sum, 1)

            nc.vector.memset(v_out[:, :, :, HD:HD + 1], 1.0)

            with dve.Fori(0, B) as b:
                for k in range(TPB):
                    i = TPB * b + k
                    dve.wait_ge(xc_ok, i + 1)
                    for half in range(2):
                        xh = x_tile(i, half * 512, 512)
                        dve.wait_ge(xa_ready, 2 * i + half + 1)
                        nc.vector.scalar_tensor_tensor(xh, bank(2 * (k % 2) + half), col(ALPHA), xh, ALU.mult, ALU.add
                                                       ).then_inc(xa_ok, 1)
                    dve.wait_ge(xa_ok, 2 * i + 2)
                    stats(i, LN2)

            def take_low(i, n):
                dve.wait_ge(tl_hi, n + 1)
                minus(slab(i, LO), wide(6), slab(i, HI)).then_inc(tl_lo, 1)

            def add_ffn(i, half):
                if half == 0:
                    dve.wait_ge(xbias_ok, i + 1)
                xh = x_tile(i, half * 512, 512)
                dve.wait_ge(ff_ready, 2 * i + half + 1)
                nc.vector.scalar_tensor_tensor(xh, bank(4 + half), col(TGW), xh, ALU.mult, ALU.add
                                               ).then_inc(ff_ok, 1)
                if half == 1:
                    dve.wait_ge(ff_ok, 2 * i + 2)
                    stats(i, LN3)

            take_low(0, 0)
            take_low(1, 1)
            add_ffn(0, 0)
            add_ffn(0, 1)
            take_low(2, 2)
            add_ffn(1, 0)
            add_ffn(1, 1)

            def ffn_step(i, ahead):
                if ahead:
                    take_low(i + 1, 2 * i - 1)
                add_ffn(i, 0)
                take_low(i - 2, 2 * i if ahead else 2 * i - 1)
                add_ffn(i, 1)

            with dve.Fori(0, 2) as r:
                for k in range(2):
                    ffn_step(2 * r + 2 + k, True)
            ffn_step(6, True)
            ffn_step(7, False)
            with dve.Fori(0, B) as b:
                take_low(6 + b, 14 + b)
                keys(4 + b)
                for tt in range(TPB):
                    values(4 + b, tt)

            def split_wq(n, s):
                dve.wait_ge(w_hi, n + 1)
                minus(wq[:, LO, 2 * s:2 * s + 2, :], stage[:, s, 0:2 * QG].rearrange("p (c n) -> p c n", c=2),
                      wq[:, HI, 2 * s:2 * s + 2, :]).then_inc(w_split, 1)

            def split_wo(n, s):
                dve.wait_ge(w_hi, n + 1)
                cs = slice(s * 256, (s + 1) * 256)
                minus(wo[:, LO, :, cs], stage[:, s, 0:NJ * 256].rearrange("p (j n) -> p j n", j=NJ), wo[:, HI, :, cs]
                      ).then_inc(w_split, 1)

            def take_low_of(dst, n, k, j):
                dve.wait_ge(sp_hi, n + 1)
                minus(dst[:, j, LO, :], bank(spare(k)), dst[:, j, HI, :]).then_inc(sp_free, 1)

            def add_out(first, k, b, w):
                xh = x_tile(TPB * b + w // 2, (w % 2) * 512, 512)
                dve.wait_ge(sp_ready, first + 1)
                nc.vector.scalar_tensor_tensor(xh, bank(spare(k)), tg[:, 1:2], xh, ALU.mult, ALU.add
                                               ).then_inc(sp_free, 1)

            def reduce_max(v, s, k):
                dve.wait_ge(pre_ready, N_PRE * v + k + 1)
                nc.vector.reduce_max(pre_max[:, s % 2, k // 3, k % 3:k % 3 + 1], bank(pre_bank(s, k)), axis=AX
                                     ).then_inc(pre_ok, 1)

            def final_max(v, s):
                dve.wait_ge(pre_ok, N_PRE * (v + 1))
                nc.vector.reduce_max(row_max[:, :], pre_max[:, s % 2, :, :], axis=AX).then_inc(max_step, 1)
                dve.wait_ge(max_step, v + 1)
                nc.vector.tensor_scalar(neg_max[:, s % 2, :, HD:HD + 1], row_max[:, :].rearrange("p (t o) -> p t o", o=1),
                                        -1.0, None, ALU.mult).then_inc(nm_ok, 1)

            def divide(u, b, h):
                dve.wait_ge(oraw_ok, u + 1)
                nc.vector.reciprocal(den_inv[:, :].rearrange("p (t o) -> p t o", o=1), o_raw[:, :, HD:HD + 1])
                nc.vector.tensor_tensor(o_sum[:, :, :], o_raw[:, :, 0:HD], o_raw[:, :, HD + 1:VW], ALU.add
                                        ).then_inc(osum_ok, 1)
                dve.wait_ge(osum_ok, u + 1)
                den = den_inv[:, :].rearrange("p (t o) -> p t o", o=1).broadcast_to([P, TPB, HD])
                nc.vector.tensor_tensor(o_tok[:, b, :, h * HD:(h + 1) * HD], o_sum[:, :, :], den, ALU.mult
                                        ).then_inc(o_ok, 1)

            nc.vector.memset(neg_max[:, :, :, :], 0.0)
            nc.vector.memset(k_head[HD:HD + 1, :, HI, :], 1.0)
            for s in range(RING):
                split_wq(W_WQ0 + s, s)
            dve.wait_ge(w_hi, W_E + 1)
            minus(rw[:, :, NE:2 * NE], stage[:, 0, 0:NC * NE].rearrange("p (c n) -> p c n", c=NC), rw[:, :, 0:NE]
                  ).then_inc(w_split, 1)
            for s in range(1, RING):
                c0, c1 = EB_CUTS[s - 1:s + 1]
                dve.wait_ge(w_hi, W_E + s + 1)
                minus(eb_lo[:, c0:c1], stage[0:NE, s, 0:c1 - c0], eb_hi[0:NE, c0:c1]).then_inc(w_split, 1)
            for j in range(NJ):
                dve.wait_ge(sp_hi, j + 1)
                minus(q_blk[:, j, LO, :], bank(6 + j % 2), q_blk[:, j, HI, :]).then_inc(sp_free, 1)
            for k in range(N_PRE):
                reduce_max(0, 0, k)
            final_max(0, 0)

            def iteration(g, last):
                base, high = SP0 + SP_ITER * g, SP0 + 4 * NJ * g
                u0 = SLOTS * g
                for s in range(SLOTS):
                    k = 0
                    for i in range(NS):
                        if s < SLOTS - 1:
                            for _ in range(PRE_AT[i]):
                                reduce_max(u0 + s + 1, s + 1, k)
                                k += 1
                            if i == MAX_STEP:
                                final_max(u0 + s + 1, s + 1)
                        if s > 0 and i == LAG + 1:
                            divide(u0 + s - 1, (s - 1) // G, (s - 1) % G)
                        if (s, i) in Q1_TAKE:
                            j = Q1_TAKE[s, i]
                            take_low_of(q_blk, high + j, SPQ1 + j, j)
                        if s == G and i - 1 in T0_STEPS:
                            j = T0_STEPS[i - 1]
                            take_low_of(o_t, high + NJ + j, SPT0 + j, j)
                        if s in WO_STEPS and i - 1 in WO_STEPS[s]:
                            w = WO_STEPS[s][i - 1]
                            add_out(base + SPO0 + w, SPO0 + w, 0, w)
                        if s == WO_SPLIT and i in SPLIT_STEPS:
                            split_wo(W_G + 2 * RING * g + SPLIT_STEPS[i], SPLIT_STEPS[i])
                        if s == WQ_SPLIT and i in SPLIT_STEPS and not last:
                            split_wq(W_G + 2 * RING * g + RING + SPLIT_STEPS[i], SPLIT_STEPS[i])
                divide(u0 + SLOTS - 1, 1, G - 1)
                k, high = SPQ0, high + 2 * NJ
                if not last:
                    for j in range(NJ):
                        take_low_of(q_blk, high + j, k, j)
                        k += 1
                    high = high + NJ
                for j in range(NJ):
                    take_low_of(o_t, high + j, k, j)
                    k += 1
                m = 0
                for w in range(8):
                    add_out(base + k, k, 1, w)
                    k += 1
                    if not last and 2 <= w <= 5:
                        for _ in range(3):
                            reduce_max(u0 + SLOTS, 0, m)
                            m += 1
                    if not last and w == 5:
                        final_max(u0 + SLOTS, 0)

            with dve.Fori(0, KV - 1) as g:
                iteration(g, False)
            iteration(KV - 1, True)

            def expert_low(i, k):
                dve.wait_ge(t4_hi, i + 1)
                minus(slab(i, LO), wide(2 * k), slab(i, HI)).then_inc(t4_lo, 1)

            def logits(i, k):
                n = LG_STEPS * i
                dve.wait_ge(lg_ready, i + 1)
                nc.vector.tensor_tensor(logit[:, k, :], bank(4, NE), rb[:, :], ALU.add).then_inc(lg_step, 1)
                dve.wait_ge(lg_step, n + 1)
                nc.vector.tensor_tensor(logit[:, k, :], bank(4, 2 * NE)[:, NE:2 * NE], logit[:, k, :], ALU.add
                                        ).then_inc(lg_step, 1)
                dve.wait_ge(lg_step, n + 2)
                nc.vector.reduce_max(row_max[:, k:k + 1], logit[:, k, :], axis=AX).then_inc(lg_step, 1)
                dve.wait_ge(lg_step, n + 3)
                nc.vector.tensor_scalar(nmx[:, k:k + 1], row_max[:, k:k + 1], -1.0, None, ALU.mult).then_inc(lg_ok, 1)

            def choose(i, k):
                n = TOP_STEPS * i
                p = prob[:, k, :]
                dve.wait_ge(ex_ok, i + 1)
                nc.vector.reciprocal(einv[:, :], esum[:, k:k + 1]).then_inc(top_step, 1)
                dve.wait_ge(top_step, n + 1)
                nc.vector.tensor_scalar(p, p, einv[:, 0:1], None, ALU.mult).then_inc(top_step, 1)
                dve.wait_ge(top_step, n + 2)
                dve.sem_inc(top_go, 1)
                nc.vector.max(top8[:, :], p).then_inc(top_step, 1)
                dve.wait_ge(top_step, n + 3)
                nc.vector.reduce_sum(wsum8[:, :], top8[:, :], axis=AX)
                nc.vector.match_replace(rest[:, :], top8[:, :], p, 0.0).then_inc(top_step, 1)
                dve.wait_ge(top_step, n + 4)
                nc.vector.tensor_scalar(ascale[:, k:k + 1], wsum8[:, :], tg[:, 3:4], None, ALU.mult)
                minus(p, p, rest[:, :]).then_inc(top_step, 1)
                dve.wait_ge(top_step, n + 5)
                dve.wait_ge(wx_ready, i)
                nc.vector.tensor_copy(w_tok[:, 0:NE], p).then_inc(top_step, 1)
                dve.wait_ge(top_step, n + 6)
                minus(w_tok[:, NE:2 * NE], p, w_tok[:, 0:NE]).then_inc(wt_ok, 1)

            def add_mix(i):
                dve.wait_ge(xy_ok, i + 1)
                for half in range(2):
                    xh = x_tile(i, half * 512, 512)
                    dve.wait_ge(mix_ready, 2 * i + half + 1)
                    nc.vector.scalar_tensor_tensor(xh, bank(6 + half), tg[:, 3:4], xh, ALU.mult, ALU.add
                                                   ).then_inc(fin_ok, 1)

            def expert_step(i, k, ahead):
                choose(i, k)
                if ahead > 0:
                    expert_low(i + 1, 1 - k)
                    logits(i + 1, 1 - k)
                add_mix(i)
                if ahead > 1:
                    stats(i + 2, LN4)

            dve.wait_ge(sp_free, SP0 + SP_ITER * KV - NJ)
            stats(0, LN4)
            stats(1, LN4)
            dve.wait_ge(rb_ld, 16)
            expert_low(0, 0)
            logits(0, 0)
            with dve.Fori(0, NT // 2 - 1) as r:
                for k in range(2):
                    expert_step(2 * r + k, k, 2)
            expert_step(NT - 2, 0, 1)
            expert_step(NT - 1, 1, 0)

        @block.gpsimd
        def _(pool):
            def tt(out, a, b, op):
                return nc.gpsimd.tensor_tensor(out, a, b, op)

            def deviations(i, ln):
                n = ln + i
                pool.wait_ge(ln_var, n + 1)
                tt(cols(rstd, n, 1), cols(var_c, n, 1), mhalf[:, :], ALU.pow).then_inc(ln_pow, 1)
                pool.wait_ge(ln_pow, n + 1)
                tt(cols(nmr, n, 1), cols(nmean, n, 1), cols(rstd, n, 1), ALU.mult).then_inc(ln_ok, 1)

            def split_ctx(t, half):
                for s in range(RING):
                    pool.wait_ge(c_hi, RING * t + s + 1)
                    tt(ctx_t[:, half, 2 * s:2 * s + 2, LO, :], stage[:, s, :].rearrange("p (c n) -> p c n", c=2),
                       ctx_t[:, half, 2 * s:2 * s + 2, HI, :], ALU.subtract).then_inc(c_split, 1)

            def add_columns(b):
                pool.wait_ge(cs_ok, 2 * b + 2)
                for k in range(TPB):
                    i = TPB * b + k
                    pool.wait_ge(xb_ok, i + 1)
                    tt(x_tile(i), x_tile(i), bc_buf[:, b, :], ALU.add).then_inc(xc_ok, 1)

            nc.gpsimd.memset(mhalf[:, :], -0.5)
            pool.sem_inc(plo_ok, NPF)
            for b in range(B):
                split_ctx(2 * b, 0)
                for k in range(TPB):
                    deviations(TPB * b + k, LN1)
                split_ctx(2 * b + 1, 1)
                if b > 0:
                    add_columns(b - 1)
            add_columns(B - 1)
            for c in range(NC):
                pool.wait_ge(we_hi, c + 1)
                tt(w_eff[:, LO, c, :], stage[:, c % RING, :], w_eff[:, HI, c, :], ALU.subtract).then_inc(we_ok, 1)
            with pool.Fori(0, NT) as i:
                deviations(i, LN2)
            pool.wait_ge(bias_ok, 1)
            with pool.Fori(0, NT) as i:
                pool.wait_ge(y2_ok, i + 1)
                tt(x_tile(i), x_tile(i), bias_rows, ALU.add).then_inc(xbias_ok, 1)
                deviations(i, LN3)
            with pool.Fori(0, SLOTS * KV) as u:
                for i in range(NS):
                    n = NS * u + i
                    pool.wait_ge(exp_ok, 2 + n + 1)
                    tt(p_lo[:, i % NPB, :], p_f32[:, i % NPF, :], p_hi[:, i % NPB, :], ALU.subtract).then_inc(plo_ok, 1)

            def add_scaled(i, k):
                pool.wait_ge(ya_ok, i + 1)
                tt(x_tile(i), x_tile(i), y_buf[:, k, :], ALU.add).then_inc(xy_ok, 1)

            deviations(0, LN4)
            deviations(1, LN4)
            with pool.Fori(0, NT // 2 - 1) as r:
                for k in range(2):
                    add_scaled(2 * r + k, k)
                    deviations(2 * r + k + 2, LN4)
            add_scaled(NT - 2, 0)
            add_scaled(NT - 1, 1)


def kernel(x, ctx_4096, g_xattn, g_ffn, L0_xattn_x1_scale, L0_xattn_x1_zp, L0_xattn_x2_scale, L0_xattn_x2_zp,
           L0_ffn_W_base, L0_ffn_b_base, L0_ffn_enc0, L0_ffn_enc1, L0_ffn_coefs0, L0_ffn_coefs1, L0_ffn_mask0,
           L0_ffn_mask1, L1_xattn_Wq, L1_xattn_Wk, L1_xattn_Wv, L1_xattn_Wo, L1_ffn_router_weight,
           L1_ffn_router_bias, L1_ffn_expert_bias):
    import concourse.bacc as bacc
    import numpy as np
    from concourse.bass_utils import run_bass_kernel_spmd

    c = np.ascontiguousarray

    def by_chunk(w):
        return c(w.reshape(NC, P, -1).transpose(1, 0, 2))

    def rows(v):
        return c(np.broadcast_to(v.reshape(1, -1), (P, v.size)))

    o = np.arange(D)
    table = np.zeros((D, D))
    table[0] = 1 / np.sqrt(D)
    for k in range(1, D // 2):
        table[2 * k - 1] = np.sqrt(2 / D) * np.cos(2 * np.pi * (k * o % D) / D)
        table[2 * k] = np.sqrt(2 / D) * np.sin(2 * np.pi * (k * o % D) / D)
    table[D - 1] = (1 - 2 * (o % 2)) / np.sqrt(D)
    table = (table * (WS / 2)).astype(np.float32)

    coef = np.concatenate([L0_ffn_coefs0, L0_ffn_coefs1], 2).transpose(1, 2, 0)
    mask = np.concatenate([L0_ffn_mask0, L0_ffn_mask1], 2).transpose(1, 2, 0)
    eb = np.concatenate([L1_ffn_expert_bias, L1_ffn_expert_bias], 0)
    wq = L1_xattn_Wq.T.reshape(NC, P, KV, QG).transpose(2, 1, 0, 3).reshape(KV * P, NC, QG)
    wo = L1_xattn_Wo.T.reshape(KV, NJ, P, D).transpose(0, 2, 1, 3).reshape(KV * P, NJ, D)
    host = {
        "x": c(x.reshape(B * QL, D)),
        "ctx": c(ctx_4096),
        "ctx_t": c(ctx_4096.transpose(0, 2, 1)),
        "par": rows(np.concatenate([g_xattn, g_ffn, L0_xattn_x1_scale, L0_xattn_x1_zp, L0_xattn_x2_scale,
                                    L0_xattn_x2_zp])),
        "ident": np.eye(P, dtype=np.float32),
        "wk": by_chunk(L1_xattn_Wk.T),
        "wv": by_chunk(L1_xattn_Wv.T),
        "wq": c(wq),
        "wo": c(wo),
        "wb": c(L0_ffn_W_base.T),
        "bb": rows(L0_ffn_b_base),
        "ft": by_chunk(table),
        "coef": by_chunk(coef.reshape(D, R * E)).reshape(P, NC * R, E),
        "mask": by_chunk(mask.reshape(D, R * E)).view(np.int32),
        "enc": c(np.concatenate([L0_ffn_enc0, L0_ffn_enc1], 0)),
        "rw": by_chunk(L1_ffn_router_weight.T),
        "rb": rows(L1_ffn_router_bias),
        "eb": c(eb),
    }
    nc = bacc.Bacc("TRN2", target_bir_lowering=False, num_devices=1)
    aps = [nc.dram_tensor(f"{name}_in", a.shape, I32 if name == "mask" else F32, kind="ExternalInput").ap()
           for name, a in host.items()]
    out = nc.dram_tensor("out", (B * QL, D), F32, kind="ExternalOutput").ap()
    flamingo(nc, *aps, out)
    result = run_bass_kernel_spmd(nc, [{f"{name}_in": a for name, a in host.items()}], core_ids=[0])
    return result.results[0]["out"].reshape(B, QL, D)
```

```python
from contextlib import ExitStack

import concourse.bass as bass
from concourse import mybir
from concourse.alu_op_type import AluOpType as ALU

ACT = mybir.ActivationFunctionType
F32 = mybir.dt.float32
F16 = mybir.dt.float16
U8 = mybir.dt.uint8
I32 = mybir.dt.int32
AX = mybir.AxisListType.X

P = 128
D = 1024
NC = D // P
B, QL, CTX = 2, 512, 1024
NT = B * QL // P
TPB = QL // P
SL = CTX + QL
NS = SL // P
KV, G, HD = 4, 4, 96
KVD = KV * HD
QG = G * HD
NJ = QG // P
VW = 2 * HD + 1
E, R = 3, 40
NE, TOP = 64, 8
EPS = 1e-5
MAGIC = 1.5 * 2.0 ** 23
MID = 128.0
QMAX = 255.0
WS = 64.0
SCALE = 1.0 / float(HD) ** 0.5
RING = 4
LAG = 3
NPF, NPB = 4, 6
HSLAB = 2 * NC * P
HI, LO = 0, 1


def flamingo(nc, x_d, ctx_d, ctx_t_d, par_d, ident_d, wk_d, wv_d, wq_d, wo_d, wb_d, bb_d, ft_d,
             coef_d, mask_d, enc_d, rw_d, rb_d, eb_d, out_d):
    with ExitStack() as ctx:
        def sb(name, shape, dt):
            return ctx.enter_context(nc.sbuf_tensor(name, shape, dt))

        def sem(name):
            return ctx.enter_context(nc.semaphore(name))

        x_res = sb("x_res", [P, NT * D], F32)
        ln_t = sb("ln_t", [P, NT * HSLAB], F16)
        stage = sb("stage", [P, RING, D], F32)
        region_w = sb("region_w", [P, 4 * NC * KVD], F16)
        region_o = sb("region_o", [P, 6176], F16)
        region_c = sb("region_c", [P, 16384], F16)
        region_q = sb("region_q", [P, 16384], F16)
        region_y = sb("region_y", [P, 2 * D], F32)
        region_s = sb("region_s", [P, 2 * D], F16)
        region_b = sb("region_b", [P, 2 * D], F32)

        def view(region, start, n, dt=F16):
            per = 2 if (dt == F32 and region.dtype == F16) else 1
            v = region[:, start:start + n * per]
            return v.bitcast(F32) if per == 2 else v

        wk = view(region_w, 0, 2 * NC * KVD).rearrange("p (h c n) -> p h c n", h=2, c=NC)
        wv = view(region_w, 2 * NC * KVD, 2 * NC * KVD).rearrange("p (h c n) -> p h c n", h=2, c=NC)
        wq = wk
        wo = view(region_w, 2 * NC * KVD, 2 * NJ * D).rearrange("p (h j n) -> p h j n", h=2, j=NJ)
        k_out = view(region_o, 0, NJ * 2 * QL).rearrange("p (j h s) -> p j h s", j=NJ, h=2)
        v_out = view(region_o, NJ * 2 * QL, KV * 4 * VW).rearrange("p (k t w) -> p k t w", k=KV, t=4)
        enc_f = view(region_o, 0, D, F32)
        enc = view(region_o, 2 * D, 2 * D).rearrange("p (h d) -> p h d", h=2)
        u_t = view(region_o, 4 * D, 2 * D).rearrange("p (h o) -> p h o", h=2)
        ctx_t = view(region_c, 0, 16384).rearrange("p (b c h s) -> p b c h s", b=2, c=NC, h=2)
        w_eff = view(region_c, 0, 16384).rearrange("p (h c n) -> p h c n", h=2, c=NC)
        q_head = view(region_c, 0, 8192).rearrange("p (b g h s) -> p b g h s", b=2, g=G, h=2)
        p_hi = view(region_c, 8192, NPB * QL).rearrange("p (r q) -> p r q", r=NPB)
        p_lo = view(region_c, 8192 + NPB * QL, NPB * QL).rearrange("p (r q) -> p r q", r=NPB)
        neg_max = view(region_c, 8192 + 2 * NPB * QL, 2 * TPB * 98).rearrange("p (b t n) -> p b t n", b=2, t=TPB)
        q2 = region_q[:, :]
        k_head = view(region_q, 0, 4 * SL).rearrange("p (b h s) -> p b h s", b=2, h=2)
        v_head = view(region_q, 4 * SL, 2 * NS * VW).rearrange("p (b s w) -> p b s w", b=2, s=NS)
        q_blk = view(region_q, 10776, NJ * 2 * QL).rearrange("p (j h s) -> p j h s", j=NJ, h=2)
        o_sum = view(region_q, 13848, TPB * HD, F32).rearrange("p (t d) -> p t d", t=TPB)
        o_raw = view(region_q, 14616, TPB * VW, F32).rearrange("p (t w) -> p t w", t=TPB)
        o_tok = view(region_o, 0, 2 * TPB * QG, F32).rearrange("p (b t n) -> p b t n", b=2, t=TPB)
        y_buf = region_y[:, :].rearrange("p (b d) -> p b d", b=2)
        p_f32 = region_y[:, :].rearrange("p (r q) -> p r q", r=NPF)
        q1_buf = region_s[:, :].rearrange("p (b d) -> p b d", b=2)
        bc_buf = region_b[:, :].rearrange("p (b d) -> p b d", b=2)
        w_land = view(region_q, 0, 2 * NC * KVD, F32).rearrange("p (w c n) -> p w c n", w=2, c=NC)
        coef = view(region_q, 4 * NC * KVD, NC * R * E, F32).rearrange("p (n e) -> p n e", e=E)
        mask_words = region_q[:, 15000:15000 + NC * R * E // 2].bitcast(I32)
        mask = region_q[:, 15000:15000 + NC * R * E // 2].bitcast(U8).rearrange("p (n e) -> p n e", e=E)
        y3_buf = region_b[:, 0:D]
        bias_rows = region_b[:, D:2 * D]
        o_t = region_b[:, 0:NJ * QL].bitcast(F16).rearrange("p (j h s) -> p j h s", j=NJ, h=2)

        y_all = view(region_c, 0, NT * D, F32).rearrange("p (t d) -> p t d", t=NT)
        rw = region_s[:, 0:NC * 2 * NE].rearrange("p (c n) -> p c n", c=NC)
        eb_hi = region_s[:, D:2 * D]
        eb_lo = region_b[0:NE, 3 * D // 2:2 * D].bitcast(F16)

        ident = sb("ident", [P, P], F32)
        ident_h = sb("ident_h", [P, P], F16)
        ones_h = sb("ones_h", [P, P], F16)
        par = sb("par", [P, 8], F32)
        tg = sb("tg", [P, 4], F32)
        sc = sb("sc", [P, 16], F32)
        w_sum = sb("w_sum", [P, NC, R], F32)
        bn = sb("bn", [P, 2, 6], F32)
        mv = sb("mv", [P, 2], F32)
        var_c = sb("var_c", [P, 4 * NT], F32)
        nmean = sb("nmean", [P, 4 * NT], F32)
        rstd = sb("rstd", [P, 4 * NT], F32)
        nmr = sb("nmr", [P, 4 * NT], F32)
        mhalf = sb("mhalf", [P, 1], F32)
        row_q = sb("row_q", [P, NT], F32)
        beta = sb("beta", [P, NT], F32)
        pre_max = sb("pre_max", [P, 2, TPB, SL // 512], F32)
        row_max = sb("row_max", [P, TPB], F32)
        den_inv = sb("den_inv", [P, TPB], F32)
        rb = sb("rb", [P, NE], F32)
        logit = sb("logit", [P, NT, NE], F32)
        rest = sb("rest", [P, NE], F32)
        top8 = sb("top8", [P, TOP], F32)
        lmax = sb("lmax", [P, 1], F32)
        nmx = sb("nmx", [P, NT], F32)
        esum = sb("esum", [P, NT], F32)
        einv = sb("einv", [P, 1], F32)
        wsum8 = sb("wsum8", [P, 1], F32)
        mscale = sb("mscale", [P, NT], F32)
        ascale = sb("ascale", [P, NT], F32)
        w_tok = sb("w_tok", [P, 2, 2 * NE], F16)
        w_exp = sb("w_exp", [P, 2, P], F16)
        ps = ctx.enter_context(nc.psum_tensor("ps", [P, 8, 512], F32))

        S1, Z1, S2, Z2 = 4, 5, 6, 7
        RS1, RS2, ALPHA, CC, CR, CK, TGW, D1, D2, TMP = range(10)

        k_dram = nc.dram_tensor("k_scratch", (B, 2, KVD, SL), F16).ap()
        v_dram = nc.dram_tensor("v_scratch", (B, KV, P, NS, VW), F16).ap()

        par_ld, x_ld, id_ld, small_ld, enc_ld, bb_ld, rb_ld = (
            sem(n) for n in ("par_ld", "x_ld", "id_ld", "small_ld", "enc_ld", "bb_ld", "rb_ld"))
        ld = [sem(f"ld{s}") for s in range(RING)]
        w_ld = [[sem(f"{w}_ld{s}") for s in range(RING)] for w in ("wk", "wv")]
        const_ok, half_ok, tanh_ok, scal_step, scal_ok = (sem(n) for n in ("const_ok", "half_ok", "tanh_ok", "scal_step", "scal_ok"))
        wsum_step, wsum_ok = sem("wsum_step"), sem("wsum_ok")
        w_hi, w_split = sem("w_hi"), sem("w_split")
        c_hi, c_split = sem("c_hi"), sem("c_split")
        n_aff, n_clip, n_done = sem("n_aff"), sem("n_clip"), sem("n_done")
        k_ready, k_hi_ok, k_lo_ok = sem("k_ready"), sem("k_hi_ok"), sem("k_lo_ok")
        v_ready, v_hi_ok, v_lo_ok = sem("v_ready"), sem("v_hi_ok"), sem("v_lo_ok")
        kv_stored = sem("kv_stored")
        bn_step, bn_go, ln_var, ln_pow, ln_ok = sem("bn_step"), sem("bn_go"), sem("ln_var"), sem("ln_pow"), sem("ln_ok")
        y1_ok, t1_ok, q1_clip, q1_ok, rowq_ok, beta_ok = (
            sem(n) for n in ("y1_ok", "t1_ok", "q1_clip", "q1_ok", "rowq_ok", "beta_ok"))
        xb_ok, xc_ok = sem("xb_ok"), sem("xc_ok")
        tq_ready, tq_ok, cs_ready, cs_ok = (sem(n) for n in ("tq_ready", "tq_ok", "cs_ready", "cs_ok"))
        f_used, u_hi, u_lo, enc_hi, enc_ok = (sem(n) for n in ("f_used", "u_hi", "u_lo", "enc_hi", "enc_ok"))
        dl_ready, we_sum, we_hi, we_ok = (sem(n) for n in ("dl_ready", "we_sum", "we_hi", "we_ok"))
        bias_ok, xbias_ok = sem("bias_ok"), sem("xbias_ok")
        xa_ready, xa_ok = sem("xa_ready"), sem("xa_ok")
        y2_ok, y3_ok = sem("y2_ok"), sem("y3_ok")
        tl_ready, tl_hi, tl_lo = sem("tl_ready"), sem("tl_hi"), sem("tl_lo")
        ff_ready, ff_ok = sem("ff_ready"), sem("ff_ok")
        k_ld = [sem(f"k_ld{b}") for b in range(B)]
        v_ld = [sem(f"v_ld{b}") for b in range(B)]
        q_ld = [sem(f"q_ld{b}") for b in range(B)]
        sp_ready, sp_hi, sp_free = sem("sp_ready"), sem("sp_hi"), sem("sp_free")
        pre_ready, pre_ok, max_step, nm_ok = sem("pre_ready"), sem("pre_ok"), sem("max_step"), sem("nm_ok")
        row_ready, row_ok = sem("row_ready"), sem("row_ok")
        sc_ready, exp_ok, plo_ok, pv_ok = (sem(n) for n in ("sc_ready", "exp_ok", "plo_ok", "pv_ok"))
        oraw_ok, oraw2_ok, osum_ok, o_ok = sem("oraw_ok"), sem("oraw2_ok"), sem("osum_ok"), sem("o_ok")
        y4_ok, t4_ready, t4_hi, t4_lo = (sem(n) for n in ("y4_ok", "t4_ready", "t4_hi", "t4_lo"))
        lg_ready, lg_step, lg_ok, ex_ok = (sem(n) for n in ("lg_ready", "lg_step", "lg_ok", "ex_ok"))
        top_step, top_go, wt_ok, wx_ready, wx_ok, ya_ok, xy_ok, mix_ready, fin_ok = (
            sem(n) for n in ("top_step", "top_go", "wt_ok", "wx_ready", "wx_ok", "ya_ok", "xy_ok", "mix_ready", "fin_ok"))
        out_st = sem("out_st")

        def cols(t, start, n):
            return t[:, bass.ds(start, n)]

        def x_tile(i, start=0, n=D):
            return cols(x_res, i * D + start, n)

        def slab(i, h):
            return cols(ln_t, i * HSLAB + h * NC * P, NC * P)

        def batch_slabs(b):
            return cols(ln_t, b * TPB * HSLAB, TPB * HSLAB).rearrange(
                "p (t h c k) -> p t h c k", t=TPB, h=2, c=NC)

        def bank(i, n=512, m=P):
            return ps[0:m, i, 0:n]

        def wide(i, dt=F32):
            if dt == F16:
                return ps[:, i, :].bitcast(F16)
            return ps[:, i:i + 2, :].rearrange("p b n -> p (b n)")

        def split_passes(a, b):
            return ((a(HI), b(HI)), (a(HI), b(LO)), (a(LO), b(HI)))

        CY_B, CY_F, CY_WB, CY_WQ0, CY_E, CY_G = 0, 8, 10, 12, 13, 14
        W_WQ0, W_E, W_G = 2 * RING, 3 * RING, 4 * RING
        EB_CUTS = (0, 384, 704, D)
        LG_STEPS, TOP_STEPS = 2, 4
        LN1, LN2, LN3, LN4 = 0, NT, 2 * NT, 3 * NT

        SLOTS = B * G
        PRE_AT = (2, 2, 1, 2, 1, 2, 1, 1, 0, 0, 0, 0)
        N_PRE = TPB * (SL // 512)
        MAX_STEP, ROW_STEP = 8, 9
        SP_ITER = 2 * NJ + 2 * (NJ + 8)
        SP0 = NJ
        SPQ1, SPT0, SPO0, SPX = 0, NJ, 2 * NJ, 2 * NJ + 8
        END = (("q", 0), ("o", 0), ("q", 1), ("o", 1), ("o", 2), ("q", 2))
        END_LAST = (("o", 0), ("o", 1), ("o", 2))
        Q0_USES = tuple(SPX + END.index(("q", j)) for j in range(NJ))
        Q1_TAKE = {(0, 8): 0, (1, 4): 1, (2, 0): 2}
        T0_STEPS = {7: 0, 8: 1, 9: 2}
        WO_STEPS = {5: {1: 0, 5: 1, 9: 2}, 6: {1: 3, 5: 4, 9: 5}, 7: {1: 6, 5: 7}}
        WO_SPLIT, WQ_SPLIT = 2, 5
        SPLIT_STEPS = {1: 0, 4: 1, 7: 2, 10: 3}

        def spare(k):
            return 6 + (SP0 + k) % 2

        def pre_bank(v, k):
            return 2 + (v + k) % 2

        block = ctx.enter_context(nc.Block())

        @block.sync
        def _(sp):
            def ring(s, dst, src, used=None, count=0):
                if used is not None:
                    sp.wait_ge(used, count)
                sp.dma_start(dst, src).then_inc(ld[s], 16)

            def pair(s, n):
                return stage[:, s, 0:2 * n].rearrange("p (c n) -> p c n", c=2)

            def load_ctx_t(t, used=None, count=0):
                b, half = t // 2, t % 2
                src = ctx_t_d[b].rearrange("(c p) s -> p c s", p=P)
                for s in range(RING):
                    ring(s, pair(s, QL), src[:, 2 * s:2 * s + 2, half * QL:(half + 1) * QL], used, count + s)

            def load_ctx(b, part):
                for n in range(part * RING, (part + 1) * RING):
                    used, count = (n_done, NC * b + n - RING + 1) if part else (c_split, RING * (2 * b + 1) + n + 1)
                    ring(n % RING, stage[:, n % RING, :], ctx_d[b, n * P:(n + 1) * P, :], used, count)

            def load_x(b):
                for k in range(TPB):
                    i = TPB * b + k
                    sp.dma_start(x_tile(i), x_d[i * P:(i + 1) * P, :]).then_inc(x_ld, 16)

            def store_kv(t, b, s0):
                sp.wait_ge(k_lo_ok, NJ * (t + 1))
                for h in (HI, LO):
                    dst = k_dram[b, h].rearrange("(j p) s -> p j s", p=P)[:, :, s0:s0 + QL]
                    sp.dma_start(dst, k_out[:, :, h, :]).then_inc(kv_stored, 16)
                sp.wait_ge(v_lo_ok, 4 * (t + 1))
                dst = v_dram[b].rearrange("k p s w -> p k s w")[:, :, s0 // P:s0 // P + 4, :]
                sp.dma_start(dst, v_out[:, :, :, :]).then_inc(kv_stored, 16)

            sp.dma_start(par[:, :], par_d).then_inc(par_ld, 16)
            def load_w(w, w_d):
                for s in range(RING):
                    cs = slice(2 * s, 2 * s + 2)
                    sp.dma_start(w_land[:, w, cs, :], w_d[:, cs, :]).then_inc(w_ld[w][s], 16)

            load_w(0, wk_d)
            load_ctx_t(0)
            load_w(1, wv_d)
            sp.dma_start(ident[:, :], ident_d).then_inc(id_ld, 16)
            load_x(0)
            load_ctx_t(1, c_split, 1)
            sp.dma_start(coef, coef_d).then_inc(small_ld, 16)
            sp.dma_start(mask_words, mask_d).then_inc(small_ld, 16)
            sp.dma_start(rb[:, :], rb_d).then_inc(rb_ld, 16)
            sp.wait_ge(x_ld, 16 * TPB)
            load_x(1)
            load_ctx(0, 0)
            store_kv(0, 0, 0)
            load_ctx(0, 1)
            load_ctx_t(2, n_done, RING + 1)
            store_kv(1, 0, QL)
            load_ctx_t(3, c_split, 2 * RING + 1)
            load_ctx(1, 0)
            store_kv(2, 1, 0)
            load_ctx(1, 1)
            for n in range(NC):
                if n == RING:
                    store_kv(3, 1, QL)
                    sp.wait_ge(kv_stored, 4 * 48)
                    sp.dma_start(enc_f[0:R, :], enc_d).then_inc(enc_ld, 16)
                used, count = (n_done, NC + RING + n + 1) if n < RING else (f_used, n - RING + 1)
                ring(n % RING, stage[:, n % RING, :], ft_d[:, n, :], used, count)
            for n in range(NC):
                used, count = (f_used, RING + n + 1) if n < RING else (we_ok, n - RING + 1)
                ring(n % RING, stage[:, n % RING, :], wb_d[n * P:(n + 1) * P, :], used, count)
            sp.wait_ge(xc_ok, NT)
            sp.dma_start(bias_rows, bb_d).then_inc(bb_ld, 16)

            def load_wq(g, used, count):
                for s in range(RING):
                    ring(s, pair(s, QG), wq_d[bass.ds(g * P, P), 2 * s:2 * s + 2, :], used, count + s)

            def load_wo(g, used, count):
                for s in range(RING):
                    dst = stage[:, s, 0:NJ * 256].rearrange("p (j n) -> p j n", j=NJ)
                    ring(s, dst, wo_d[bass.ds(g * P, P), :, s * 256:(s + 1) * 256], used, count + s)

            def load_kv(g, b):
                src = k_dram[b, :, bass.ds(g * HD, HD), :].rearrange("h d s -> d h s")
                sp.dma_start(k_head[0:HD, b, :, :], src).then_inc(k_ld[b], 16)
                src = v_dram[b, bass.ds(g, 1), :, :, :].rearrange("k p s w -> (k p) (s w)")
                sp.dma_start(v_head[:, b, :, :].rearrange("p s w -> p (s w)"), src).then_inc(v_ld[b], 16)

            def load_q(uses, b):
                for j in range(NJ):
                    sp.wait_ge(sp_free, uses[j] + 1)
                    row = j * P
                    while row < (j + 1) * P:
                        h, d = row // HD, row % HD
                        n = min(HD - d, (j + 1) * P - row)
                        sp.dma_start(q_head[d:d + n, b, h, :, :], q_blk[row - j * P:row - j * P + n, j, :, :]
                                     ).then_inc(q_ld[b], 16)
                        row += n

            load_wq(0, we_ok, RING + 1)
            store_kv(4, 0, CTX)
            sp.wait_ge(kv_stored, 5 * 48)
            sp.wait_ge(xa_ok, 2 * NT)
            load_kv(0, 0)
            ring(0, stage[:, 0, 0:NC * NE], rw_d, w_split, W_WQ0 + 1)
            for s in range(1, RING):
                c0, c1 = EB_CUTS[s - 1:s + 1]
                ring(s, stage[:, s, 0:c1 - c0], eb_d[:, c0:c1], w_split, W_WQ0 + s + 1)
            load_q(range(NJ), 0)
            store_kv(5, 1, CTX)
            sp.wait_ge(kv_stored, 6 * 48)

            def iteration(g, last):
                sp.wait_ge(pv_ok, NPB + SLOTS * NS * g)
                load_kv(g, 1)
                load_wo(g, w_split, W_G + 2 * RING * g - RING + 1)
                load_q([SP0 + SP_ITER * g + SPQ1 + j for j in range(NJ)], 1)
                if not last:
                    load_wq(g + 1, w_split, W_G + 2 * RING * g + 1)
                    sp.wait_ge(pv_ok, NPB + SLOTS * NS * g + G * NS)
                    load_kv(g + 1, 0)
                    load_q([SP0 + SP_ITER * g + k for k in Q0_USES], 0)

            with sp.Fori(0, KV - 1) as g:
                iteration(g, False)
            iteration(KV - 1, True)

            with sp.Fori(0, NT) as i:
                sp.wait_ge(fin_ok, 2 * i + 2)
                sp.dma_start(out_d[bass.ds(i * P, P), :], x_tile(i)).then_inc(out_st, 16)
            sp.wait_ge(out_st, 16 * NT)

        @block.tensor
        def _(pe):
            def passes(out, pairs, first, last):
                for n, (a, b) in enumerate(pairs):
                    ins = nc.tensor.matmul(out, a, b, start=first and n == 0, stop=last and n == len(pairs) - 1)
                return ins

            def by_tile(out):
                return out.rearrange("p (t k) -> p t k", t=TPB)

            def project_k(t, chunk_wait, x_of, shape=lambda out: out):
                pe.wait_ge(k_lo_ok, NJ * t)
                for c in range(NC):
                    chunk_wait(c)
                    for j in range(NJ):
                        ins = passes(shape(bank(j)), split_passes(lambda h: wk[:, h, c, j * P:(j + 1) * P],
                                                                  lambda h: x_of(c, h)), c == 0, c == NC - 1)
                        if c == NC - 1:
                            ins.then_inc(k_ready, 1)

            def project_v(t, tt, tile_of, between=lambda c: None):
                pe.wait_ge(v_lo_ok, 4 * t + max(0, tt - 1))
                for c in range(NC):
                    ins = passes(bank(3 + tt % 2, KVD), split_passes(lambda h: tile_of(c, h), lambda h: wv[:, h, c, :]),
                                 c == 0, c == NC - 1)
                    if c == NC - 1:
                        ins.then_inc(v_ready, 1)
                    between(c)

            def transpose_q1(i, k):
                pe.wait_ge(const_ok, 2)
                pe.wait_ge(q1_ok, i + 1)
                for c in range(NC):
                    ins = nc.tensor.transpose(wide((5, 0)[k % 2], F16)[:, c * P:(c + 1) * P],
                                              q1_buf[:, k % 2, c * P:(c + 1) * P], ident_h[:, :])
                ins.then_inc(tq_ready, 1)

            pe.sem_inc(pv_ok, NPB)
            pe.wait_ge(w_split, RING)
            with pe.Fori(0, B) as b:
                for half in range(2):
                    t = 2 * b + half

                    def chunk(c):
                        if c == 0:
                            pe.wait_ge(tq_ok, TPB * b + 2 * half)
                        if c % 2 == 0:
                            pe.wait_ge(c_split, RING * t + c // 2 + 1)

                    project_k(t, chunk, lambda c, h: ctx_t[:, half, c, h, :])
                    pe.wait_ge(w_split, 2 * RING)
                    for tt in range(TPB):
                        project_v(t, tt, lambda c, h: ctx_t[:, half, c, h, tt * P:(tt + 1) * P])
                    for k in (2 * half, 2 * half + 1):
                        if k % 2 == 1:
                            pe.wait_ge(k_lo_ok, NJ * (t + 1))
                        pe.wait_ge(tq_ok, TPB * b + 2 * half)
                        transpose_q1(TPB * b + k, k)
                pe.wait_ge(n_done, NC * (b + 1))
                pe.wait_ge(cs_ok, 2 * b)
                for half in range(2):
                    for c in range(NC):
                        ins = nc.tensor.matmul(bank(6 + half), ones_h[:, :],
                                               cols(q2, b * NC * D + c * D + half * 512, 512),
                                               start=c == 0, stop=c == NC - 1)
                    ins.then_inc(cs_ready, 1)

            pe.wait_ge(wsum_ok, 1)
            pe.wait_ge(k_lo_ok, 4 * NJ)
            for c in range(NC):
                pe.wait_ge(ld[c % RING], 16 * (CY_F + c // RING + 1))
                for half in range(2):
                    ins = nc.tensor.matmul(bank(1 + half, 512, R), w_sum[:, c, :],
                                           stage[:, c % RING, half * 512:(half + 1) * 512],
                                           start=c == 0, stop=c == NC - 1)
                ins.then_inc(f_used, 1)
            pe.wait_ge(enc_ok, 1)
            pe.wait_ge(u_lo, 2)
            pe.wait_ge(cs_ok, 2 * B)
            pe.wait_ge(v_lo_ok, 4 * 4)
            pe.wait_ge(tq_ok, NT)
            for c in range(NC):
                if c >= 2:
                    pe.wait_ge(we_sum, 2 * (c - 1))
                for half in range(2):
                    ins = passes(bank((4, 6)[c % 2] + half),
                                 split_passes(lambda h: enc[0:R, h, c * P:(c + 1) * P],
                                              lambda h: u_t[0:R, h, half * 512:(half + 1) * 512]), True, True)
                    ins.then_inc(dl_ready, 1)

            with pe.Fori(0, B) as b:
                for k in range(TPB):
                    i = TPB * b + k
                    pe.wait_ge(xa_ok, 2 * (TPB * b + max(0, k - 1)))
                    for half in range(2):
                        for c in range(NC):
                            ins = nc.tensor.matmul(bank(2 * (k % 2) + half), cols(ln_t, i * HSLAB + c * P, P),
                                                   cols(q2, b * NC * D + c * D + half * 512, 512),
                                                   start=c == 0, stop=c == NC - 1)
                        ins.then_inc(xa_ready, 1)

            def transpose_y(src, n):
                pe.wait_ge(tl_lo, n)
                for c in range(NC):
                    ins = nc.tensor.transpose(wide(6)[:, c * P:(c + 1) * P], src[:, c * P:(c + 1) * P], ident[:, :])
                ins.then_inc(tl_ready, 1)

            def ffn_half(i, half):
                if half or not isinstance(i, int) or i > 0:
                    pe.wait_ge(ff_ok, 2 * i + half - 1)
                for c in range(NC):
                    ins = passes(bank(4 + half),
                                 split_passes(lambda h: cols(ln_t, i * HSLAB + (h * NC + c) * P, P),
                                              lambda h: w_eff[:, h, c, half * 512:(half + 1) * 512]),
                                 c == 0, c == NC - 1)
                ins.then_inc(ff_ready, 1)

            pe.wait_ge(we_sum, 2 * NC)
            pe.wait_ge(y2_ok, 1)
            transpose_y(y_buf[:, 0, :], 0)
            pe.wait_ge(y2_ok, 2)
            transpose_y(y_buf[:, 1, :], 1)
            pe.wait_ge(we_ok, NC)
            for half in range(2):
                ffn_half(0, half)
            pe.wait_ge(y2_ok, 3)
            transpose_y(y_buf[:, 0, :], 2)
            for half in range(2):
                ffn_half(1, half)

            def ffn_step(i, buf):
                if buf is not None:
                    pe.wait_ge(y2_ok, i + 2)
                    transpose_y(y_buf[:, buf, :], 2 * i - 1)
                ffn_half(i, 0)
                pe.wait_ge(y3_ok, i - 1)
                transpose_y(y3_buf, 2 * i if buf is not None else 2 * i - 1)
                ffn_half(i, 1)

            with pe.Fori(0, 2) as r:
                for k in range(2):
                    ffn_step(2 * r + 2 + k, (k + 1) % 2)
            ffn_step(6, 1)
            ffn_step(7, None)

            def latents(b):
                return lambda c, h: batch_slabs(b)[:, :, h, c, :]

            def latent(i):
                return lambda c, h: slab(i, h)[:, c * P:(c + 1) * P]

            pe.wait_ge(ff_ok, 2 * NT)
            project_k(4, lambda c: None, latents(0), by_tile)
            pe.wait_ge(y3_ok, 7)
            transpose_y(y3_buf, 14)
            for tt in range(TPB):
                project_v(4, tt, latent(tt))
                if tt == 1:
                    pe.wait_ge(y3_ok, 8)
                    transpose_y(y3_buf, 15)
            pe.wait_ge(tl_lo, 2 * NT)
            project_k(5, lambda c: None, latents(1), by_tile)
            for tt in range(2):
                project_v(5, tt, latent(TPB + tt))

            def q_parts(b, blocks=range(NJ)):
                src = ln_t[:, b * TPB * HSLAB:(b + 1) * TPB * HSLAB].rearrange(
                    "p (t h c k) -> p t h c k", t=TPB, h=2, c=NC)
                for j in blocks:
                    for c in range(NC):
                        for n, (hw, hx) in enumerate(((HI, HI), (HI, LO), (LO, HI))):
                            yield j, c, n, wq[:, hw, c, j * P:(j + 1) * P], src[:, :, hx, c, :]

            def q_product(base, k, part):
                j, c, n, a, x = part
                if c == 0 and n == 0:
                    pe.wait_ge(sp_free, base + k - 1)
                ins = nc.tensor.matmul(by_tile(bank(spare(k))), a, x,
                                       start=c == 0 and n == 0, stop=c == NC - 1 and n == 2)
                if c == NC - 1 and n == 2:
                    ins.then_inc(sp_ready, 1)

            def o_transposes(base, k, b, j):
                pe.wait_ge(sp_free, base + k - 1)
                for qt in range(TPB):
                    ins = nc.tensor.transpose(bank(spare(k))[:, qt * P:(qt + 1) * P],
                                              o_tok[:, b, qt, j * P:(j + 1) * P], ident[:, :])
                ins.then_inc(sp_ready, 1)

            def out_product(base, k, w, last_o, between=lambda: None):
                if w == 0:
                    pe.wait_ge(sp_free, base + last_o + 1)
                if w > 0 or last_o < k - 2:
                    pe.wait_ge(sp_free, base + k - 1)
                qt, half = w // 2, w % 2
                for j in range(NJ):
                    ins = passes(bank(spare(k)), split_passes(lambda h: o_t[:, j, h, qt * P:(qt + 1) * P],
                                                              lambda h: wo[:, h, j, half * 512:(half + 1) * 512]),
                                 j == 0, j == NJ - 1)
                    if j == NJ - 1:
                        ins.then_inc(sp_ready, 1)
                    between()

            def pre_product(v, s, b, h, k):
                if k == 0:
                    pe.wait_ge(pre_ok, N_PRE * v)
                elif k == 1:
                    pe.wait_ge(row_ok, v)
                else:
                    pe.wait_ge(pre_ok, N_PRE * v + k - 1)
                qt, sb_ = k // 3, k % 3
                nc.tensor.matmul(bank(pre_bank(s, k)), q_head[0:HD, b, h, HI, qt * P:(qt + 1) * P],
                                 k_head[0:HD, b, HI, sb_ * 512:(sb_ + 1) * 512], start=True, stop=True
                                 ).then_inc(pre_ready, 1)

            def row_transpose(v, s):
                pe.wait_ge(nm_ok, v + 1)
                for qt in range(TPB):
                    ins = nc.tensor.matmul(bank(pre_bank(s, N_PRE), 512, HD + 1)[:, qt * P:(qt + 1) * P],
                                           neg_max[:, s % 2, qt, 0:HD + 1], ident_h[:, :], start=True, stop=True)
                ins.then_inc(row_ready, 1)

            def score_block(u, n, b, h, i):
                if i == 0:
                    pe.wait_ge(row_ok, u + 1)
                pe.wait_ge(exp_ok, n + 1)
                ks = slice(i * P, (i + 1) * P)
                out = bank(i % 2)
                nc.tensor.matmul(out, k_head[0:HD + 1, b, HI, ks], q_head[0:HD + 1, b, h, HI, :], start=True, stop=False)
                nc.tensor.matmul(out, k_head[0:HD, b, HI, ks], q_head[0:HD, b, h, LO, :], start=False, stop=False)
                nc.tensor.matmul(out, k_head[0:HD, b, LO, ks], q_head[0:HD, b, h, HI, :], start=False, stop=True
                                 ).then_inc(sc_ready, 1)

            def pv_block(g, u, n, b, i):
                if i == 0:
                    pe.wait_ge(v_ld[b], 16 * (g + 1))
                pe.wait_ge(plo_ok, NPF + n + 1)
                for qt in range(TPB):
                    if i == 0 and qt % 2 == 0:
                        pe.wait_ge((oraw_ok, oraw2_ok)[qt // 2], u)
                    tok = slice(qt * P, (qt + 1) * P)
                    out = bank(4 + qt // 2)[:, (qt % 2) * VW:(qt % 2 + 1) * VW]
                    nc.tensor.matmul(out, p_hi[:, i % NPB, tok], v_head[:, b, i, :],
                                     start=i == 0 and qt % 2 == 0, stop=False, skip_group_check=True)
                    ins = nc.tensor.matmul(out[:, 0:HD + 1], p_lo[:, i % NPB, tok], v_head[:, b, i, 0:HD + 1],
                                           start=False, stop=i == NS - 1, skip_group_check=True)
                ins.then_inc(pv_ok, 1)

            pe.wait_ge(w_split, W_WQ0 + RING)
            for part in q_parts(0):
                j, c, n, a, x = part
                if j == 2 and c == 0 and n == 0:
                    pe.wait_ge(sp_free, 1)
                ins = nc.tensor.matmul(by_tile(bank(6 + j % 2)), a, x, start=c == 0 and n == 0, stop=c == NC - 1 and n == 2)
                if c == NC - 1 and n == 2:
                    ins.then_inc(sp_ready, 1)

            def first_maxima(c):
                if c == 0:
                    pe.wait_ge(k_lo_ok, 6 * NJ)
                    pe.wait_ge(v_lo_ok, 6 * 4 - 1)
                    pe.wait_ge(k_ld[0], 16)
                    pe.wait_ge(q_ld[0], 16 * 6)
                for k in range(N_PRE * c // NC, N_PRE * (c + 1) // NC):
                    pre_product(0, 0, 0, 0, k)

            project_v(5, 2, latent(TPB + 2))
            project_v(5, 3, latent(TPB + 3), first_maxima)
            row_transpose(0, 0)
            pe.wait_ge(v_lo_ok, 6 * 4)

            def expert_transposes(i):
                pe.wait_ge(y4_ok, i + 1)
                if i > 1:
                    pe.wait_ge(t4_lo, i - 1)
                for c in range(NC):
                    ins = nc.tensor.transpose(wide(2 * (i % 2))[:, c * P:(c + 1) * P],
                                              y_all[:, i, c * P:(c + 1) * P], ident[:, :])
                ins.then_inc(t4_ready, 1)

            def router(i):
                pe.wait_ge(t4_lo, i + 1)
                if i > 0:
                    pe.wait_ge(lg_step, LG_STEPS * i - 1)
                for c in range(NC):
                    ins = passes(bank(4, NE), split_passes(lambda h: slab(i, h)[:, c * P:(c + 1) * P],
                                                           lambda h: rw[:, c, h * NE:(h + 1) * NE]), c == 0, c == NC - 1)
                ins.then_inc(lg_ready, 1)

            def iteration(g, last):
                base = SP0 + SP_ITER * g
                u0, n0 = SLOTS * g, SLOTS * NS * g
                queries = list(q_parts(1))
                for s in range(SLOTS):
                    b, h = s // G, s % G
                    nb, nh = (s + 1) // G, (s + 1) % G
                    k = 0
                    if s == G - 1:
                        pe.wait_ge(k_ld[1], 16 * (g + 1))
                        pe.wait_ge(q_ld[1], 16 * 6 * (g + 1))
                    if s == 5:
                        pe.wait_ge(w_split, W_G + 2 * RING * g + RING)
                    for i in range(NS):
                        score_block(u0 + s, n0 + NS * s + i, b, h, i)
                        if s < SLOTS - 1:
                            for _ in range(PRE_AT[i]):
                                pre_product(u0 + s + 1, s + 1, nb, nh, k)
                                k += 1
                            if i == ROW_STEP:
                                row_transpose(u0 + s + 1, s + 1)
                        if i >= LAG:
                            pv_block(g, u0 + s, n0 + NS * s + i - LAG, b, i - LAG)
                        elif s > 0:
                            pv_block(g, u0 + s - 1, n0 + NS * s + i - LAG, (s - 1) // G, NS + i - LAG)
                        for _ in range(3):
                            if s < 2:
                                q_product(base, SPQ1 + queries[0][0], queries.pop(0))
                        if s == G and i in T0_STEPS:
                            if T0_STEPS[i] == 0:
                                pe.wait_ge(o_ok, u0 + G)
                            o_transposes(base, SPT0 + T0_STEPS[i], 0, T0_STEPS[i])
                        if s in WO_STEPS and i in WO_STEPS[s]:
                            out_product(base, SPO0 + WO_STEPS[s][i], WO_STEPS[s][i], SPO0 - 1)
                for i in range(NS - LAG, NS):
                    pv_block(g, u0 + SLOTS - 1, n0 + NS * (SLOTS - 1) + i, 1, i)
                k, m = SPX, 0
                if not last:
                    pe.wait_ge(w_split, W_G + 2 * RING * (g + 1))
                for what, j in END_LAST if last else END:
                    if what == "q":
                        for part in q_parts(0, (j,)):
                            q_product(base, k, part)
                    else:
                        if j == 0:
                            pe.wait_ge(o_ok, u0 + SLOTS)
                        o_transposes(base, k, 1, j)
                        last_o = k
                    k += 1

                def next_maxima():
                    nonlocal m
                    if m == 0:
                        pe.wait_ge(k_ld[0], 16 * (g + 2))
                        pe.wait_ge(q_ld[0], 16 * 6 * (g + 2))
                    pre_product(u0 + SLOTS, 0, 0, 0, m)
                    m += 1

                if last:
                    pe.wait_ge(exp_ok, 2 + SLOTS * NS * KV)
                    expert_transposes(0)
                for w in range(8):
                    if not last and 2 <= w <= 5:
                        out_product(base, k, w, last_o, next_maxima)
                    else:
                        out_product(base, k, w, last_o)
                    k += 1
                    if not last and w == 6:
                        row_transpose(u0 + SLOTS, 0)
                    if last and w % 2 == 1:
                        if w == 1:
                            pe.wait_ge(oraw_ok, SLOTS * KV)
                            pe.wait_ge(oraw2_ok, SLOTS * KV)
                        router(w // 2)
                        if w // 2 + 1 < TPB:
                            expert_transposes(w // 2 + 1)

            with pe.Fori(0, KV - 1) as g:
                iteration(g, False)
            iteration(KV - 1, True)

            sp_end = SP0 + SP_ITER * KV - NJ
            pe.wait_ge(sp_free, sp_end)
            for i in range(NT):
                pe.wait_ge(wt_ok, i + 1)
                nc.tensor.transpose(wide(5, F16)[:, 0:P], w_tok[:, i % 2, :], ident_h[:, :]).then_inc(wx_ready, 1)
                if i + TPB < NT:
                    expert_transposes(i + TPB)
                pe.wait_ge(wx_ok, i + 1)
                if i > 0:
                    pe.wait_ge(fin_ok, 2 * i)
                for half in range(2):
                    hs = slice(half * 512, (half + 1) * 512)
                    nc.tensor.matmul(bank(6 + half), w_exp[:, i % 2, :], eb_hi[:, hs], start=True, stop=False)
                    nc.tensor.matmul(bank(6 + half), w_exp[0:NE, i % 2, :], eb_lo[:, hs], start=False, stop=True
                                     ).then_inc(mix_ready, 1)
                if i + TPB < NT:
                    router(i + TPB)

        @block.scalar
        def _(act):
            def copy(out, in_):
                return nc.scalar.activation(out, in_, ACT.Copy)

            def affine(out, in_, scale, bias):
                return nc.scalar.activation(out, in_, ACT.Identity, scale=scale, bias=bias)

            def keys(t):
                act.wait_ge(kv_stored, 48 * t)
                for j in range(NJ):
                    act.wait_ge(k_ready, NJ * t + j + 1)
                    copy(k_out[:, j, HI, :], bank(j)).then_inc(k_hi_ok, 1)

            def values(t, tt):
                act.wait_ge(v_ready, 4 * t + tt + 1)
                copy(v_out[:, :, tt, 0:HD], bank(3 + tt % 2, KVD).rearrange("p (k d) -> p k d", k=KV)
                     ).then_inc(v_hi_ok, 1)

            def normalise(out, i, ln):
                act.wait_ge(ln_ok, ln + i + 1)
                return affine(out, x_tile(i), cols(rstd, ln + i, 1), cols(nmr, ln + i, 1))

            act.sem_inc(exp_ok, 2)
            act.wait_ge(par_ld, 16)
            nc.scalar.activation(tg[:, :], par[:, 0:4], ACT.Tanh).then_inc(tanh_ok, 1)
            def split_kv_weights(w):
                for s in range(RING):
                    act.wait_ge(w_ld[w][s], 16)
                    cs = slice(2 * s, 2 * s + 2)
                    copy((wk, wv)[w][:, HI, cs, :], w_land[:, w, cs, :]).then_inc(w_hi, 1)

            def split_ctx(t):
                if t >= 2:
                    act.wait_ge(v_ready, 4 * (t - 1))
                for s in range(RING):
                    act.wait_ge(ld[s], 16 * (CY_B + 4 * (t // 2) + t % 2 + 1))
                    copy(ctx_t[:, t % 2, 2 * s:2 * s + 2, HI, :],
                         stage[:, s, :].rearrange("p (c n) -> p c n", c=2)).then_inc(c_hi, 1)

            def scale_ctx(b, n):
                s = n % RING
                act.wait_ge(ld[s], 16 * (CY_B + 4 * b + 2 + n // RING + 1))
                affine(stage[:, s, :], stage[:, s, :], sc[:, RS2:RS2 + 1], par[:, Z2:Z2 + 1]).then_inc(n_aff, 1)

            def scale_x(i):
                if i >= 2:
                    act.wait_ge(q1_ok, i - 1)
                y = y_buf[:, i % 2, :]
                normalise(y, i, LN1).then_inc(y1_ok, 1)
                act.wait_ge(y1_ok, i + 1)
                affine(y, y, sc[:, RS1:RS1 + 1], par[:, Z1:Z1 + 1]).then_inc(t1_ok, 1)

            def add_beta(i):
                act.wait_ge(beta_ok, i + 1)
                nc.scalar.activation(x_tile(i), x_tile(i), ACT.Identity, bias=cols(beta, i, 1)).then_inc(xb_ok, 1)

            def take_q1(i):
                act.wait_ge(tq_ready, i + 1)
                copy(slab(i, HI), wide((5, 0)[i % 2], F16)).then_inc(tq_ok, 1)

            split_kv_weights(0)
            split_ctx(0)
            split_kv_weights(1)
            act.wait_ge(scal_ok, 1)
            act.wait_ge(id_ld, 16)
            copy(ident_h[:, :], ident[:, :]).then_inc(const_ok, 1)
            for b in range(B):
                t, i0 = 2 * b, TPB * b
                scale_x(i0)
                scale_x(i0 + 1)
                keys(t)
                values(t, 0)
                split_ctx(t + 1)
                for tt in range(1, TPB):
                    values(t, tt)
                take_q1(i0)
                take_q1(i0 + 1)
                for n in range(4):
                    scale_ctx(b, n)
                scale_x(i0 + 2)
                scale_x(i0 + 3)
                keys(t + 1)
                for tt in range(TPB):
                    values(t + 1, tt)
                    if tt < 2:
                        scale_ctx(b, 4 + 2 * tt)
                        scale_ctx(b, 5 + 2 * tt)
                    add_beta(i0 + tt)
                take_q1(i0 + 2)
                take_q1(i0 + 3)
                if b + 1 < B:
                    split_ctx(t + 2)
                for half in range(2):
                    act.wait_ge(cs_ready, 2 * b + half + 1)
                    nc.scalar.activation(cols(region_b, b * D + half * 512, 512), bank(6 + half), ACT.Copy,
                                         scale=sc[:, CC:CC + 1]).then_inc(cs_ok, 1)

            act.wait_ge(enc_ld, 16)
            copy(enc[0:R, HI, :], enc_f[0:R, :]).then_inc(enc_hi, 1)
            act.wait_ge(f_used, NC)
            for half in range(2):
                copy(u_t[0:R, HI, half * 512:(half + 1) * 512], bank(1 + half, 512, R)).then_inc(u_hi, 1)
            for c in range(NC):
                act.wait_ge(we_sum, 2 * (c + 1))
                copy(w_eff[:, HI, c, :], stage[:, c % RING, :]).then_inc(we_hi, 1)
            act.wait_ge(bb_ld, 16)
            nc.scalar.activation(bias_rows, bias_rows, ACT.Copy, scale=tg[:, 2:3]).then_inc(bias_ok, 1)

            def take_high(i, n):
                act.wait_ge(tl_ready, n + 1)
                copy(slab(i, HI), wide(6)).then_inc(tl_hi, 1)

            def norm2(i, buf, before):
                if before is not None:
                    act.wait_ge(tl_ready, before)
                normalise(buf, i, LN2).then_inc(y2_ok, 1)

            def norm3(i, before):
                if before is not None:
                    act.wait_ge(tl_ready, before)
                normalise(y3_buf, i, LN3).then_inc(y3_ok, 1)

            norm2(0, y_buf[:, 0, :], None)
            norm2(1, y_buf[:, 1, :], None)
            take_high(0, 0)
            norm2(2, y_buf[:, 0, :], 1)
            take_high(1, 1)
            norm2(3, y_buf[:, 1, :], 2)
            take_high(2, 2)
            act.wait_ge(xc_ok, NT)

            def ffn_step(i, par):
                if par is not None:
                    take_high(i + 1, 2 * i - 1)
                    if not isinstance(i, int):
                        norm2(i + 2, y_buf[:, 1 - par, :], 2 * i - 1)
                norm3(i - 2, 2 * i - 1)
                take_high(i - 2, 2 * i if par is not None else 2 * i - 1)

            with act.Fori(0, 2) as r:
                for k in range(2):
                    ffn_step(2 * r + 2 + k, (k + 1) % 2)
            ffn_step(6, 1)
            ffn_step(7, None)
            norm3(6, 14)
            keys(4)
            take_high(6, 14)
            values(4, 0)
            norm3(7, 15)
            values(4, 1)
            take_high(7, 15)
            values(4, 2)
            values(4, 3)
            keys(5)

            def wq_hi(cycle, s):
                act.wait_ge(ld[s], 16 * (cycle + 1))
                copy(wq[:, HI, 2 * s:2 * s + 2, :], stage[:, s, 0:2 * QG].rearrange("p (c n) -> p c n", c=2)
                     ).then_inc(w_hi, 1)

            def wo_hi(cycle, s):
                act.wait_ge(ld[s], 16 * (cycle + 1))
                copy(wo[:, HI, :, s * 256:(s + 1) * 256], stage[:, s, 0:NJ * 256].rearrange("p (j n) -> p j n", j=NJ)
                     ).then_inc(w_hi, 1)

            def take_q(first, k, j):
                act.wait_ge(sp_ready, first + 1)
                copy(q_blk[:, j, HI, :], bank(spare(k))).then_inc(sp_hi, 1)

            def take_o(first, k, j):
                act.wait_ge(sp_ready, first + 1)
                copy(o_t[:, j, HI, :], bank(spare(k))).then_inc(sp_hi, 1)

            def take_row(v, s, b, h):
                act.wait_ge(row_ready, v + 1)
                copy(q_head[HD:HD + 1, b, h, HI, :], ps[HD:HD + 1, pre_bank(s, N_PRE), :]).then_inc(row_ok, 1)

            def take_sums(u):
                act.wait_ge(pv_ok, NPB + NS * (u + 1))
                act.wait_ge(o_ok, u)
                copy(o_raw[:, 0:2, :].rearrange("p t w -> p (t w)"), bank(4, 2 * VW)).then_inc(oraw_ok, 1)

            act.wait_ge(k_ready, 6 * NJ)
            for s in range(RING):
                wq_hi(CY_WQ0, s)
            values(5, 0)
            values(5, 1)
            for j in range(NJ):
                act.wait_ge(sp_ready, j + 1)
                copy(q_blk[:, j, HI, :], bank(6 + j % 2)).then_inc(sp_hi, 1)
            values(5, 2)
            values(5, 3)
            act.wait_ge(ld[0], 16 * (CY_E + 1))
            copy(rw[:, :, 0:NE], stage[:, 0, 0:NC * NE].rearrange("p (c n) -> p c n", c=NC)).then_inc(w_hi, 1)
            for s in range(1, RING):
                c0, c1 = EB_CUTS[s - 1:s + 1]
                act.wait_ge(ld[s], 16 * (CY_E + 1))
                copy(eb_hi[:, c0:c1], stage[:, s, 0:c1 - c0]).then_inc(w_hi, 1)
            take_row(0, 0, 0, 0)

            def iteration(g, last):
                base = SP0 + SP_ITER * g
                u0, n0 = SLOTS * g, SLOTS * NS * g
                for s in range(SLOTS):
                    for i in range(NS):
                        n = n0 + NS * s + i
                        if s > 0 and i == LAG:
                            take_sums(u0 + s - 1)
                        if s < SLOTS - 1 and i == ROW_STEP + 1:
                            take_row(u0 + s + 1, s + 1, (s + 1) // G, (s + 1) % G)
                        act.wait_ge(sc_ready, n + 1)
                        act.wait_ge(plo_ok, n + 1)
                        nc.scalar.activation(p_f32[:, i % NPF, :], bank(i % 2), ACT.Exp, scale=SCALE)
                        act.wait_ge(pv_ok, n + 1)
                        nc.scalar.activation(p_hi[:, i % NPB, :], bank(i % 2), ACT.Exp, scale=SCALE).then_inc(exp_ok, 1)
                        if (s, i) in Q1_TAKE:
                            j = Q1_TAKE[s, i]
                            take_q(base + SPQ1 + j, SPQ1 + j, j)
                        if s == G and i - 1 in T0_STEPS:
                            j = T0_STEPS[i - 1]
                            take_o(base + SPT0 + j, SPT0 + j, j)
                        if s == WO_SPLIT and i in SPLIT_STEPS:
                            wo_hi(CY_G + 2 * g, SPLIT_STEPS[i])
                        if s == WQ_SPLIT and i in SPLIT_STEPS and not last:
                            wq_hi(CY_G + 1 + 2 * g, SPLIT_STEPS[i])
                take_sums(u0 + SLOTS - 1)
                for k, (what, j) in enumerate(END_LAST if last else END, SPX):
                    (take_q if what == "q" else take_o)(base + k, k, j)
                if not last:
                    take_row(u0 + SLOTS, 0, 0, 0)

            with act.Fori(0, KV - 1) as g:
                iteration(g, False)
            iteration(KV - 1, True)

            def expert_norm(i):
                normalise(y_all[:, i, :], i, LN4).then_inc(y4_ok, 1)

            def expert_high(i):
                act.wait_ge(t4_ready, i + 1)
                copy(slab(i, HI), wide(2 * (i % 2))).then_inc(t4_hi, 1)

            def expert_exp(i):
                act.wait_ge(lg_ok, i + 1)
                nc.scalar.activation(logit[:, i, :], logit[:, i, :], ACT.Exp, bias=nmx[:, i:i + 1],
                                     accum_out=esum[:, i:i + 1]).then_inc(ex_ok, 1)

            expert_norm(0)
            expert_norm(1)
            for i in range(TPB):
                expert_high(i)
                if i + 2 < TPB:
                    expert_norm(i + 2)
                if i > 0:
                    expert_exp(i - 1)
            act.wait_ge(pv_ok, NPB + SLOTS * NS * KV)
            expert_norm(TPB)
            expert_exp(TPB - 1)
            for i in range(NT):
                act.wait_ge(wx_ready, i + 1)
                if i > 1:
                    act.wait_ge(mix_ready, 2 * (i - 1))
                copy(w_exp[:, i % 2, :], wide(5, F16)[:, 0:P]).then_inc(wx_ok, 1)
                if i + TPB < NT:
                    expert_high(i + TPB)
                nc.scalar.activation(y_all[:, i, :], y_all[:, i, :], ACT.Copy, scale=ascale[:, i:i + 1]
                                     ).then_inc(ya_ok, 1)
                if i + TPB < NT:
                    if i + TPB + 1 < NT:
                        expert_norm(i + TPB + 1)
                    expert_exp(i + TPB)

        @block.vector
        def _(dve):
            def minus(out, a, b):
                return nc.vector.tensor_tensor(out, a, b, ALU.subtract)

            def stats(i, ln):
                n = ln + i
                dve.sem_inc(bn_go, 1)
                for half in range(2):
                    ins = nc.vector.bn_stats(bn[:, half, :], x_tile(i, half * 512, 512))
                ins.then_inc(bn_step, 1)
                dve.wait_ge(bn_step, 2 * n + 1)
                dve.sem_inc(bn_go, 1)
                nc.vector.bn_aggr(mv[:, :], bn[:, :, :]).then_inc(bn_step, 1)
                dve.wait_ge(bn_step, 2 * n + 2)
                nc.vector.tensor_scalar(cols(nmean, n, 1), mv[:, 0:1], -1.0, None, ALU.mult)
                nc.vector.tensor_scalar(cols(var_c, n, 1), mv[:, 1:2], EPS, None, ALU.add).then_inc(ln_var, 1)

            def keys(t):
                for j in range(NJ):
                    dve.wait_ge(k_hi_ok, NJ * t + j + 1)
                    minus(k_out[:, j, LO, :], bank(j), k_out[:, j, HI, :]).then_inc(k_lo_ok, 1)

            def values(t, tt):
                dve.wait_ge(v_hi_ok, 4 * t + tt + 1)
                minus(v_out[:, :, tt, HD + 1:VW], bank(3 + tt % 2, KVD).rearrange("p (k d) -> p k d", k=KV),
                      v_out[:, :, tt, 0:HD]).then_inc(v_lo_ok, 1)

            def col(i):
                return sc[:, i:i + 1]

            def scalar(i, out, in_, s1, s2, op0, op1=ALU.bypass):
                nc.vector.tensor_scalar(col(out), in_, s1, s2, op0, op1).then_inc(scal_step, 1)
                dve.wait_ge(scal_step, i + 1)

            nc.vector.memset(v_out[:, :, :, HD:HD + 1], 1.0)
            nc.vector.memset(ones_h[:, :], 1.0).then_inc(const_ok, 1)
            dve.wait_ge(par_ld, 16)
            dve.wait_ge(tanh_ok, 1)
            nc.vector.reciprocal(col(RS1), par[:, S1:S1 + 1])
            nc.vector.reciprocal(col(RS2), par[:, S2:S2 + 1])
            scalar(0, ALPHA, tg[:, 0:1], par[:, S1:S1 + 1], par[:, S2:S2 + 1], ALU.mult, ALU.mult)
            scalar(1, D1, par[:, Z1:Z1 + 1], -1.0, MID, ALU.mult, ALU.add)
            scalar(2, D2, par[:, Z2:Z2 + 1], -1.0, MID, ALU.mult, ALU.add)
            scalar(3, CC, col(D1), col(ALPHA), None, ALU.mult)
            scalar(4, CR, col(D2), col(ALPHA), None, ALU.mult)
            scalar(5, CK, col(CR), col(D1), float(D), ALU.mult, ALU.mult)
            nc.vector.tensor_scalar(col(TGW), tg[:, 2:3], 1.0 / WS, None, ALU.mult).then_inc(scal_ok, 1)
            def split_kv_weights(w):
                for s in range(RING):
                    cs, k = slice(2 * s, 2 * s + 2), (wk, wv)[w]
                    dve.wait_ge(w_hi, RING * w + s + 1)
                    minus(k[:, LO, cs, :], w_land[:, w, cs, :], k[:, HI, cs, :]).then_inc(w_split, 1)

            def quant_ctx(b, n):
                s = n % RING
                dve.wait_ge(n_aff, NC * b + n + 1)
                nc.vector.tensor_scalar(stage[:, s, :], stage[:, s, :], 0.0, QMAX, ALU.max, ALU.min
                                        ).then_inc(n_clip, 1)
                dve.wait_ge(n_clip, NC * b + n + 1)
                nc.vector.tensor_scalar(cols(q2, (NC * b + n) * D, D), stage[:, s, :], MAGIC, MAGIC + MID,
                                        ALU.add, ALU.subtract).then_inc(n_done, 1)

            def quant_x(i):
                y, q = y_buf[:, i % 2, :], q1_buf[:, i % 2, :]
                dve.wait_ge(t1_ok, i + 1)
                nc.vector.tensor_scalar(y, y, 0.0, QMAX, ALU.max, ALU.min).then_inc(q1_clip, 1)
                dve.wait_ge(q1_clip, i + 1)
                if i >= 2:
                    dve.wait_ge(tq_ready, i - 1)
                nc.vector.tensor_scalar(q, y, MAGIC, MAGIC + MID, ALU.add, ALU.subtract).then_inc(q1_ok, 1)
                dve.wait_ge(q1_ok, i + 1)
                nc.vector.reduce_sum(cols(row_q, i, 1), q, axis=AX).then_inc(rowq_ok, 1)
                dve.wait_ge(rowq_ok, i + 1)
                nc.vector.tensor_scalar(cols(beta, i, 1), cols(row_q, i, 1), col(CR), col(CK), ALU.mult, ALU.add
                                        ).then_inc(beta_ok, 1)

            split_kv_weights(0)
            split_kv_weights(1)
            dve.wait_ge(scal_ok, 1)
            for b in range(B):
                t, i0 = 2 * b, TPB * b
                dve.wait_ge(x_ld, 16 * TPB * (b + 1))
                for k in range(TPB):
                    stats(i0 + k, LN1)
                quant_x(i0)
                quant_x(i0 + 1)
                keys(t)
                for tt in range(TPB):
                    values(t, tt)
                if b == 0:
                    dve.wait_ge(small_ld, 32)
                    nc.vector.tensor_tensor(coef, coef, mask, ALU.mult).then_inc(wsum_step, 1)
                    dve.wait_ge(wsum_step, 1)
                    nc.vector.reduce_sum(w_sum[:, :, :].rearrange("p c r -> p (c r)"), coef, axis=AX
                                         ).then_inc(wsum_ok, 1)
                for n in range(4):
                    quant_ctx(b, n)
                quant_x(i0 + 2)
                quant_x(i0 + 3)
                keys(t + 1)
                for tt in range(TPB):
                    values(t + 1, tt)
                    if tt < 2:
                        quant_ctx(b, 4 + 2 * tt)
                        quant_ctx(b, 5 + 2 * tt)

            dve.wait_ge(enc_hi, 1)
            minus(enc[0:R, LO, :], enc_f[0:R, :], enc[0:R, HI, :]).then_inc(enc_ok, 1)
            for half in range(2):
                hs = slice(half * 512, (half + 1) * 512)
                dve.wait_ge(u_hi, half + 1)
                minus(u_t[0:R, LO, hs], bank(1 + half, 512, R), u_t[0:R, HI, hs]).then_inc(u_lo, 1)
            for c in range(NC):
                s = c % RING
                dve.wait_ge(ld[s], 16 * (CY_WB + c // RING + 1))
                for half in range(2):
                    part = stage[:, s, half * 512:(half + 1) * 512]
                    dve.wait_ge(dl_ready, 2 * c + half + 1)
                    nc.vector.scalar_tensor_tensor(part, part, WS, bank((4, 6)[c % 2] + half), ALU.mult, ALU.add
                                                   ).then_inc(we_sum, 1)

            nc.vector.memset(v_out[:, :, :, HD:HD + 1], 1.0)

            with dve.Fori(0, B) as b:
                for k in range(TPB):
                    i = TPB * b + k
                    dve.wait_ge(xc_ok, i + 1)
                    for half in range(2):
                        xh = x_tile(i, half * 512, 512)
                        dve.wait_ge(xa_ready, 2 * i + half + 1)
                        nc.vector.scalar_tensor_tensor(xh, bank(2 * (k % 2) + half), col(ALPHA), xh, ALU.mult, ALU.add
                                                       ).then_inc(xa_ok, 1)
                    dve.wait_ge(xa_ok, 2 * i + 2)
                    stats(i, LN2)

            def take_low(i, n):
                dve.wait_ge(tl_hi, n + 1)
                minus(slab(i, LO), wide(6), slab(i, HI)).then_inc(tl_lo, 1)

            def add_ffn(i, half):
                if half == 0:
                    dve.wait_ge(xbias_ok, i + 1)
                xh = x_tile(i, half * 512, 512)
                dve.wait_ge(ff_ready, 2 * i + half + 1)
                nc.vector.scalar_tensor_tensor(xh, bank(4 + half), col(TGW), xh, ALU.mult, ALU.add
                                               ).then_inc(ff_ok, 1)
                if half == 1:
                    dve.wait_ge(ff_ok, 2 * i + 2)
                    stats(i, LN3)

            take_low(0, 0)
            take_low(1, 1)
            add_ffn(0, 0)
            add_ffn(0, 1)
            take_low(2, 2)
            add_ffn(1, 0)
            add_ffn(1, 1)

            def ffn_step(i, ahead):
                if ahead:
                    take_low(i + 1, 2 * i - 1)
                add_ffn(i, 0)
                take_low(i - 2, 2 * i if ahead else 2 * i - 1)
                add_ffn(i, 1)

            with dve.Fori(0, 2) as r:
                for k in range(2):
                    ffn_step(2 * r + 2 + k, True)
            ffn_step(6, True)
            ffn_step(7, False)
            nc.vector.memset(neg_max[:, :, :, :], 0.0)
            nc.vector.memset(k_head[HD:HD + 1, :, HI, :], 1.0)
            keys(4)
            take_low(6, 14)
            values(4, 0)
            values(4, 1)
            take_low(7, 15)
            values(4, 2)
            values(4, 3)
            keys(5)

            def split_wq(n, s):
                dve.wait_ge(w_hi, n + 1)
                minus(wq[:, LO, 2 * s:2 * s + 2, :], stage[:, s, 0:2 * QG].rearrange("p (c n) -> p c n", c=2),
                      wq[:, HI, 2 * s:2 * s + 2, :]).then_inc(w_split, 1)

            def split_wo(n, s):
                dve.wait_ge(w_hi, n + 1)
                cs = slice(s * 256, (s + 1) * 256)
                minus(wo[:, LO, :, cs], stage[:, s, 0:NJ * 256].rearrange("p (j n) -> p j n", j=NJ), wo[:, HI, :, cs]
                      ).then_inc(w_split, 1)

            def take_low_of(dst, n, k, j):
                dve.wait_ge(sp_hi, n + 1)
                minus(dst[:, j, LO, :], bank(spare(k)), dst[:, j, HI, :]).then_inc(sp_free, 1)

            def add_out(first, k, b, w):
                xh = x_tile(TPB * b + w // 2, (w % 2) * 512, 512)
                dve.wait_ge(sp_ready, first + 1)
                nc.vector.scalar_tensor_tensor(xh, bank(spare(k)), tg[:, 1:2], xh, ALU.mult, ALU.add
                                               ).then_inc(sp_free, 1)

            def reduce_max(v, s, k):
                dve.wait_ge(pre_ready, N_PRE * v + k + 1)
                nc.vector.reduce_max(pre_max[:, s % 2, k // 3, k % 3:k % 3 + 1], bank(pre_bank(s, k)), axis=AX
                                     ).then_inc(pre_ok, 1)

            def final_max(v, s):
                dve.wait_ge(pre_ok, N_PRE * (v + 1))
                nc.vector.reduce_max(row_max[:, :], pre_max[:, s % 2, :, :], axis=AX).then_inc(max_step, 1)
                dve.wait_ge(max_step, v + 1)
                nc.vector.tensor_scalar(neg_max[:, s % 2, :, HD:HD + 1], row_max[:, :].rearrange("p (t o) -> p t o", o=1),
                                        -1.0, None, ALU.mult).then_inc(nm_ok, 1)

            def take_sums(u):
                dve.wait_ge(pv_ok, NPB + NS * (u + 1))
                nc.vector.tensor_copy(o_raw[:, 2:4, :].rearrange("p t w -> p (t w)"), bank(5, 2 * VW)
                                      ).then_inc(oraw2_ok, 1)

            def divide(u, b, h):
                dve.wait_ge(oraw_ok, u + 1)
                dve.wait_ge(oraw2_ok, u + 1)
                nc.vector.reciprocal(den_inv[:, :].rearrange("p (t o) -> p t o", o=1), o_raw[:, :, HD:HD + 1])
                nc.vector.tensor_tensor(o_sum[:, :, :], o_raw[:, :, 0:HD], o_raw[:, :, HD + 1:VW], ALU.add
                                        ).then_inc(osum_ok, 1)
                dve.wait_ge(osum_ok, u + 1)
                den = den_inv[:, :].rearrange("p (t o) -> p t o", o=1).broadcast_to([P, TPB, HD])
                nc.vector.tensor_tensor(o_tok[:, b, :, h * HD:(h + 1) * HD], o_sum[:, :, :], den, ALU.mult
                                        ).then_inc(o_ok, 1)

            def expert_low(i):
                dve.wait_ge(t4_hi, i + 1)
                minus(slab(i, LO), wide(2 * (i % 2)), slab(i, HI)).then_inc(t4_lo, 1)

            def logits(i):
                n = LG_STEPS * i
                dve.wait_ge(lg_ready, i + 1)
                nc.vector.tensor_tensor(logit[:, i, :], bank(4, NE), rb[:, :], ALU.add).then_inc(lg_step, 1)
                dve.wait_ge(lg_step, n + 1)
                nc.vector.reduce_max(lmax[:, :], logit[:, i, :], axis=AX).then_inc(lg_step, 1)
                dve.wait_ge(lg_step, n + 2)
                nc.vector.tensor_scalar(nmx[:, i:i + 1], lmax[:, :], -1.0, None, ALU.mult).then_inc(lg_ok, 1)

            def choose(i):
                n = TOP_STEPS * i
                p, w = logit[:, i, :], w_tok[:, i % 2, :]
                dve.wait_ge(ex_ok, i + 1)
                nc.vector.max(top8[:, :], p).then_inc(top_step, 1)
                nc.vector.reciprocal(einv[:, :], esum[:, i:i + 1]).then_inc(top_step, 1)
                dve.wait_ge(top_step, n + 2)
                nc.vector.match_replace(rest[:, :], top8[:, :], p, 0.0)
                nc.vector.reduce_sum(wsum8[:, :], top8[:, :], axis=AX)
                nc.vector.tensor_scalar(mscale[:, i:i + 1], einv[:, :], tg[:, 3:4], None, ALU.mult).then_inc(top_step, 1)
                dve.wait_ge(top_step, n + 3)
                minus(p, p, rest[:, :]).then_inc(top_step, 1)
                nc.vector.tensor_scalar(ascale[:, i:i + 1], wsum8[:, :], mscale[:, i:i + 1], None, ALU.mult)
                dve.wait_ge(top_step, n + 4)
                if i > 1:
                    dve.wait_ge(wx_ready, i - 1)
                nc.vector.tensor_copy(w[:, 0:NE], p).then_inc(top_go, 1)
                dve.wait_ge(top_go, i + 1)
                minus(w[:, NE:2 * NE], p, w[:, 0:NE]).then_inc(wt_ok, 1)

            def add_mix(i):
                dve.wait_ge(xy_ok, i + 1)
                for half in range(2):
                    xh = x_tile(i, half * 512, 512)
                    dve.wait_ge(mix_ready, 2 * i + half + 1)
                    nc.vector.scalar_tensor_tensor(xh, bank(6 + half), mscale[:, i:i + 1], xh, ALU.mult, ALU.add
                                                   ).then_inc(fin_ok, 1)

            for s in range(RING):
                split_wq(W_WQ0 + s, s)
            values(5, 0)
            values(5, 1)
            for j in range(NJ):
                dve.wait_ge(sp_hi, j + 1)
                minus(q_blk[:, j, LO, :], bank(6 + j % 2), q_blk[:, j, HI, :]).then_inc(sp_free, 1)
            values(5, 2)
            for k in range(N_PRE):
                reduce_max(0, 0, k)
            final_max(0, 0)
            values(5, 3)
            dve.wait_ge(w_hi, W_E + 1)
            minus(rw[:, :, NE:2 * NE], stage[:, 0, 0:NC * NE].rearrange("p (c n) -> p c n", c=NC), rw[:, :, 0:NE]
                  ).then_inc(w_split, 1)
            for s in range(1, RING):
                c0, c1 = EB_CUTS[s - 1:s + 1]
                dve.wait_ge(w_hi, W_E + s + 1)
                minus(eb_lo[:, c0:c1], stage[0:NE, s, 0:c1 - c0], eb_hi[0:NE, c0:c1]).then_inc(w_split, 1)

            def iteration(g, last):
                base, high = SP0 + SP_ITER * g, SP0 + 4 * NJ * g
                u0 = SLOTS * g
                for s in range(SLOTS):
                    k = 0
                    for i in range(NS):
                        if s > 0 and i == LAG:
                            take_sums(u0 + s - 1)
                        if s < SLOTS - 1:
                            for _ in range(PRE_AT[i]):
                                reduce_max(u0 + s + 1, s + 1, k)
                                k += 1
                            if i == MAX_STEP:
                                final_max(u0 + s + 1, s + 1)
                        if s > 0 and i == LAG + 1:
                            if s == 1:
                                dve.wait_ge(kv_stored, 6 * 48)
                            divide(u0 + s - 1, (s - 1) // G, (s - 1) % G)
                        if (s, i) in Q1_TAKE:
                            j = Q1_TAKE[s, i]
                            take_low_of(q_blk, high + j, SPQ1 + j, j)
                        if s == G and i - 1 in T0_STEPS:
                            j = T0_STEPS[i - 1]
                            take_low_of(o_t, high + NJ + j, SPT0 + j, j)
                        if s in WO_STEPS and i - 1 in WO_STEPS[s]:
                            w = WO_STEPS[s][i - 1]
                            add_out(base + SPO0 + w, SPO0 + w, 0, w)
                        if s == WO_SPLIT and i in SPLIT_STEPS:
                            split_wo(W_G + 2 * RING * g + SPLIT_STEPS[i], SPLIT_STEPS[i])
                        if s == WQ_SPLIT and i in SPLIT_STEPS and not last:
                            split_wq(W_G + 2 * RING * g + RING + SPLIT_STEPS[i], SPLIT_STEPS[i])
                        if last and s == SLOTS - 1 and i >= NS - TPB:
                            if i == NS - TPB:
                                dve.wait_ge(sp_free, base + SPX)
                            stats(i - NS + TPB, LN4)
                take_sums(u0 + SLOTS - 1)
                divide(u0 + SLOTS - 1, 1, G - 1)
                k = SPX
                for what, j in END_LAST if last else END:
                    take_low_of(q_blk if what == "q" else o_t, high + 2 * NJ + k - SPX, k, j)
                    k += 1
                if last:
                    dve.wait_ge(rb_ld, 16)
                    expert_low(0)
                m = 0
                for w in range(8):
                    if not last and 2 <= w <= 5:
                        for _ in range(3):
                            reduce_max(u0 + SLOTS, 0, m)
                            m += 1
                        if w == 5:
                            final_max(u0 + SLOTS, 0)
                    add_out(base + k, k, 1, w)
                    k += 1
                    if last and w % 2 == 1:
                        dve.wait_ge(sp_free, base + k)
                        stats(TPB + w // 2, LN4)
                        logits(w // 2)
                        if w // 2 + 1 < TPB:
                            expert_low(w // 2 + 1)

            with dve.Fori(0, KV - 1) as g:
                iteration(g, False)
            iteration(KV - 1, True)

            for i in range(NT):
                choose(i)
                if i > 0:
                    add_mix(i - 1)
                if i + TPB < NT:
                    expert_low(i + TPB)
                if i + TPB < NT:
                    logits(i + TPB)
            add_mix(NT - 1)

        @block.gpsimd
        def _(pool):
            def tt(out, a, b, op):
                return nc.gpsimd.tensor_tensor(out, a, b, op)

            def deviations(i, ln):
                n = ln + i
                pool.wait_ge(ln_var, n + 1)
                tt(cols(rstd, n, 1), cols(var_c, n, 1), mhalf[:, :], ALU.pow).then_inc(ln_pow, 1)
                pool.wait_ge(ln_pow, n + 1)
                tt(cols(nmr, n, 1), cols(nmean, n, 1), cols(rstd, n, 1), ALU.mult).then_inc(ln_ok, 1)

            def split_ctx(t, half):
                for s in range(RING):
                    pool.wait_ge(c_hi, RING * t + s + 1)
                    tt(ctx_t[:, half, 2 * s:2 * s + 2, LO, :], stage[:, s, :].rearrange("p (c n) -> p c n", c=2),
                       ctx_t[:, half, 2 * s:2 * s + 2, HI, :], ALU.subtract).then_inc(c_split, 1)

            def add_columns(b):
                pool.wait_ge(cs_ok, 2 * b + 2)
                for k in range(TPB):
                    i = TPB * b + k
                    pool.wait_ge(xb_ok, i + 1)
                    tt(x_tile(i), x_tile(i), bc_buf[:, b, :], ALU.add).then_inc(xc_ok, 1)

            nc.gpsimd.memset(mhalf[:, :], -0.5).then_inc(half_ok, 1)
            pool.wait_ge(half_ok, 1)
            pool.sem_inc(plo_ok, NPF)
            for b in range(B):
                split_ctx(2 * b, 0)
                for k in range(TPB):
                    deviations(TPB * b + k, LN1)
                split_ctx(2 * b + 1, 1)
                if b > 0:
                    add_columns(b - 1)
            add_columns(B - 1)
            for c in range(NC):
                pool.wait_ge(we_hi, c + 1)
                tt(w_eff[:, LO, c, :], stage[:, c % RING, :], w_eff[:, HI, c, :], ALU.subtract).then_inc(we_ok, 1)
            with pool.Fori(0, NT) as i:
                deviations(i, LN2)
            pool.wait_ge(bias_ok, 1)
            with pool.Fori(0, NT) as i:
                pool.wait_ge(y2_ok, i + 1)
                tt(x_tile(i), x_tile(i), bias_rows, ALU.add).then_inc(xbias_ok, 1)
                deviations(i, LN3)
            with pool.Fori(0, SLOTS * KV) as u:
                for i in range(NS):
                    n = NS * u + i
                    pool.wait_ge(exp_ok, 2 + n + 1)
                    tt(p_lo[:, i % NPB, :], p_f32[:, i % NPF, :], p_hi[:, i % NPB, :], ALU.subtract).then_inc(plo_ok, 1)

            for i in range(NT):
                deviations(i, LN4)
            for i in range(NT):
                pool.wait_ge(ya_ok, i + 1)
                tt(x_tile(i), x_tile(i), y_all[:, i, :], ALU.add).then_inc(xy_ok, 1)


def kernel(x, ctx_4096, g_xattn, g_ffn, L0_xattn_x1_scale, L0_xattn_x1_zp, L0_xattn_x2_scale, L0_xattn_x2_zp,
           L0_ffn_W_base, L0_ffn_b_base, L0_ffn_enc0, L0_ffn_enc1, L0_ffn_coefs0, L0_ffn_coefs1, L0_ffn_mask0,
           L0_ffn_mask1, L1_xattn_Wq, L1_xattn_Wk, L1_xattn_Wv, L1_xattn_Wo, L1_ffn_router_weight,
           L1_ffn_router_bias, L1_ffn_expert_bias):
    import concourse.bacc as bacc
    import numpy as np
    from concourse.bass_utils import run_bass_kernel_spmd

    c = np.ascontiguousarray

    def by_chunk(w):
        return c(w.reshape(NC, P, -1).transpose(1, 0, 2))

    def rows(v):
        return c(np.broadcast_to(v.reshape(1, -1), (P, v.size)))

    o = np.arange(D)
    table = np.zeros((D, D))
    table[0] = 1 / np.sqrt(D)
    for k in range(1, D // 2):
        table[2 * k - 1] = np.sqrt(2 / D) * np.cos(2 * np.pi * (k * o % D) / D)
        table[2 * k] = np.sqrt(2 / D) * np.sin(2 * np.pi * (k * o % D) / D)
    table[D - 1] = (1 - 2 * (o % 2)) / np.sqrt(D)
    table = (table * (WS / 2)).astype(np.float32)

    coef = np.concatenate([L0_ffn_coefs0, L0_ffn_coefs1], 2).transpose(1, 2, 0)
    mask = np.concatenate([L0_ffn_mask0, L0_ffn_mask1], 2).transpose(1, 2, 0)
    eb = np.concatenate([L1_ffn_expert_bias, L1_ffn_expert_bias], 0)
    wq = L1_xattn_Wq.T.reshape(NC, P, KV, QG).transpose(2, 1, 0, 3).reshape(KV * P, NC, QG)
    wo = L1_xattn_Wo.T.reshape(KV, NJ, P, D).transpose(0, 2, 1, 3).reshape(KV * P, NJ, D)
    host = {
        "x": c(x.reshape(B * QL, D)),
        "ctx": c(ctx_4096),
        "ctx_t": c(ctx_4096.transpose(0, 2, 1)),
        "par": rows(np.concatenate([g_xattn, g_ffn, L0_xattn_x1_scale, L0_xattn_x1_zp, L0_xattn_x2_scale,
                                    L0_xattn_x2_zp])),
        "ident": np.eye(P, dtype=np.float32),
        "wk": by_chunk(L1_xattn_Wk.T),
        "wv": by_chunk(L1_xattn_Wv.T),
        "wq": c(wq),
        "wo": c(wo),
        "wb": c(L0_ffn_W_base.T),
        "bb": rows(L0_ffn_b_base),
        "ft": by_chunk(table),
        "coef": by_chunk(coef.reshape(D, R * E)).reshape(P, NC * R, E),
        "mask": by_chunk(mask.reshape(D, R * E)).view(np.int32),
        "enc": c(np.concatenate([L0_ffn_enc0, L0_ffn_enc1], 0)),
        "rw": by_chunk(L1_ffn_router_weight.T),
        "rb": rows(L1_ffn_router_bias),
        "eb": c(eb),
    }
    nc = bacc.Bacc("TRN2", target_bir_lowering=False, num_devices=1)
    aps = [nc.dram_tensor(f"{name}_in", a.shape, I32 if name == "mask" else F32, kind="ExternalInput").ap()
           for name, a in host.items()]
    out = nc.dram_tensor("out", (B * QL, D), F32, kind="ExternalOutput").ap()
    flamingo(nc, *aps, out)
    result = run_bass_kernel_spmd(nc, [{f"{name}_in": a for name, a in host.items()}], core_ids=[0])
    return result.results[0]["out"].reshape(B, QL, D)
```

```python
from contextlib import ExitStack

import concourse.bass as bass
from concourse import mybir
from concourse.alu_op_type import AluOpType as ALU

ACT = mybir.ActivationFunctionType
F32 = mybir.dt.float32
F16 = mybir.dt.float16
U8 = mybir.dt.uint8
I32 = mybir.dt.int32
AX = mybir.AxisListType.X

P = 128
D = 1024
NC = D // P
B, QL, CTX = 2, 512, 1024
NT = B * QL // P
TPB = QL // P
SL = CTX + QL
NS = SL // P
KV, G, HD = 4, 4, 96
KVD = KV * HD
QG = G * HD
NJ = QG // P
VW = 2 * HD + 1
E, R = 3, 40
NE, TOP = 64, 8
EPS = 1e-5
MAGIC = 1.5 * 2.0 ** 23
MID = 128.0
QMAX = 255.0
WS = 64.0
SCALE = 1.0 / float(HD) ** 0.5
RING = 4
LAG = 3
NPF, NPB = 4, 6
HSLAB = 2 * NC * P
HI, LO = 0, 1


def flamingo(nc, x_d, ctx_d, ctx_t_d, par_d, ident_d, wk_d, wv_d, wq_d, wo_d, wb_d, bb_d, ft_d,
             coef_d, mask_d, enc_d, rw_d, rb_d, eb_d, out_d):
    with ExitStack() as ctx:
        def sb(name, shape, dt):
            return ctx.enter_context(nc.sbuf_tensor(name, shape, dt))

        def sem(name):
            return ctx.enter_context(nc.semaphore(name))

        x_res = sb("x_res", [P, NT * D], F32)
        ln_t = sb("ln_t", [P, NT * HSLAB], F16)
        stage = sb("stage", [P, RING, D], F32)
        region_w = sb("region_w", [P, 4 * NC * KVD], F16)
        region_o = sb("region_o", [P, 6176], F16)
        region_c = sb("region_c", [P, 16384], F16)
        region_q = sb("region_q", [P, 16384], F16)
        region_y = sb("region_y", [P, 2 * D], F32)
        region_s = sb("region_s", [P, 2 * D], F16)
        region_b = sb("region_b", [P, 2 * D], F32)

        def view(region, start, n, dt=F16):
            per = 2 if (dt == F32 and region.dtype == F16) else 1
            v = region[:, start:start + n * per]
            return v.bitcast(F32) if per == 2 else v

        wk = view(region_w, 0, 2 * NC * KVD).rearrange("p (h c n) -> p h c n", h=2, c=NC)
        wv = view(region_w, 2 * NC * KVD, 2 * NC * KVD).rearrange("p (h c n) -> p h c n", h=2, c=NC)
        wq = wk
        wo = view(region_w, 2 * NC * KVD, 2 * NJ * D).rearrange("p (h j n) -> p h j n", h=2, j=NJ)
        k_out = view(region_o, 0, NJ * 2 * QL).rearrange("p (j h s) -> p j h s", j=NJ, h=2)
        v_out = view(region_o, NJ * 2 * QL, KV * 4 * VW).rearrange("p (k t w) -> p k t w", k=KV, t=4)
        enc_f = view(region_o, 0, D, F32)
        enc = view(region_o, 2 * D, 2 * D).rearrange("p (h d) -> p h d", h=2)
        u_t = view(region_o, 4 * D, 2 * D).rearrange("p (h o) -> p h o", h=2)
        ctx_t = view(region_c, 0, 16384).rearrange("p (b c h s) -> p b c h s", b=2, c=NC, h=2)
        w_eff = view(region_c, 0, 16384).rearrange("p (h c n) -> p h c n", h=2, c=NC)
        q_head = view(region_c, 0, 8192).rearrange("p (b g h s) -> p b g h s", b=2, g=G, h=2)
        p_hi = view(region_c, 8192, NPB * QL).rearrange("p (r q) -> p r q", r=NPB)
        p_lo = view(region_c, 8192 + NPB * QL, NPB * QL).rearrange("p (r q) -> p r q", r=NPB)
        neg_max = view(region_c, 8192 + 2 * NPB * QL, 2 * TPB * 98).rearrange("p (b t n) -> p b t n", b=2, t=TPB)
        q2 = region_q[:, :]
        k_head = view(region_q, 0, 4 * SL).rearrange("p (b h s) -> p b h s", b=2, h=2)
        v_head = view(region_q, 4 * SL, 2 * NS * VW).rearrange("p (b s w) -> p b s w", b=2, s=NS)
        q_blk = view(region_q, 10776, NJ * 2 * QL).rearrange("p (j h s) -> p j h s", j=NJ, h=2)
        o_sum = view(region_q, 13848, TPB * HD, F32).rearrange("p (t d) -> p t d", t=TPB)
        o_raw = view(region_q, 14616, TPB * VW, F32).rearrange("p (t w) -> p t w", t=TPB)
        o_tok = view(region_o, 0, 2 * TPB * QG, F32).rearrange("p (b t n) -> p b t n", b=2, t=TPB)
        y_buf = region_y[:, :].rearrange("p (b d) -> p b d", b=2)
        p_f32 = region_y[:, :].rearrange("p (r q) -> p r q", r=NPF)
        q1_buf = region_s[:, :].rearrange("p (b d) -> p b d", b=2)
        bc_buf = region_b[:, :].rearrange("p (b d) -> p b d", b=2)
        w_land = view(region_q, 0, 2 * NC * KVD, F32).rearrange("p (w c n) -> p w c n", w=2, c=NC)
        coef = view(region_q, 4 * NC * KVD, NC * R * E, F32).rearrange("p (n e) -> p n e", e=E)
        mask_words = region_q[:, 15000:15000 + NC * R * E // 2].bitcast(I32)
        mask = region_q[:, 15000:15000 + NC * R * E // 2].bitcast(U8).rearrange("p (n e) -> p n e", e=E)
        y3_buf = region_b[:, 0:D]
        bias_rows = region_b[:, D:2 * D]
        o_t = region_b[:, 0:NJ * QL].bitcast(F16).rearrange("p (j h s) -> p j h s", j=NJ, h=2)

        y_all = view(region_c, 0, NT * D, F32).rearrange("p (t d) -> p t d", t=NT)
        rw = region_s[:, 0:NC * 2 * NE].rearrange("p (c n) -> p c n", c=NC)
        eb_hi = region_s[:, D:2 * D]
        eb_lo = region_b[0:NE, 3 * D // 2:2 * D].bitcast(F16)

        ident = sb("ident", [P, P], F32)
        ident_h = sb("ident_h", [P, P], F16)
        ones_h = sb("ones_h", [P, P], F16)
        par = sb("par", [P, 8], F32)
        tg = sb("tg", [P, 4], F32)
        sc = sb("sc", [P, 16], F32)
        w_sum = sb("w_sum", [P, NC, R], F32)
        bn = sb("bn", [P, 2, 6], F32)
        mv = sb("mv", [P, 2], F32)
        var_c = sb("var_c", [P, 4 * NT], F32)
        nmean = sb("nmean", [P, 4 * NT], F32)
        rstd = sb("rstd", [P, 4 * NT], F32)
        nmr = sb("nmr", [P, 4 * NT], F32)
        mhalf = sb("mhalf", [P, 1], F32)
        row_q = sb("row_q", [P, NT], F32)
        beta = sb("beta", [P, NT], F32)
        pre_max = sb("pre_max", [P, 2, TPB, SL // 512], F32)
        row_max = sb("row_max", [P, TPB], F32)
        den_inv = sb("den_inv", [P, TPB], F32)
        rb = sb("rb", [P, NE], F32)
        logit = sb("logit", [P, NT, NE], F32)
        rest = sb("rest", [P, 2, NE], F32)
        top8 = sb("top8", [P, 2, TOP], F32)
        lmax = sb("lmax", [P, 1], F32)
        nmx = sb("nmx", [P, NT], F32)
        esum = sb("esum", [P, NT], F32)
        einv = sb("einv", [P, 2], F32)
        wsum8 = sb("wsum8", [P, 2], F32)
        mscale = sb("mscale", [P, NT], F32)
        ascale = sb("ascale", [P, NT], F32)
        w_tok = sb("w_tok", [P, 2, 2 * NE], F16)
        w_exp = sb("w_exp", [P, 2, P], F16)
        ps = ctx.enter_context(nc.psum_tensor("ps", [P, 8, 512], F32))

        S1, Z1, S2, Z2 = 4, 5, 6, 7
        RS1, RS2, ALPHA, CC, CR, CK, TGW, D1, D2 = range(9)

        k_dram = nc.dram_tensor("k_scratch", (B, 2, KVD, SL), F16).ap()
        v_dram = nc.dram_tensor("v_scratch", (B, KV, P, NS, VW), F16).ap()

        par_ld, x_ld, id_ld, small_ld, enc_ld, bb_ld, rb_ld = (
            sem(n) for n in ("par_ld", "x_ld", "id_ld", "small_ld", "enc_ld", "bb_ld", "rb_ld"))
        ld = [sem(f"ld{s}") for s in range(RING)]
        w_ld = [[sem(f"{w}_ld{s}") for s in range(RING)] for w in ("wk", "wv")]
        const_ok, half_ok, tanh_ok, scal_step, scal_ok = (sem(n) for n in ("const_ok", "half_ok", "tanh_ok", "scal_step", "scal_ok"))
        wsum_step, wsum_ok = sem("wsum_step"), sem("wsum_ok")
        w_hi, w_split = sem("w_hi"), sem("w_split")
        c_hi, c_split = sem("c_hi"), sem("c_split")
        n_aff, n_clip, n_done = sem("n_aff"), sem("n_clip"), sem("n_done")
        k_ready, k_hi_ok, k_lo_ok = sem("k_ready"), sem("k_hi_ok"), sem("k_lo_ok")
        v_ready, v_hi_ok, v_lo_ok = sem("v_ready"), sem("v_hi_ok"), sem("v_lo_ok")
        kv_stored = sem("kv_stored")
        bn_step, bn_go, ln_var, ln_pow, ln_ok = sem("bn_step"), sem("bn_go"), sem("ln_var"), sem("ln_pow"), sem("ln_ok")
        y1_ok, t1_ok, q1_clip, q1_ok, rowq_ok, beta_ok = (
            sem(n) for n in ("y1_ok", "t1_ok", "q1_clip", "q1_ok", "rowq_ok", "beta_ok"))
        xb_ok, xc_ok = sem("xb_ok"), sem("xc_ok")
        tq_ready, tq_ok, cs_ready, cs_ok = (sem(n) for n in ("tq_ready", "tq_ok", "cs_ready", "cs_ok"))
        f_used, u_hi, u_lo, enc_hi, enc_ok = (sem(n) for n in ("f_used", "u_hi", "u_lo", "enc_hi", "enc_ok"))
        dl_ready, we_sum, we_hi, we_ok = (sem(n) for n in ("dl_ready", "we_sum", "we_hi", "we_ok"))
        bias_ok, xbias_ok = sem("bias_ok"), sem("xbias_ok")
        xa_ready, xa_ok = sem("xa_ready"), sem("xa_ok")
        y2_ok, y3_ok = sem("y2_ok"), sem("y3_ok")
        tl_ready, tl_hi, tl_lo = sem("tl_ready"), sem("tl_hi"), sem("tl_lo")
        ff_ready, ff_ok = sem("ff_ready"), sem("ff_ok")
        k_ld = [sem(f"k_ld{b}") for b in range(B)]
        v_ld = [sem(f"v_ld{b}") for b in range(B)]
        q_ld = [sem(f"q_ld{b}") for b in range(B)]
        sp_ready, sp_hi, sp_free = sem("sp_ready"), sem("sp_hi"), sem("sp_free")
        pre_ready, pre_ok, max_step, nm_ok = sem("pre_ready"), sem("pre_ok"), sem("max_step"), sem("nm_ok")
        row_ready, row_ok = sem("row_ready"), sem("row_ok")
        sc_ready, exp_ok, plo_ok, pv_ok = (sem(n) for n in ("sc_ready", "exp_ok", "plo_ok", "pv_ok"))
        oraw_ok, oraw2_ok, osum_ok, o_ok = sem("oraw_ok"), sem("oraw2_ok"), sem("osum_ok"), sem("o_ok")
        y4_ok, t4_ready, t4_hi, t4_lo = (sem(n) for n in ("y4_ok", "t4_ready", "t4_hi", "t4_lo"))
        lg_ready, lg_step, lg_ok, ex_ok = (sem(n) for n in ("lg_ready", "lg_step", "lg_ok", "ex_ok"))
        top_step, wt_ok, wx_ready, wx_ok, ya_ok, xy_ok, xs_ok, mix_ready, fin_ok = (
            sem(n) for n in ("top_step", "wt_ok", "wx_ready", "wx_ok", "ya_ok", "xy_ok", "xs_ok", "mix_ready", "fin_ok"))
        out_st = sem("out_st")

        def cols(t, start, n):
            return t[:, bass.ds(start, n)]

        def x_tile(i, start=0, n=D):
            return cols(x_res, i * D + start, n)

        def slab(i, h):
            return cols(ln_t, i * HSLAB + h * NC * P, NC * P)

        def batch_slabs(b):
            return cols(ln_t, b * TPB * HSLAB, TPB * HSLAB).rearrange(
                "p (t h c k) -> p t h c k", t=TPB, h=2, c=NC)

        def bank(i, n=512, m=P):
            return ps[0:m, i, 0:n]

        def wide(i, dt=F32):
            if dt == F16:
                return ps[:, i, :].bitcast(F16)
            return ps[:, i:i + 2, :].rearrange("p b n -> p (b n)")

        def split_passes(a, b):
            return ((a(HI), b(HI)), (a(HI), b(LO)), (a(LO), b(HI)))

        CY_B, CY_F, CY_WB, CY_WQ0, CY_E, CY_G = 0, 8, 10, 12, 13, 14
        W_WQ0, W_E, W_G = 2 * RING, 3 * RING, 4 * RING
        EB_CUTS = (0, 384, 704, D)
        POOL_TILES = 6
        LG_STEPS, TOP_STEPS = 2, 4
        LN1, LN2, LN3, LN4 = 0, NT, 2 * NT, 3 * NT

        SLOTS = B * G
        PRE_AT = (2, 2, 1, 2, 1, 2, 1, 1, 0, 0, 0, 0)
        N_PRE = TPB * (SL // 512)
        MAX_STEP, ROW_STEP = 8, 9
        SP_ITER = 2 * NJ + 2 * (NJ + 8)
        SP0 = NJ
        SPQ1, SPT0, SPO0, SPX = 0, NJ, 2 * NJ, 2 * NJ + 8
        END = (("q", 0, 6, 0), ("o", 0, 0, 0), ("o", 1, 1, 0), ("q", 1, 7, 0), ("o", 2, 0, 2), ("q", 2, 6, 1))
        END_LAST = (("o", 0, 6, 0), ("o", 1, 7, 0), ("o", 2, 6, 1))
        Q0_USES = tuple(SPX + n for n, (what, _, _, _) in enumerate(END) if what == "q")
        Q1_TAKE = {(0, 8): 0, (1, 4): 1, (2, 0): 2}
        T0_STEPS = {7: 0, 8: 1, 9: 2}
        WO_STEPS = {5: {1: 0, 4: 1, 7: 2, 10: 3}, 6: {1: 4, 4: 5, 7: 6, 10: 7}}
        WO_SPLIT = {(2, 3): 0, (2, 9): 1, (3, 3): 2, (3, 9): 3}
        WQ_SPLIT = {(5, 3): 0, (5, 9): 1, (6, 3): 2, (6, 9): 3}
        NORM_AT = {9: 0, 11: 1}
        DEV_AT = {6: 0, 8: 1}

        def spare(k):
            return 6 + (SP0 + k) % 2

        def end_bank(w):
            return 7 - w % 2

        def pre_bank(v, k):
            return 2 + (v + k) % 2

        block = ctx.enter_context(nc.Block())

        @block.sync
        def _(sp):
            def ring(s, dst, src, used=None, count=0):
                if used is not None:
                    sp.wait_ge(used, count)
                sp.dma_start(dst, src).then_inc(ld[s], 16)

            def pair(s, n):
                return stage[:, s, 0:2 * n].rearrange("p (c n) -> p c n", c=2)

            def load_ctx_t(t, used=None, count=0, pieces=range(RING)):
                b, half = t // 2, t % 2
                src = ctx_t_d[b].rearrange("(c p) s -> p c s", p=P)
                for s in pieces:
                    ring(s, pair(s, QL), src[:, 2 * s:2 * s + 2, half * QL:(half + 1) * QL], used, count + s)

            def load_ctx(b, part):
                for n in range(part * RING, (part + 1) * RING):
                    used, count = (n_done, NC * b + n - RING + 1) if part else (c_split, RING * (2 * b + 1) + n + 1)
                    ring(n % RING, stage[:, n % RING, :], ctx_d[b, n * P:(n + 1) * P, :], used, count)

            def load_x(b):
                for k in range(TPB):
                    i = TPB * b + k
                    sp.dma_start(x_tile(i), x_d[i * P:(i + 1) * P, :]).then_inc(x_ld, 16)

            def store_kv(t, b, s0):
                sp.wait_ge(k_lo_ok, NJ * (t + 1))
                for h in (HI, LO):
                    dst = k_dram[b, h].rearrange("(j p) s -> p j s", p=P)[:, :, s0:s0 + QL]
                    sp.dma_start(dst, k_out[:, :, h, :]).then_inc(kv_stored, 16)
                sp.wait_ge(v_lo_ok, 4 * (t + 1))
                dst = v_dram[b].rearrange("k p s w -> p k s w")[:, :, s0 // P:s0 // P + 4, :]
                sp.dma_start(dst, v_out[:, :, :, :]).then_inc(kv_stored, 16)

            sp.dma_start(par[:, :], par_d).then_inc(par_ld, 16)
            def load_w(w, w_d, s):
                cs = slice(2 * s, 2 * s + 2)
                sp.dma_start(w_land[:, w, cs, :], w_d[:, cs, :]).then_inc(w_ld[w][s], 16)

            for s in range(RING):
                load_w(0, wk_d, s)
                load_ctx_t(0, pieces=(s,))
            for s in range(RING):
                load_w(1, wv_d, s)
            sp.dma_start(ident[:, :], ident_d).then_inc(id_ld, 16)
            load_x(0)
            load_ctx_t(1, c_split, 1)
            sp.dma_start(coef, coef_d).then_inc(small_ld, 16)
            sp.dma_start(mask_words, mask_d).then_inc(small_ld, 16)
            sp.dma_start(rb[:, :], rb_d).then_inc(rb_ld, 16)
            sp.wait_ge(x_ld, 16 * TPB)
            load_x(1)
            load_ctx(0, 0)
            store_kv(0, 0, 0)
            load_ctx(0, 1)
            load_ctx_t(2, n_done, RING + 1)
            store_kv(1, 0, QL)
            load_ctx_t(3, c_split, 2 * RING + 1)
            load_ctx(1, 0)
            store_kv(2, 1, 0)
            load_ctx(1, 1)
            for n in range(NC):
                if n == RING:
                    store_kv(3, 1, QL)
                    sp.wait_ge(kv_stored, 4 * 48)
                    sp.dma_start(enc_f[0:R, :], enc_d).then_inc(enc_ld, 16)
                used, count = (n_done, NC + RING + n + 1) if n < RING else (f_used, n - RING + 1)
                ring(n % RING, stage[:, n % RING, :], ft_d[:, n, :], used, count)
            for n in range(NC):
                used, count = (f_used, RING + n + 1) if n < RING else (we_ok, n - RING + 1)
                ring(n % RING, stage[:, n % RING, :], wb_d[n * P:(n + 1) * P, :], used, count)
            sp.wait_ge(xc_ok, NT)
            sp.dma_start(bias_rows, bb_d).then_inc(bb_ld, 16)

            def load_wq(g, used, count):
                for s in range(RING):
                    ring(s, pair(s, QG), wq_d[bass.ds(g * P, P), 2 * s:2 * s + 2, :], used, count + s)

            def load_wo(g, used, count):
                for s in range(RING):
                    dst = stage[:, s, 0:NJ * 256].rearrange("p (j n) -> p j n", j=NJ)
                    ring(s, dst, wo_d[bass.ds(g * P, P), :, s * 256:(s + 1) * 256], used, count + s)

            def load_kv(g, b):
                src = k_dram[b, :, bass.ds(g * HD, HD), :].rearrange("h d s -> d h s")
                sp.dma_start(k_head[0:HD, b, :, :], src).then_inc(k_ld[b], 16)
                src = v_dram[b, bass.ds(g, 1), :, :, :].rearrange("k p s w -> (k p) (s w)")
                sp.dma_start(v_head[:, b, :, :].rearrange("p s w -> p (s w)"), src).then_inc(v_ld[b], 16)

            def load_q(uses, b):
                for j in range(NJ):
                    sp.wait_ge(sp_free, uses[j] + 1)
                    row = j * P
                    while row < (j + 1) * P:
                        h, d = row // HD, row % HD
                        n = min(HD - d, (j + 1) * P - row)
                        sp.dma_start(q_head[d:d + n, b, h, :, :], q_blk[row - j * P:row - j * P + n, j, :, :]
                                     ).then_inc(q_ld[b], 16)
                        row += n

            load_wq(0, we_ok, RING + 1)
            store_kv(4, 0, CTX)
            sp.wait_ge(kv_stored, 5 * 48)
            sp.wait_ge(xa_ok, 2 * NT)
            load_kv(0, 0)
            ring(0, stage[:, 0, 0:NC * NE], rw_d, w_split, W_WQ0 + 1)
            for s in range(1, RING):
                c0, c1 = EB_CUTS[s - 1:s + 1]
                ring(s, stage[:, s, 0:c1 - c0], eb_d[:, c0:c1], w_split, W_WQ0 + s + 1)
            load_q(range(NJ), 0)
            store_kv(5, 1, CTX)
            sp.wait_ge(kv_stored, 6 * 48)

            def iteration(g, last):
                sp.wait_ge(pv_ok, NPB + SLOTS * NS * g)
                load_kv(g, 1)
                load_wo(g, w_split, W_G + 2 * RING * g - RING + 1)
                load_q([SP0 + SP_ITER * g + SPQ1 + j for j in range(NJ)], 1)
                if not last:
                    load_wq(g + 1, w_split, W_G + 2 * RING * g + 1)
                    sp.wait_ge(pv_ok, NPB + SLOTS * NS * g + G * NS)
                    load_kv(g + 1, 0)
                    load_q([SP0 + SP_ITER * g + k for k in Q0_USES], 0)

            with sp.Fori(0, KV - 1) as g:
                iteration(g, False)
            iteration(KV - 1, True)

            with sp.Fori(0, NT) as i:
                sp.wait_ge(fin_ok, 2 * i + 2)
                sp.dma_start(out_d[bass.ds(i * P, P), :], x_tile(i)).then_inc(out_st, 16)
            sp.wait_ge(out_st, 16 * NT)

        @block.tensor
        def _(pe):
            def passes(out, pairs, first, last):
                for n, (a, b) in enumerate(pairs):
                    ins = nc.tensor.matmul(out, a, b, start=first and n == 0, stop=last and n == len(pairs) - 1)
                return ins

            def by_tile(out):
                return out.rearrange("p (t k) -> p t k", t=TPB)

            def project_k(t, chunk_wait, x_of, shape=lambda out: out, waits=True):
                if waits:
                    pe.wait_ge(k_lo_ok, NJ * t)
                for c in range(NC):
                    chunk_wait(c)
                    for j in range(NJ):
                        ins = passes(shape(bank(j)), split_passes(lambda h: wk[:, h, c, j * P:(j + 1) * P],
                                                                  lambda h: x_of(c, h)), c == 0, c == NC - 1)
                        if c == NC - 1:
                            ins.then_inc(k_ready, 1)

            def project_v(t, tt, tile_of, between=lambda c: None, waits=True):
                if waits or tt > 1:
                    pe.wait_ge(v_lo_ok, 4 * t + max(0, tt - 1))
                for c in range(NC):
                    ins = passes(bank(3 + tt % 2, KVD), split_passes(lambda h: tile_of(c, h), lambda h: wv[:, h, c, :]),
                                 c == 0, c == NC - 1)
                    if c == NC - 1:
                        ins.then_inc(v_ready, 1)
                    between(c)

            def transpose_q1(i, k):
                pe.wait_ge(const_ok, 2)
                pe.wait_ge(q1_ok, i + 1)
                for c in range(NC):
                    ins = nc.tensor.transpose(wide((5, 7)[k % 2], F16)[:, c * P:(c + 1) * P],
                                              q1_buf[:, k % 2, c * P:(c + 1) * P], ident_h[:, :])
                ins.then_inc(tq_ready, 1)

            pe.sem_inc(pv_ok, NPB)
            with pe.Fori(0, B) as b:
                for half in range(2):
                    t = 2 * b + half

                    def chunk(c):
                        if c % 2 == 0:
                            pe.wait_ge(w_split, c // 2 + 1)
                            pe.wait_ge(c_split, RING * t + c // 2 + 1)

                    project_k(t, chunk, lambda c, h: ctx_t[:, half, c, h, :], waits=half > 0)
                    pe.wait_ge(w_split, 2 * RING)
                    for tt in range(TPB):
                        project_v(t, tt, lambda c, h: ctx_t[:, half, c, h, tt * P:(tt + 1) * P], waits=half > 0)
                    for k in (2 * half, 2 * half + 1):
                        if half > 0:
                            pe.wait_ge(tq_ok, TPB * b + 2)
                        transpose_q1(TPB * b + k, k)
                pe.wait_ge(n_done, NC * (b + 1))
                for half in range(2):
                    if half == 1:
                        pe.wait_ge(tq_ok, TPB * (b + 1))
                    for c in range(NC):
                        ins = nc.tensor.matmul(bank(6 + half), ones_h[:, :],
                                               cols(q2, b * NC * D + c * D + half * 512, 512),
                                               start=c == 0, stop=c == NC - 1)
                    ins.then_inc(cs_ready, 1)
                pe.wait_ge(v_lo_ok, 2 * TPB * (b + 1))

            pe.wait_ge(wsum_ok, 1)
            pe.wait_ge(k_lo_ok, 4 * NJ)
            pe.wait_ge(v_lo_ok, 4 * 4)
            for c in range(NC):
                pe.wait_ge(ld[c % RING], 16 * (CY_F + c // RING + 1))
                for half in range(2):
                    ins = nc.tensor.matmul(bank(2 + half, 512, R), w_sum[:, c, :],
                                           stage[:, c % RING, half * 512:(half + 1) * 512],
                                           start=c == 0, stop=c == NC - 1)
                ins.then_inc(f_used, 1)
            def low_rank(c):
                if c == 0:
                    pe.wait_ge(enc_ok, 1)
                    pe.wait_ge(u_lo, 2)
                    pe.wait_ge(cs_ok, 2 * B)
                    pe.wait_ge(tq_ok, NT)
                if c >= 2:
                    pe.wait_ge(we_sum, 2 * (c - 1))
                for half in range(2):
                    ins = passes(bank((4, 6)[c % 2] + half),
                                 split_passes(lambda h: enc[0:R, h, c * P:(c + 1) * P],
                                              lambda h: u_t[0:R, h, half * 512:(half + 1) * 512]), True, True)
                    ins.then_inc(dl_ready, 1)

            def cross(i):
                if i == 1:
                    pe.wait_ge(u_lo, 2)
                if i >= 2:
                    pe.wait_ge(xa_ok, 2 * (i - 1))
                for half in range(2):
                    for c in range(NC):
                        ins = nc.tensor.matmul(bank(2 * (i % 2) + half), cols(ln_t, i * HSLAB + c * P, P),
                                               cols(q2, (i // TPB * NC + c) * D + half * 512, 512),
                                               start=c == 0, stop=c == NC - 1)
                    ins.then_inc(xa_ready, 1)

            def transpose_y(src, n):
                if not isinstance(n, int) or n > 0:
                    pe.wait_ge(tl_lo, n)
                for c in range(NC):
                    ins = nc.tensor.transpose(wide(6)[:, c * P:(c + 1) * P], src[:, c * P:(c + 1) * P], ident[:, :])
                ins.then_inc(tl_ready, 1)

            def ffn_half(i, half):
                if not isinstance(i, int) or i > 0:
                    pe.wait_ge(ff_ok, 2 * i + half - 1)
                for c in range(NC):
                    ins = passes(bank(4 + half),
                                 split_passes(lambda h: cols(ln_t, i * HSLAB + (h * NC + c) * P, P),
                                              lambda h: w_eff[:, h, c, half * 512:(half + 1) * 512]),
                                 c == 0, c == NC - 1)
                ins.then_inc(ff_ready, 1)

            for i in range(NT // 2):
                cross(i)
                low_rank(2 * i)
                low_rank(2 * i + 1)
            cross(4)
            cross(5)
            pe.wait_ge(we_sum, 2 * NC)
            pe.wait_ge(y2_ok, 1)
            transpose_y(y_buf[:, 0, :], 0)
            cross(6)
            pe.wait_ge(y2_ok, 2)
            transpose_y(y_buf[:, 1, :], 1)
            cross(7)
            pe.wait_ge(we_ok, NC)
            for half in range(2):
                ffn_half(0, half)
            pe.wait_ge(y2_ok, 3)
            transpose_y(y_buf[:, 0, :], 2)
            for half in range(2):
                ffn_half(1, half)

            def ffn_step(i, buf):
                if buf is not None:
                    pe.wait_ge(y2_ok, i + 2)
                    transpose_y(y_buf[:, buf, :], 2 * i - 1)
                ffn_half(i, 0)
                pe.wait_ge(y3_ok, i - 1)
                transpose_y(y3_buf, 2 * i if buf is not None else 2 * i - 1)
                ffn_half(i, 1)

            with pe.Fori(0, 2) as r:
                for k in range(2):
                    ffn_step(2 * r + 2 + k, (k + 1) % 2)
            ffn_step(6, 1)
            ffn_step(7, None)

            def latents(b):
                return lambda c, h: batch_slabs(b)[:, :, h, c, :]

            def latent(i):
                return lambda c, h: slab(i, h)[:, c * P:(c + 1) * P]

            pe.wait_ge(ff_ok, 2 * NT)
            project_k(4, lambda c: None, latents(0), by_tile)
            pe.wait_ge(y3_ok, 7)
            transpose_y(y3_buf, 14)
            for tt in range(TPB):
                project_v(4, tt, latent(tt))
                if tt == 1:
                    pe.wait_ge(y3_ok, 8)
                    transpose_y(y3_buf, 15)
            pe.wait_ge(tl_lo, 2 * NT)
            project_k(5, lambda c: None, latents(1), by_tile)
            for tt in range(2):
                project_v(5, tt, latent(TPB + tt))

            def q_parts(b, blocks=range(NJ)):
                src = ln_t[:, b * TPB * HSLAB:(b + 1) * TPB * HSLAB].rearrange(
                    "p (t h c k) -> p t h c k", t=TPB, h=2, c=NC)
                for j in blocks:
                    for c in range(NC):
                        for n, (hw, hx) in enumerate(((HI, HI), (HI, LO), (LO, HI))):
                            yield j, c, n, wq[:, hw, c, j * P:(j + 1) * P], src[:, :, hx, c, :]

            def q_product(taken, at, part):
                j, c, n, a, x = part
                if c == 0 and n == 0:
                    pe.wait_ge(sp_free, taken)
                ins = nc.tensor.matmul(by_tile(bank(at)), a, x,
                                       start=c == 0 and n == 0, stop=c == NC - 1 and n == 2)
                if c == NC - 1 and n == 2:
                    ins.then_inc(sp_ready, 1)

            def o_transposes(taken, at, b, j):
                pe.wait_ge(sp_free, taken)
                for qt in range(TPB):
                    ins = nc.tensor.transpose(bank(at)[:, qt * P:(qt + 1) * P],
                                              o_tok[:, b, qt, j * P:(j + 1) * P], ident[:, :])
                ins.then_inc(sp_ready, 1)

            def out_product(taken, at, w, between=lambda: None):
                pe.wait_ge(sp_free, taken)
                qt, half = w // 2, w % 2
                for j in range(NJ):
                    ins = passes(bank(at), split_passes(lambda h: o_t[:, j, h, qt * P:(qt + 1) * P],
                                                              lambda h: wo[:, h, j, half * 512:(half + 1) * 512]),
                                 j == 0, j == NJ - 1)
                    if j == NJ - 1:
                        ins.then_inc(sp_ready, 1)
                    between()

            def pre_product(v, s, b, h, k):
                if k < 2 and isinstance(v, int) and v == 0:
                    pass
                elif k == 0:
                    pe.wait_ge(pre_ok, N_PRE * v)
                elif k == 1:
                    pe.wait_ge(row_ok, v)
                else:
                    pe.wait_ge(pre_ok, N_PRE * v + k - 1)
                qt, sb_ = k // 3, k % 3
                nc.tensor.matmul(bank(pre_bank(s, k)), q_head[0:HD, b, h, HI, qt * P:(qt + 1) * P],
                                 k_head[0:HD, b, HI, sb_ * 512:(sb_ + 1) * 512], start=True, stop=True
                                 ).then_inc(pre_ready, 1)

            def row_transpose(v, s):
                pe.wait_ge(nm_ok, v + 1)
                for qt in range(TPB):
                    ins = nc.tensor.matmul(bank(pre_bank(s, N_PRE), 512, HD + 1)[:, qt * P:(qt + 1) * P],
                                           neg_max[:, s % 2, qt, 0:HD + 1], ident_h[:, :], start=True, stop=True)
                ins.then_inc(row_ready, 1)

            def score_block(u, n, b, h, i):
                if i == 0:
                    pe.wait_ge(row_ok, u + 1)
                pe.wait_ge(exp_ok, n + 1)
                ks = slice(i * P, (i + 1) * P)
                out = bank(i % 2)
                nc.tensor.matmul(out, k_head[0:HD + 1, b, HI, ks], q_head[0:HD + 1, b, h, HI, :], start=True, stop=False)
                nc.tensor.matmul(out, k_head[0:HD, b, HI, ks], q_head[0:HD, b, h, LO, :], start=False, stop=False)
                nc.tensor.matmul(out, k_head[0:HD, b, LO, ks], q_head[0:HD, b, h, HI, :], start=False, stop=True
                                 ).then_inc(sc_ready, 1)

            def pv_block(g, u, n, b, i):
                if i == 0:
                    pe.wait_ge(v_ld[b], 16 * (g + 1))
                pe.wait_ge(plo_ok, NPF + n + 1)
                for qt in range(TPB):
                    if i == 0 and qt % 2 == 0:
                        pe.wait_ge((oraw_ok, oraw2_ok)[qt // 2], u + 1)
                    tok = slice(qt * P, (qt + 1) * P)
                    out = bank(4 + qt // 2)[:, (qt % 2) * VW:(qt % 2 + 1) * VW]
                    nc.tensor.matmul(out, p_hi[:, i % NPB, tok], v_head[:, b, i, :],
                                     start=i == 0 and qt % 2 == 0, stop=False, skip_group_check=True)
                    ins = nc.tensor.matmul(out[:, 0:HD + 1], p_lo[:, i % NPB, tok], v_head[:, b, i, 0:HD + 1],
                                           start=False, stop=i == NS - 1, skip_group_check=True)
                ins.then_inc(pv_ok, 1)

            pe.wait_ge(w_split, W_WQ0 + RING)
            for part in q_parts(0):
                j, c, n, a, x = part
                if j == 2 and c == 0 and n == 0:
                    pe.wait_ge(sp_free, 1)
                ins = nc.tensor.matmul(by_tile(bank(6 + j % 2)), a, x, start=c == 0 and n == 0, stop=c == NC - 1 and n == 2)
                if c == NC - 1 and n == 2:
                    ins.then_inc(sp_ready, 1)

            def first_maxima(c):
                if c == 0:
                    pe.wait_ge(k_lo_ok, 6 * NJ)
                    pe.wait_ge(v_lo_ok, 6 * 4 - 1)
                    pe.wait_ge(k_ld[0], 16)
                    pe.wait_ge(q_ld[0], 16 * 6)
                for k in range(N_PRE * c // NC, N_PRE * (c + 1) // NC):
                    pre_product(0, 0, 0, 0, k)

            project_v(5, 2, latent(TPB + 2))
            project_v(5, 3, latent(TPB + 3), first_maxima)
            row_transpose(0, 0)
            pe.wait_ge(v_lo_ok, 6 * 4)

            def expert_transposes(i):
                pe.wait_ge(y4_ok, i + 1)
                if i > 1:
                    pe.wait_ge(t4_lo, i - 1)
                for c in range(NC):
                    ins = nc.tensor.transpose(wide(2 * (i % 2))[:, c * P:(c + 1) * P],
                                              y_all[:, i, c * P:(c + 1) * P], ident[:, :])
                ins.then_inc(t4_ready, 1)

            def router(i):
                pe.wait_ge(t4_lo, i + 1)
                if i > 0:
                    pe.wait_ge(lg_step, LG_STEPS * i - 1)
                for c in range(NC):
                    ins = passes(bank(4, NE), split_passes(lambda h: slab(i, h)[:, c * P:(c + 1) * P],
                                                           lambda h: rw[:, c, h * NE:(h + 1) * NE]), c == 0, c == NC - 1)
                ins.then_inc(lg_ready, 1)

            def iteration(g, last):
                base = SP0 + SP_ITER * g
                u0, n0 = SLOTS * g, SLOTS * NS * g
                queries = list(q_parts(1))
                for s in range(SLOTS):
                    b, h = s // G, s % G
                    nb, nh = (s + 1) // G, (s + 1) % G
                    k = 0
                    if s == G - 1:
                        pe.wait_ge(k_ld[1], 16 * (g + 1))
                        pe.wait_ge(q_ld[1], 16 * 6 * (g + 1))
                    if s == 5:
                        pe.wait_ge(w_split, W_G + 2 * RING * g + RING)
                    for i in range(NS):
                        score_block(u0 + s, n0 + NS * s + i, b, h, i)
                        if s < SLOTS - 1:
                            for _ in range(PRE_AT[i]):
                                pre_product(u0 + s + 1, s + 1, nb, nh, k)
                                k += 1
                            if i == ROW_STEP:
                                row_transpose(u0 + s + 1, s + 1)
                        if i >= LAG:
                            pv_block(g, u0 + s, n0 + NS * s + i - LAG, b, i - LAG)
                        elif s > 0:
                            pv_block(g, u0 + s - 1, n0 + NS * s + i - LAG, (s - 1) // G, NS + i - LAG)
                        for _ in range(3):
                            if s < 2:
                                k1 = SPQ1 + queries[0][0]
                                q_product(base + k1 - 1, spare(k1), queries.pop(0))
                        if s == G and i in T0_STEPS:
                            if T0_STEPS[i] == 0:
                                pe.wait_ge(o_ok, u0 + G + 1)
                            k1 = SPT0 + T0_STEPS[i]
                            o_transposes(base + k1 - 1, spare(k1), 0, T0_STEPS[i])
                        if s in WO_STEPS and i in WO_STEPS[s]:
                            w = WO_STEPS[s][i]
                            out_product(base + SPO0 + max(0, w - 1), spare(SPO0 + w), w)
                for i in range(NS - LAG, NS):
                    pv_block(g, u0 + SLOTS - 1, n0 + NS * (SLOTS - 1) + i, 1, i)
                m = 0
                first = base + SPX
                if not last:
                    pe.wait_ge(w_split, W_G + 2 * RING * (g + 1))
                pe.wait_ge(exp_ok, 2 + SLOTS * NS * (g + 1))
                if last:
                    expert_transposes(0)
                for what, j, at, taken in END_LAST if last else END:
                    if what == "q":
                        for part in q_parts(0, (j,)):
                            q_product(first + taken, at, part)
                    else:
                        if j == 0:
                            pe.wait_ge(o_ok, u0 + SLOTS + 1)
                        o_transposes(first + taken, at, 1, j)

                def next_maxima():
                    nonlocal m
                    if m == 0:
                        pe.wait_ge(k_ld[0], 16 * (g + 2))
                        pe.wait_ge(q_ld[0], 16 * 6 * (g + 2))
                    pre_product(u0 + SLOTS, 0, 0, 0, m)
                    m += 1

                if last:
                    expert_transposes(1)
                ends = len(END_LAST if last else END)
                for w in range(8):
                    taken = first + (ends + w - 1 if w > 1 else ends if w or last else ends - 1)
                    if not last and 2 <= w <= 5:
                        out_product(taken, end_bank(w), w, next_maxima)
                    else:
                        out_product(taken, end_bank(w), w)
                    if not last and w == 6:
                        row_transpose(u0 + SLOTS, 0)
                    if last and w in (1, 3, 5, 7):
                        if w == 1:
                            pe.wait_ge(oraw_ok, SLOTS * KV + 1)
                            pe.wait_ge(oraw2_ok, SLOTS * KV + 1)
                        router(w // 2)
                    if last and w in (1, 3, 6):
                        expert_transposes((w + 1) // 2 + 1)

            with pe.Fori(0, KV - 1) as g:
                iteration(g, False)
            iteration(KV - 1, True)

            sp_end = SP0 + SP_ITER * KV - NJ
            pe.wait_ge(sp_free, sp_end)

            def expert_pair(r):
                pe.wait_ge(wt_ok, r + 1)
                if r > 0:
                    pe.wait_ge(wx_ok, r)
                for k in range(2):
                    ins = nc.tensor.transpose(wide(5, F16)[:, k * P:(k + 1) * P], w_tok[:, k, :], ident_h[:, :])
                ins.then_inc(wx_ready, 1)

            def expert_mix(i):
                pe.wait_ge(wx_ok, i // 2 + 1)
                for half in range(2):
                    if i > 0:
                        pe.wait_ge(fin_ok, 2 * i + half - 1)
                    hs = slice(half * 512, (half + 1) * 512)
                    nc.tensor.matmul(bank(6 + half), w_exp[:, i % 2, :], eb_hi[:, hs], start=True, stop=False)
                    nc.tensor.matmul(bank(6 + half), w_exp[0:NE, i % 2, :], eb_lo[:, hs], start=False, stop=True
                                     ).then_inc(mix_ready, 1)

            expert_pair(0)
            expert_transposes(5)
            router(4)
            expert_mix(0)
            expert_transposes(6)
            router(5)
            expert_mix(1)
            expert_pair(1)
            expert_transposes(7)
            router(6)
            expert_mix(2)
            expert_mix(3)
            router(7)
            expert_pair(2)
            expert_mix(4)
            expert_mix(5)
            expert_pair(3)
            expert_mix(6)
            expert_mix(7)

        @block.scalar
        def _(act):
            def copy(out, in_):
                return nc.scalar.activation(out, in_, ACT.Copy)

            def affine(out, in_, scale, bias):
                return nc.scalar.activation(out, in_, ACT.Identity, scale=scale, bias=bias)

            def keys(t):
                if t > 0:
                    act.wait_ge(kv_stored, 48 * t)
                for j in range(NJ):
                    act.wait_ge(k_ready, NJ * t + j + 1)
                    copy(k_out[:, j, HI, :], bank(j)).then_inc(k_hi_ok, 1)

            def values(t, tt):
                act.wait_ge(v_ready, 4 * t + tt + 1)
                copy(v_out[:, :, tt, 0:HD], bank(3 + tt % 2, KVD).rearrange("p (k d) -> p k d", k=KV)
                     ).then_inc(v_hi_ok, 1)

            def normalise(out, i, ln):
                act.wait_ge(ln_ok, ln + i + 1)
                return affine(out, x_tile(i), cols(rstd, ln + i, 1), cols(nmr, ln + i, 1))

            act.sem_inc(exp_ok, 2)
            act.sem_inc(oraw_ok, 1)
            act.wait_ge(par_ld, 16)
            nc.scalar.activation(tg[:, :], par[:, 0:4], ACT.Tanh).then_inc(tanh_ok, 1)
            def split_kv_weights(w, s):
                act.wait_ge(w_ld[w][s], 16)
                cs = slice(2 * s, 2 * s + 2)
                copy((wk, wv)[w][:, HI, cs, :], w_land[:, w, cs, :]).then_inc(w_hi, 1)

            def split_ctx(t, pieces=range(RING)):
                if t >= 2:
                    act.wait_ge(v_ready, 4 * (t - 1))
                for s in pieces:
                    act.wait_ge(ld[s], 16 * (CY_B + 4 * (t // 2) + t % 2 + 1))
                    copy(ctx_t[:, t % 2, 2 * s:2 * s + 2, HI, :],
                         stage[:, s, :].rearrange("p (c n) -> p c n", c=2)).then_inc(c_hi, 1)

            def scale_ctx(b, n):
                s = n % RING
                act.wait_ge(ld[s], 16 * (CY_B + 4 * b + 2 + n // RING + 1))
                affine(stage[:, s, :], stage[:, s, :], sc[:, RS2:RS2 + 1], par[:, Z2:Z2 + 1]).then_inc(n_aff, 1)

            def scale_x(i):
                if i >= 2:
                    act.wait_ge(q1_ok, i - 1)
                y = y_buf[:, i % 2, :]
                normalise(y, i, LN1).then_inc(y1_ok, 1)
                act.wait_ge(y1_ok, i + 1)
                affine(y, y, sc[:, RS1:RS1 + 1], par[:, Z1:Z1 + 1]).then_inc(t1_ok, 1)

            def add_beta(i):
                act.wait_ge(beta_ok, i + 1)
                nc.scalar.activation(x_tile(i), x_tile(i), ACT.Identity, bias=cols(beta, i, 1)).then_inc(xb_ok, 1)

            def take_q1(i):
                act.wait_ge(tq_ready, i + 1)
                copy(slab(i, HI), wide((5, 7)[i % 2], F16)).then_inc(tq_ok, 1)

            for s in range(RING):
                split_kv_weights(0, s)
                split_ctx(0, (s,))
            for s in range(RING):
                split_kv_weights(1, s)
            act.wait_ge(scal_ok, 1)
            act.wait_ge(id_ld, 16)
            copy(ident_h[:, :], ident[:, :]).then_inc(const_ok, 1)
            for b in range(B):
                t, i0 = 2 * b, TPB * b
                if b > 0:
                    scale_x(i0)
                    scale_x(i0 + 1)
                keys(t)
                values(t, 0)
                if b == 0:
                    scale_x(i0)
                    scale_x(i0 + 1)
                values(t, 1)
                split_ctx(t + 1, (0, 1))
                values(t, 2)
                split_ctx(t + 1, (2, 3))
                values(t, 3)
                take_q1(i0)
                take_q1(i0 + 1)
                for n in range(4):
                    scale_ctx(b, n)
                scale_x(i0 + 2)
                scale_x(i0 + 3)
                keys(t + 1)
                for tt in range(TPB):
                    values(t + 1, tt)
                    if tt < 2:
                        scale_ctx(b, 4 + 2 * tt)
                        scale_ctx(b, 5 + 2 * tt)
                    add_beta(i0 + tt)
                if b + 1 < B:
                    split_ctx(t + 2, (0,))
                take_q1(i0 + 2)
                take_q1(i0 + 3)
                if b + 1 < B:
                    split_ctx(t + 2, range(1, RING))
                for half in range(2):
                    act.wait_ge(cs_ready, 2 * b + half + 1)
                    nc.scalar.activation(cols(region_b, b * D + half * 512, 512), bank(6 + half), ACT.Copy,
                                         scale=sc[:, CC:CC + 1]).then_inc(cs_ok, 1)

            act.wait_ge(enc_ld, 16)
            copy(enc[0:R, HI, :], enc_f[0:R, :]).then_inc(enc_hi, 1)
            act.wait_ge(f_used, NC)
            for half in range(2):
                copy(u_t[0:R, HI, half * 512:(half + 1) * 512], bank(2 + half, 512, R)).then_inc(u_hi, 1)
            for c in range(NC):
                act.wait_ge(we_sum, 2 * (c + 1))
                copy(w_eff[:, HI, c, :], stage[:, c % RING, :]).then_inc(we_hi, 1)
            act.wait_ge(bb_ld, 16)
            nc.scalar.activation(bias_rows, bias_rows, ACT.Copy, scale=tg[:, 2:3]).then_inc(bias_ok, 1)

            def take_high(i, n):
                act.wait_ge(tl_ready, n + 1)
                copy(slab(i, HI), wide(6)).then_inc(tl_hi, 1)

            def norm2(i, buf, before):
                if before is not None:
                    act.wait_ge(tl_ready, before)
                normalise(buf, i, LN2).then_inc(y2_ok, 1)

            def norm3(i, before):
                if before is not None:
                    act.wait_ge(tl_ready, before)
                normalise(y3_buf, i, LN3).then_inc(y3_ok, 1)

            norm2(0, y_buf[:, 0, :], None)
            norm2(1, y_buf[:, 1, :], None)
            take_high(0, 0)
            norm2(2, y_buf[:, 0, :], 1)
            take_high(1, 1)
            norm2(3, y_buf[:, 1, :], 2)
            take_high(2, 2)
            act.wait_ge(xc_ok, NT)

            def ffn_step(i, par):
                if par is not None:
                    take_high(i + 1, 2 * i - 1)
                    if not isinstance(i, int):
                        norm2(i + 2, y_buf[:, 1 - par, :], 2 * i - 1)
                norm3(i - 2, 2 * i - 1)
                take_high(i - 2, 2 * i if par is not None else 2 * i - 1)

            with act.Fori(0, 2) as r:
                for k in range(2):
                    ffn_step(2 * r + 2 + k, (k + 1) % 2)
            ffn_step(6, 1)
            ffn_step(7, None)
            norm3(6, 14)
            keys(4)
            take_high(6, 14)
            values(4, 0)
            norm3(7, 15)
            values(4, 1)
            take_high(7, 15)
            values(4, 2)
            values(4, 3)
            keys(5)

            def wq_hi(cycle, s):
                act.wait_ge(ld[s], 16 * (cycle + 1))
                copy(wq[:, HI, 2 * s:2 * s + 2, :], stage[:, s, 0:2 * QG].rearrange("p (c n) -> p c n", c=2)
                     ).then_inc(w_hi, 1)

            def wo_hi(cycle, s):
                act.wait_ge(ld[s], 16 * (cycle + 1))
                copy(wo[:, HI, :, s * 256:(s + 1) * 256], stage[:, s, 0:NJ * 256].rearrange("p (j n) -> p j n", j=NJ)
                     ).then_inc(w_hi, 1)

            def take_q(first, at, j):
                act.wait_ge(sp_ready, first + 1)
                copy(q_blk[:, j, HI, :], bank(at)).then_inc(sp_hi, 1)

            def take_o(first, at, j):
                act.wait_ge(sp_ready, first + 1)
                copy(o_t[:, j, HI, :], bank(at)).then_inc(sp_hi, 1)

            def take_row(v, s, b, h):
                act.wait_ge(row_ready, v + 1)
                copy(q_head[HD:HD + 1, b, h, HI, :], ps[HD:HD + 1, pre_bank(s, N_PRE), :]).then_inc(row_ok, 1)

            def take_sums(u):
                act.wait_ge(pv_ok, NPB + NS * (u + 1))
                act.wait_ge(o_ok, u + 1)
                copy(o_raw[:, 0:2, :].rearrange("p t w -> p (t w)"), bank(4, 2 * VW)).then_inc(oraw_ok, 1)

            act.wait_ge(k_ready, 6 * NJ)
            for s in range(RING):
                wq_hi(CY_WQ0, s)
            values(5, 0)
            values(5, 1)
            for j in range(NJ):
                act.wait_ge(sp_ready, j + 1)
                copy(q_blk[:, j, HI, :], bank(6 + j % 2)).then_inc(sp_hi, 1)
            values(5, 2)
            values(5, 3)
            act.wait_ge(ld[0], 16 * (CY_E + 1))
            copy(rw[:, :, 0:NE], stage[:, 0, 0:NC * NE].rearrange("p (c n) -> p c n", c=NC)).then_inc(w_hi, 1)
            for s in range(1, RING):
                c0, c1 = EB_CUTS[s - 1:s + 1]
                act.wait_ge(ld[s], 16 * (CY_E + 1))
                copy(eb_hi[:, c0:c1], stage[:, s, 0:c1 - c0]).then_inc(w_hi, 1)
            take_row(0, 0, 0, 0)

            def expert_norm(i):
                normalise(y_all[:, i, :], i, LN4).then_inc(y4_ok, 1)

            def expert_high(i):
                act.wait_ge(t4_ready, i + 1)
                copy(slab(i, HI), wide(2 * (i % 2))).then_inc(t4_hi, 1)

            def expert_exp(i):
                act.wait_ge(lg_ok, i + 1)
                nc.scalar.activation(logit[:, i, :], logit[:, i, :], ACT.Exp, bias=nmx[:, i:i + 1],
                                     accum_out=esum[:, i:i + 1]).then_inc(ex_ok, 1)

            def iteration(g, last):
                base = SP0 + SP_ITER * g
                u0, n0 = SLOTS * g, SLOTS * NS * g
                for s in range(SLOTS):
                    for i in range(NS):
                        n = n0 + NS * s + i
                        if s > 0 and i == LAG:
                            take_sums(u0 + s - 1)
                        if s < SLOTS - 1 and i == ROW_STEP + 1:
                            take_row(u0 + s + 1, s + 1, (s + 1) // G, (s + 1) % G)
                        act.wait_ge(sc_ready, n + 1)
                        act.wait_ge(plo_ok, n + 1)
                        nc.scalar.activation(p_f32[:, i % NPF, :], bank(i % 2), ACT.Exp, scale=SCALE)
                        act.wait_ge(pv_ok, n + 1)
                        nc.scalar.activation(p_hi[:, i % NPB, :], bank(i % 2), ACT.Exp, scale=SCALE).then_inc(exp_ok, 1)
                        if (s, i) in Q1_TAKE:
                            j = Q1_TAKE[s, i]
                            take_q(base + SPQ1 + j, spare(SPQ1 + j), j)
                        if s == G and i - 1 in T0_STEPS:
                            j = T0_STEPS[i - 1]
                            take_o(base + SPT0 + j, spare(SPT0 + j), j)
                        if (s, i) in WO_SPLIT:
                            wo_hi(CY_G + 2 * g, WO_SPLIT[s, i])
                        if (s, i) in WQ_SPLIT and not last:
                            wq_hi(CY_G + 1 + 2 * g, WQ_SPLIT[s, i])
                        if last and s == SLOTS - 1 and i in NORM_AT:
                            expert_norm(NORM_AT[i])
                take_sums(u0 + SLOTS - 1)
                if last:
                    expert_high(0)
                for k, (what, j, at, _) in enumerate(END_LAST if last else END, SPX):
                    (take_q if what == "q" else take_o)(base + k, at, j)
                if not last:
                    take_row(u0 + SLOTS, 0, 0, 0)

            with act.Fori(0, KV - 1) as g:
                iteration(g, False)
            iteration(KV - 1, True)

            def expert_weights(r):
                act.wait_ge(wx_ready, r + 1)
                if r > 0:
                    act.wait_ge(mix_ready, 4 * r)
                copy(w_exp[:, :, :].rearrange("p k n -> p (k n)"), wide(5, F16)[:, 0:2 * P]).then_inc(wx_ok, 1)

            def expert_scale(i):
                nc.scalar.activation(y_all[:, i, :], y_all[:, i, :], ACT.Copy, scale=ascale[:, i:i + 1]
                                     ).then_inc(ya_ok, 1)

            expert_high(1)
            expert_norm(2)
            expert_norm(3)
            expert_exp(0)
            expert_high(2)
            expert_norm(4)
            expert_exp(1)
            expert_high(3)
            expert_norm(5)
            expert_exp(2)
            expert_high(4)
            expert_norm(6)
            expert_exp(3)
            expert_weights(0)
            expert_high(5)
            expert_scale(0)
            expert_scale(1)
            expert_norm(7)
            expert_exp(4)
            expert_high(6)
            expert_exp(5)
            expert_weights(1)
            expert_high(7)
            expert_scale(2)
            expert_scale(3)
            expert_exp(6)
            expert_exp(7)
            expert_weights(2)
            expert_scale(4)
            expert_scale(5)
            expert_weights(3)

        @block.vector
        def _(dve):
            def minus(out, a, b):
                return nc.vector.tensor_tensor(out, a, b, ALU.subtract)

            def stats(i, ln):
                n = ln + i
                dve.sem_inc(bn_go, 1)
                for half in range(2):
                    ins = nc.vector.bn_stats(bn[:, half, :], x_tile(i, half * 512, 512))
                ins.then_inc(bn_step, 1)
                dve.wait_ge(bn_step, 2 * n + 1)
                dve.sem_inc(bn_go, 1)
                nc.vector.bn_aggr(mv[:, :], bn[:, :, :]).then_inc(bn_step, 1)
                dve.wait_ge(bn_step, 2 * n + 2)
                nc.vector.tensor_scalar(cols(nmean, n, 1), mv[:, 0:1], -1.0, None, ALU.mult)
                nc.vector.tensor_scalar(cols(var_c, n, 1), mv[:, 1:2], EPS, None, ALU.add).then_inc(ln_var, 1)

            def keys(t):
                for j in range(NJ):
                    dve.wait_ge(k_hi_ok, NJ * t + j + 1)
                    minus(k_out[:, j, LO, :], bank(j), k_out[:, j, HI, :]).then_inc(k_lo_ok, 1)

            def values(t, tt):
                dve.wait_ge(v_hi_ok, 4 * t + tt + 1)
                minus(v_out[:, :, tt, HD + 1:VW], bank(3 + tt % 2, KVD).rearrange("p (k d) -> p k d", k=KV),
                      v_out[:, :, tt, 0:HD]).then_inc(v_lo_ok, 1)

            def col(i):
                return sc[:, i:i + 1]

            def scalar(i, out, in_, s1, s2, op0, op1=ALU.bypass):
                nc.vector.tensor_scalar(col(out), in_, s1, s2, op0, op1).then_inc(scal_step, 1)
                dve.wait_ge(scal_step, i + 1)

            dve.sem_inc(oraw2_ok, 1)
            dve.sem_inc(o_ok, 1)
            nc.vector.memset(v_out[:, :, :, HD:HD + 1], 1.0)
            nc.vector.memset(ones_h[:, :], 1.0).then_inc(const_ok, 1)
            dve.wait_ge(par_ld, 16)
            dve.wait_ge(tanh_ok, 1)
            nc.vector.reciprocal(col(RS1), par[:, S1:S1 + 1])
            nc.vector.reciprocal(col(RS2), par[:, S2:S2 + 1])
            scalar(0, ALPHA, tg[:, 0:1], par[:, S1:S1 + 1], par[:, S2:S2 + 1], ALU.mult, ALU.mult)
            scalar(1, D1, par[:, Z1:Z1 + 1], -1.0, MID, ALU.mult, ALU.add)
            scalar(2, D2, par[:, Z2:Z2 + 1], -1.0, MID, ALU.mult, ALU.add)
            scalar(3, CC, col(D1), col(ALPHA), None, ALU.mult)
            scalar(4, CR, col(D2), col(ALPHA), None, ALU.mult)
            scalar(5, CK, col(CR), col(D1), float(D), ALU.mult, ALU.mult)
            nc.vector.tensor_scalar(col(TGW), tg[:, 2:3], 1.0 / WS, None, ALU.mult).then_inc(scal_ok, 1)
            def split_kv_weights(w):
                for s in range(RING):
                    cs, k = slice(2 * s, 2 * s + 2), (wk, wv)[w]
                    dve.wait_ge(w_hi, RING * w + s + 1)
                    minus(k[:, LO, cs, :], w_land[:, w, cs, :], k[:, HI, cs, :]).then_inc(w_split, 1)

            def quant_ctx(b, n):
                s = n % RING
                dve.wait_ge(n_aff, NC * b + n + 1)
                nc.vector.tensor_scalar(stage[:, s, :], stage[:, s, :], 0.0, QMAX, ALU.max, ALU.min
                                        ).then_inc(n_clip, 1)
                dve.wait_ge(n_clip, NC * b + n + 1)
                nc.vector.tensor_scalar(cols(q2, (NC * b + n) * D, D), stage[:, s, :], MAGIC, MAGIC + MID,
                                        ALU.add, ALU.subtract).then_inc(n_done, 1)

            def quant_x(i):
                y, q = y_buf[:, i % 2, :], q1_buf[:, i % 2, :]
                dve.wait_ge(t1_ok, i + 1)
                nc.vector.tensor_scalar(y, y, 0.0, QMAX, ALU.max, ALU.min).then_inc(q1_clip, 1)
                dve.wait_ge(q1_clip, i + 1)
                if i >= 2:
                    dve.wait_ge(tq_ready, i - 1)
                nc.vector.tensor_scalar(q, y, MAGIC, MAGIC + MID, ALU.add, ALU.subtract).then_inc(q1_ok, 1)
                dve.wait_ge(q1_ok, i + 1)
                nc.vector.reduce_sum(cols(row_q, i, 1), q, axis=AX).then_inc(rowq_ok, 1)
                dve.wait_ge(rowq_ok, i + 1)
                nc.vector.tensor_scalar(cols(beta, i, 1), cols(row_q, i, 1), col(CR), col(CK), ALU.mult, ALU.add
                                        ).then_inc(beta_ok, 1)

            for w in range(2):
                split_kv_weights(w)
            dve.wait_ge(scal_ok, 1)
            for b in range(B):
                t, i0 = 2 * b, TPB * b
                dve.wait_ge(x_ld, 16 * TPB * (b + 1))
                for k in range(TPB):
                    stats(i0 + k, LN1)
                if b > 0:
                    quant_x(i0)
                    quant_x(i0 + 1)
                keys(t)
                values(t, 0)
                if b == 0:
                    quant_x(i0)
                    quant_x(i0 + 1)
                for tt in range(1, TPB):
                    values(t, tt)
                if b == 0:
                    dve.wait_ge(small_ld, 32)
                    nc.vector.tensor_tensor(coef, coef, mask, ALU.mult).then_inc(wsum_step, 1)
                    dve.wait_ge(wsum_step, 1)
                    nc.vector.reduce_sum(w_sum[:, :, :].rearrange("p c r -> p (c r)"), coef, axis=AX
                                         ).then_inc(wsum_ok, 1)
                for n in range(4):
                    quant_ctx(b, n)
                quant_x(i0 + 2)
                quant_x(i0 + 3)
                keys(t + 1)
                for tt in range(TPB):
                    values(t + 1, tt)
                    if tt < 2:
                        quant_ctx(b, 4 + 2 * tt)
                        quant_ctx(b, 5 + 2 * tt)

            dve.wait_ge(enc_hi, 1)
            minus(enc[0:R, LO, :], enc_f[0:R, :], enc[0:R, HI, :]).then_inc(enc_ok, 1)
            for half in range(2):
                hs = slice(half * 512, (half + 1) * 512)
                dve.wait_ge(u_hi, half + 1)
                minus(u_t[0:R, LO, hs], bank(2 + half, 512, R), u_t[0:R, HI, hs]).then_inc(u_lo, 1)

            def add_low_rank(c):
                s = c % RING
                dve.wait_ge(ld[s], 16 * (CY_WB + c // RING + 1))
                for half in range(2):
                    part = stage[:, s, half * 512:(half + 1) * 512]
                    dve.wait_ge(dl_ready, 2 * c + half + 1)
                    nc.vector.scalar_tensor_tensor(part, part, WS, bank((4, 6)[c % 2] + half), ALU.mult, ALU.add
                                                   ).then_inc(we_sum, 1)

            def add_cross(i):
                dve.wait_ge(xc_ok, i + 1)
                for half in range(2):
                    xh = x_tile(i, half * 512, 512)
                    dve.wait_ge(xa_ready, 2 * i + half + 1)
                    nc.vector.scalar_tensor_tensor(xh, bank(2 * (i % 2) + half), col(ALPHA), xh, ALU.mult, ALU.add
                                                   ).then_inc(xa_ok, 1)
                dve.wait_ge(xa_ok, 2 * i + 2)
                stats(i, LN2)

            def take_low(i, n):
                dve.wait_ge(tl_hi, n + 1)
                minus(slab(i, LO), wide(6), slab(i, HI)).then_inc(tl_lo, 1)

            for i in range(NT // 2):
                add_cross(i)
                add_low_rank(2 * i)
                add_low_rank(2 * i + 1)
            nc.vector.memset(v_out[:, :, :, HD:HD + 1], 1.0)
            add_cross(4)
            add_cross(5)
            take_low(0, 0)
            add_cross(6)
            take_low(1, 1)
            add_cross(7)

            def add_ffn(i, half):
                if half == 0:
                    dve.wait_ge(xbias_ok, i + 1)
                xh = x_tile(i, half * 512, 512)
                dve.wait_ge(ff_ready, 2 * i + half + 1)
                nc.vector.scalar_tensor_tensor(xh, bank(4 + half), col(TGW), xh, ALU.mult, ALU.add
                                               ).then_inc(ff_ok, 1)
                if half == 1:
                    dve.wait_ge(ff_ok, 2 * i + 2)
                    stats(i, LN3)

            add_ffn(0, 0)
            add_ffn(0, 1)
            take_low(2, 2)
            add_ffn(1, 0)
            add_ffn(1, 1)

            def ffn_step(i, ahead):
                if ahead:
                    take_low(i + 1, 2 * i - 1)
                add_ffn(i, 0)
                take_low(i - 2, 2 * i if ahead else 2 * i - 1)
                add_ffn(i, 1)

            with dve.Fori(0, 2) as r:
                for k in range(2):
                    ffn_step(2 * r + 2 + k, True)
            ffn_step(6, True)
            ffn_step(7, False)
            nc.vector.memset(neg_max[:, :, :, :], 0.0)
            nc.vector.memset(k_head[HD:HD + 1, :, HI, :], 1.0)
            keys(4)
            take_low(6, 14)
            values(4, 0)
            values(4, 1)
            take_low(7, 15)
            values(4, 2)
            values(4, 3)
            keys(5)

            def split_wq(n, s):
                dve.wait_ge(w_hi, n + 1)
                minus(wq[:, LO, 2 * s:2 * s + 2, :], stage[:, s, 0:2 * QG].rearrange("p (c n) -> p c n", c=2),
                      wq[:, HI, 2 * s:2 * s + 2, :]).then_inc(w_split, 1)

            def split_wo(n, s):
                dve.wait_ge(w_hi, n + 1)
                cs = slice(s * 256, (s + 1) * 256)
                minus(wo[:, LO, :, cs], stage[:, s, 0:NJ * 256].rearrange("p (j n) -> p j n", j=NJ), wo[:, HI, :, cs]
                      ).then_inc(w_split, 1)

            def take_low_of(dst, n, at, j):
                dve.wait_ge(sp_hi, n + 1)
                minus(dst[:, j, LO, :], bank(at), dst[:, j, HI, :]).then_inc(sp_free, 1)

            def add_out(first, at, b, w):
                xh = x_tile(TPB * b + w // 2, (w % 2) * 512, 512)
                dve.wait_ge(sp_ready, first + 1)
                nc.vector.scalar_tensor_tensor(xh, bank(at), tg[:, 1:2], xh, ALU.mult, ALU.add
                                               ).then_inc(sp_free, 1)

            def reduce_max(v, s, k):
                dve.wait_ge(pre_ready, N_PRE * v + k + 1)
                nc.vector.reduce_max(pre_max[:, s % 2, k // 3, k % 3:k % 3 + 1], bank(pre_bank(s, k)), axis=AX
                                     ).then_inc(pre_ok, 1)

            def final_max(v, s):
                dve.wait_ge(pre_ok, N_PRE * (v + 1))
                nc.vector.reduce_max(row_max[:, :], pre_max[:, s % 2, :, :], axis=AX).then_inc(max_step, 1)
                dve.wait_ge(max_step, v + 1)
                nc.vector.tensor_scalar(neg_max[:, s % 2, :, HD:HD + 1], row_max[:, :].rearrange("p (t o) -> p t o", o=1),
                                        -1.0, None, ALU.mult).then_inc(nm_ok, 1)

            def take_sums(u):
                dve.wait_ge(pv_ok, NPB + NS * (u + 1))
                nc.vector.tensor_copy(o_raw[:, 2:4, :].rearrange("p t w -> p (t w)"), bank(5, 2 * VW)
                                      ).then_inc(oraw2_ok, 1)

            def divide(u, b, h):
                dve.wait_ge(oraw_ok, u + 2)
                dve.wait_ge(oraw2_ok, u + 2)
                nc.vector.reciprocal(den_inv[:, :].rearrange("p (t o) -> p t o", o=1), o_raw[:, :, HD:HD + 1])
                nc.vector.tensor_tensor(o_sum[:, :, :], o_raw[:, :, 0:HD], o_raw[:, :, HD + 1:VW], ALU.add
                                        ).then_inc(osum_ok, 1)
                dve.wait_ge(osum_ok, u + 1)
                den = den_inv[:, :].rearrange("p (t o) -> p t o", o=1).broadcast_to([P, TPB, HD])
                nc.vector.tensor_tensor(o_tok[:, b, :, h * HD:(h + 1) * HD], o_sum[:, :, :], den, ALU.mult
                                        ).then_inc(o_ok, 1)

            def expert_low(i):
                dve.wait_ge(t4_hi, i + 1)
                minus(slab(i, LO), wide(2 * (i % 2)), slab(i, HI)).then_inc(t4_lo, 1)

            def logits(i):
                n = LG_STEPS * i
                dve.wait_ge(lg_ready, i + 1)
                nc.vector.tensor_tensor(logit[:, i, :], bank(4, NE), rb[:, :], ALU.add).then_inc(lg_step, 1)
                dve.wait_ge(lg_step, n + 1)
                nc.vector.reduce_max(lmax[:, :], logit[:, i, :], axis=AX).then_inc(lg_step, 1)
                dve.wait_ge(lg_step, n + 2)
                nc.vector.tensor_scalar(nmx[:, i:i + 1], lmax[:, :], -1.0, None, ALU.mult).then_inc(lg_ok, 1)

            def choose(r):
                n = TOP_STEPS * r
                two = slice(2 * r, 2 * r + 2)
                p = logit[:, two, :]
                dve.wait_ge(ex_ok, 2 * r + 2)
                for k in range(2):
                    nc.vector.max(top8[:, k, :], logit[:, 2 * r + k, :])
                nc.vector.reciprocal(einv[:, :], esum[:, two]).then_inc(top_step, 1)
                dve.wait_ge(top_step, n + 1)
                for k in range(2):
                    nc.vector.match_replace(rest[:, k, :], top8[:, k, :], logit[:, 2 * r + k, :], 0.0)
                nc.vector.reduce_sum(wsum8[:, :], top8[:, :, :], axis=AX)
                nc.vector.tensor_scalar(mscale[:, two], einv[:, :], tg[:, 3:4], None, ALU.mult).then_inc(top_step, 1)
                dve.wait_ge(top_step, n + 2)
                nc.vector.tensor_tensor(ascale[:, two], wsum8[:, :], mscale[:, two], ALU.mult)
                minus(p, p, rest[:, :, :]).then_inc(top_step, 1)
                dve.wait_ge(top_step, n + 3)
                if r > 0:
                    dve.wait_ge(wx_ready, r)
                nc.vector.tensor_copy(w_tok[:, :, 0:NE], p).then_inc(top_step, 1)
                dve.wait_ge(top_step, n + 4)
                minus(w_tok[:, :, NE:2 * NE], p, w_tok[:, :, 0:NE]).then_inc(wt_ok, 1)

            def add_scaled(i):
                nc.vector.scalar_tensor_tensor(x_tile(i), y_all[:, i, :], ascale[:, i:i + 1], x_tile(i), ALU.mult, ALU.add
                                               ).then_inc(xs_ok, 1)

            def add_mix(i):
                if i < POOL_TILES:
                    dve.wait_ge(xy_ok, i + 1)
                else:
                    dve.wait_ge(xs_ok, i - POOL_TILES + 1)
                for half in range(2):
                    xh = x_tile(i, half * 512, 512)
                    dve.wait_ge(mix_ready, 2 * i + half + 1)
                    nc.vector.scalar_tensor_tensor(xh, bank(6 + half), mscale[:, i:i + 1], xh, ALU.mult, ALU.add
                                                   ).then_inc(fin_ok, 1)

            for s in range(RING):
                split_wq(W_WQ0 + s, s)
            values(5, 0)
            values(5, 1)
            for j in range(NJ):
                dve.wait_ge(sp_hi, j + 1)
                minus(q_blk[:, j, LO, :], bank(6 + j % 2), q_blk[:, j, HI, :]).then_inc(sp_free, 1)
            values(5, 2)
            for k in range(N_PRE):
                reduce_max(0, 0, k)
            final_max(0, 0)
            values(5, 3)
            dve.wait_ge(w_hi, W_E + 1)
            minus(rw[:, :, NE:2 * NE], stage[:, 0, 0:NC * NE].rearrange("p (c n) -> p c n", c=NC), rw[:, :, 0:NE]
                  ).then_inc(w_split, 1)
            for s in range(1, RING):
                c0, c1 = EB_CUTS[s - 1:s + 1]
                dve.wait_ge(w_hi, W_E + s + 1)
                minus(eb_lo[:, c0:c1], stage[0:NE, s, 0:c1 - c0], eb_hi[0:NE, c0:c1]).then_inc(w_split, 1)

            def iteration(g, last):
                base, high = SP0 + SP_ITER * g, SP0 + 4 * NJ * g
                u0 = SLOTS * g
                for s in range(SLOTS):
                    k = 0
                    for i in range(NS):
                        if s > 0 and i == LAG:
                            take_sums(u0 + s - 1)
                        if s < SLOTS - 1:
                            for _ in range(PRE_AT[i]):
                                reduce_max(u0 + s + 1, s + 1, k)
                                k += 1
                            if i == MAX_STEP:
                                final_max(u0 + s + 1, s + 1)
                        if s > 0 and i == LAG + 1:
                            if s == 1:
                                dve.wait_ge(kv_stored, 6 * 48)
                            divide(u0 + s - 1, (s - 1) // G, (s - 1) % G)
                        if (s, i) in Q1_TAKE:
                            j = Q1_TAKE[s, i]
                            take_low_of(q_blk, high + j, spare(SPQ1 + j), j)
                        if s == G and i - 1 in T0_STEPS:
                            j = T0_STEPS[i - 1]
                            take_low_of(o_t, high + NJ + j, spare(SPT0 + j), j)
                        if s in WO_STEPS and i - 1 in WO_STEPS[s]:
                            w = WO_STEPS[s][i - 1]
                            add_out(base + SPO0 + w, spare(SPO0 + w), 0, w)
                        if (s, i) in WO_SPLIT:
                            split_wo(W_G + 2 * RING * g + WO_SPLIT[s, i], WO_SPLIT[s, i])
                        if (s, i) in WQ_SPLIT and not last:
                            split_wq(W_G + 2 * RING * g + RING + WQ_SPLIT[s, i], WQ_SPLIT[s, i])
                        if last and s == SLOTS - 1 and i < TPB:
                            if i == 0:
                                dve.wait_ge(sp_free, base + SPX)
                            stats(i, LN4)
                take_sums(u0 + SLOTS - 1)
                divide(u0 + SLOTS - 1, 1, G - 1)
                if last:
                    dve.wait_ge(rb_ld, 16)
                    expert_low(0)
                for k, (what, j, at, _) in enumerate(END_LAST if last else END):
                    take_low_of(q_blk if what == "q" else o_t, high + 2 * NJ + k, at, j)
                if last:
                    expert_low(1)
                k = SPX + len(END_LAST if last else END)
                m = 0
                for w in range(8):
                    if not last and 2 <= w <= 5:
                        for _ in range(3):
                            reduce_max(u0 + SLOTS, 0, m)
                            m += 1
                        if w == 5:
                            final_max(u0 + SLOTS, 0)
                    add_out(base + k, end_bank(w), 1, w)
                    k += 1
                    if last and w % 2 == 1:
                        dve.wait_ge(sp_free, base + k)
                        stats(TPB + w // 2, LN4)
                        logits(w // 2)
                        if w < 5:
                            expert_low(w // 2 + 2)
                        elif w == 5:
                            choose(0)

            with dve.Fori(0, KV - 1) as g:
                iteration(g, False)
            iteration(KV - 1, True)

            expert_low(4)
            expert_low(5)
            logits(4)
            choose(1)
            add_mix(0)
            expert_low(6)
            add_mix(1)
            logits(5)
            expert_low(7)
            add_mix(2)
            add_mix(3)
            choose(2)
            logits(6)
            logits(7)
            choose(3)
            add_scaled(6)
            add_scaled(7)
            for i in range(4, NT):
                add_mix(i)

        @block.gpsimd
        def _(pool):
            def tt(out, a, b, op):
                return nc.gpsimd.tensor_tensor(out, a, b, op)

            def deviations(i, ln):
                n = ln + i
                pool.wait_ge(ln_var, n + 1)
                tt(cols(rstd, n, 1), cols(var_c, n, 1), mhalf[:, :], ALU.pow).then_inc(ln_pow, 1)
                pool.wait_ge(ln_pow, n + 1)
                tt(cols(nmr, n, 1), cols(nmean, n, 1), cols(rstd, n, 1), ALU.mult).then_inc(ln_ok, 1)

            def split_ctx(t, half):
                for s in range(RING):
                    pool.wait_ge(c_hi, RING * t + s + 1)
                    tt(ctx_t[:, half, 2 * s:2 * s + 2, LO, :], stage[:, s, :].rearrange("p (c n) -> p c n", c=2),
                       ctx_t[:, half, 2 * s:2 * s + 2, HI, :], ALU.subtract).then_inc(c_split, 1)

            def add_columns(b):
                pool.wait_ge(cs_ok, 2 * b + 2)
                for k in range(TPB):
                    i = TPB * b + k
                    pool.wait_ge(xb_ok, i + 1)
                    tt(x_tile(i), x_tile(i), bc_buf[:, b, :], ALU.add).then_inc(xc_ok, 1)

            nc.gpsimd.memset(mhalf[:, :], -0.5).then_inc(half_ok, 1)
            pool.wait_ge(half_ok, 1)
            pool.sem_inc(plo_ok, NPF)
            for b in range(B):
                split_ctx(2 * b, 0)
                for k in range(TPB):
                    deviations(TPB * b + k, LN1)
                split_ctx(2 * b + 1, 1)
                if b > 0:
                    add_columns(b - 1)
            add_columns(B - 1)
            for c in range(NC):
                pool.wait_ge(we_hi, c + 1)
                tt(w_eff[:, LO, c, :], stage[:, c % RING, :], w_eff[:, HI, c, :], ALU.subtract).then_inc(we_ok, 1)
            with pool.Fori(0, NT) as i:
                deviations(i, LN2)
            pool.wait_ge(bias_ok, 1)
            with pool.Fori(0, NT) as i:
                pool.wait_ge(y2_ok, i + 1)
                tt(x_tile(i), x_tile(i), bias_rows, ALU.add).then_inc(xbias_ok, 1)
                deviations(i, LN3)
            def split_exp(n, i):
                pool.wait_ge(exp_ok, 2 + n + 1)
                tt(p_lo[:, i % NPB, :], p_f32[:, i % NPF, :], p_hi[:, i % NPB, :], ALU.subtract).then_inc(plo_ok, 1)

            with pool.Fori(0, SLOTS * KV - 1) as u:
                for i in range(NS):
                    split_exp(NS * u + i, i)
            for i in range(NS):
                split_exp(NS * (SLOTS * KV - 1) + i, i)
                if i in DEV_AT:
                    deviations(DEV_AT[i], LN4)
            for i in range(len(DEV_AT), NT):
                deviations(i, LN4)
            for i in range(POOL_TILES):
                pool.wait_ge(ya_ok, i + 1)
                tt(x_tile(i), x_tile(i), y_all[:, i, :], ALU.add).then_inc(xy_ok, 1)


def kernel(x, ctx_4096, g_xattn, g_ffn, L0_xattn_x1_scale, L0_xattn_x1_zp, L0_xattn_x2_scale, L0_xattn_x2_zp,
           L0_ffn_W_base, L0_ffn_b_base, L0_ffn_enc0, L0_ffn_enc1, L0_ffn_coefs0, L0_ffn_coefs1, L0_ffn_mask0,
           L0_ffn_mask1, L1_xattn_Wq, L1_xattn_Wk, L1_xattn_Wv, L1_xattn_Wo, L1_ffn_router_weight,
           L1_ffn_router_bias, L1_ffn_expert_bias):
    import concourse.bacc as bacc
    import numpy as np
    from concourse.bass_utils import run_bass_kernel_spmd

    c = np.ascontiguousarray

    def by_chunk(w):
        return c(w.reshape(NC, P, -1).transpose(1, 0, 2))

    def rows(v):
        return c(np.broadcast_to(v.reshape(1, -1), (P, v.size)))

    o = np.arange(D)
    table = np.zeros((D, D))
    table[0] = 1 / np.sqrt(D)
    for k in range(1, D // 2):
        table[2 * k - 1] = np.sqrt(2 / D) * np.cos(2 * np.pi * (k * o % D) / D)
        table[2 * k] = np.sqrt(2 / D) * np.sin(2 * np.pi * (k * o % D) / D)
    table[D - 1] = (1 - 2 * (o % 2)) / np.sqrt(D)
    table = (table * (WS / 2)).astype(np.float32)

    coef = np.concatenate([L0_ffn_coefs0, L0_ffn_coefs1], 2).transpose(1, 2, 0)
    mask = np.concatenate([L0_ffn_mask0, L0_ffn_mask1], 2).transpose(1, 2, 0)
    eb = np.concatenate([L1_ffn_expert_bias, L1_ffn_expert_bias], 0)
    wq = L1_xattn_Wq.T.reshape(NC, P, KV, QG).transpose(2, 1, 0, 3).reshape(KV * P, NC, QG)
    wo = L1_xattn_Wo.T.reshape(KV, NJ, P, D).transpose(0, 2, 1, 3).reshape(KV * P, NJ, D)
    host = {
        "x": c(x.reshape(B * QL, D)),
        "ctx": c(ctx_4096),
        "ctx_t": c(ctx_4096.transpose(0, 2, 1)),
        "par": rows(np.concatenate([g_xattn, g_ffn, L0_xattn_x1_scale, L0_xattn_x1_zp, L0_xattn_x2_scale,
                                    L0_xattn_x2_zp])),
        "ident": np.eye(P, dtype=np.float32),
        "wk": by_chunk(L1_xattn_Wk.T),
        "wv": by_chunk(L1_xattn_Wv.T),
        "wq": c(wq),
        "wo": c(wo),
        "wb": c(L0_ffn_W_base.T),
        "bb": rows(L0_ffn_b_base),
        "ft": by_chunk(table),
        "coef": by_chunk(coef.reshape(D, R * E)).reshape(P, NC * R, E),
        "mask": by_chunk(mask.reshape(D, R * E)).view(np.int32),
        "enc": c(np.concatenate([L0_ffn_enc0, L0_ffn_enc1], 0)),
        "rw": by_chunk(L1_ffn_router_weight.T),
        "rb": rows(L1_ffn_router_bias),
        "eb": c(eb),
    }
    nc = bacc.Bacc("TRN2", target_bir_lowering=False, num_devices=1)
    aps = [nc.dram_tensor(f"{name}_in", a.shape, I32 if name == "mask" else F32, kind="ExternalInput").ap()
           for name, a in host.items()]
    out = nc.dram_tensor("out", (B * QL, D), F32, kind="ExternalOutput").ap()
    flamingo(nc, *aps, out)
    result = run_bass_kernel_spmd(nc, [{f"{name}_in": a for name, a in host.items()}], core_ids=[0])
    return result.results[0]["out"].reshape(B, QL, D)
```
